# Optimizing a Trainium2 kernel written in Bass

```python
import numpy as np
import jax
import jax.numpy as jnp

def _softmax(x, axis=-1):
    return jax.nn.softmax(x, axis=axis)

def _gelu(x):
    return jax.nn.gelu(x, approximate=True)

def _silu(x):
    return jax.nn.silu(x)

def _sigmoid(x):
    return jax.nn.sigmoid(x)

def _layernorm(x, axis=-1, eps=1e-05):
    m = jnp.mean(x, axis=axis, keepdims=True)
    v = jnp.var(x, axis=axis, keepdims=True)
    return (x - m) / jnp.sqrt(v + eps)

def _scatter_add(tgt, idx, src, axis=0):
    return tgt.at[idx].add(src)

def _segment_sum(src, seg, n):
    return jax.ops.segment_sum(src, seg, n)
kernel_name = 'mk_metaformer_d1_conv_nchw512_r4_e4b340'

def setup_inputs(seed: int=0):
    np.random.seed(seed)
    _w = jnp.asarray

    def _rec_inputs():
        import jax
        import jax.numpy as jnp
        _gk = jax.random.key(seed)
        x = 7.22e-05 + 1 * jax.random.normal(jax.random.fold_in(_gk, 1), (16, 128, 32, 32), jnp.float32)
        return x
    x = _rec_inputs()

    def _L0_conv_setup():
        import jax, jax.numpy as jnp
        import numpy as np
        NUM_HEADS = 8
        HEAD_SIZE = 16
        N_EMBED = 128
        key = jax.random.key(seed)
        ks = jax.random.split(key, 6)
        B, C, H, W = (16, N_EMBED, 32, 32)
        x = jax.random.normal(ks[0], (B, C, H, W), dtype=jnp.float32)
        s = 1.0 / np.sqrt(N_EMBED)
        Wq = jax.random.normal(ks[1], (NUM_HEADS, N_EMBED, HEAD_SIZE), dtype=jnp.float32) * s
        Wk = jax.random.normal(ks[2], (NUM_HEADS, N_EMBED, HEAD_SIZE), dtype=jnp.float32) * s
        Wv = jax.random.normal(ks[3], (NUM_HEADS, N_EMBED, HEAD_SIZE), dtype=jnp.float32) * s
        Wproj = jax.random.normal(ks[4], (NUM_HEADS * HEAD_SIZE, N_EMBED), dtype=jnp.float32) * s
        bproj = jax.random.normal(ks[5], (N_EMBED,), dtype=jnp.float32) * 0.01
        return {'x': x, 'Wq': Wq, 'Wk': Wk, 'Wv': Wv, 'Wproj': Wproj, 'bproj': bproj}
    _L0_conv_all = _L0_conv_setup()
    _L0_conv_in = {k: v for k, v in _L0_conv_all.items() if k in ('Wq', 'Wk', 'Wv', 'Wproj', 'bproj')}
    del _L0_conv_all

    def _L0_ffn_setup():
        import jax, jax.numpy as jnp
        import numpy as np
        MIN_EXPERT_CAPACITY = 4
        EPS = 1e-09
        CAPACITY_FACTOR = 2.0

        def cumsum_exclusive(t, axis):
            return jnp.cumsum(t, axis=axis) - t

        def safe_one_hot(idx, depth):
            return jax.nn.one_hot(idx, depth + 1)[..., :depth]

        def top2_gating(x, w_gating):
            b, n, d = x.shape
            e = w_gating.shape[-1]
            raw_gates = jax.nn.softmax(jnp.einsum('bnd,de->bne', x, w_gating), axis=-1)
            gate_1 = jnp.max(raw_gates, axis=-1)
            index_1 = jnp.argmax(raw_gates, axis=-1)
            mask_1 = jax.nn.one_hot(index_1, e, dtype=raw_gates.dtype)
            gates_without_top1 = raw_gates * (1.0 - mask_1)
            gate_2 = jnp.max(gates_without_top1, axis=-1)
            index_2 = jnp.argmax(gates_without_top1, axis=-1)
            mask_2 = jax.nn.one_hot(index_2, e, dtype=raw_gates.dtype)
            denom = gate_1 + gate_2 + EPS
            gate_1 = gate_1 / denom
            gate_2 = gate_2 / denom
            density_1 = jnp.mean(mask_1, axis=-2)
            density_1_proxy = jnp.mean(raw_gates, axis=-2)
            loss = jnp.mean(density_1_proxy * density_1) * float(e * e)
            capacity = max(min(n, int(n * 2 * CAPACITY_FACTOR / e)), MIN_EXPERT_CAPACITY)
            cap_f = float(capacity)
            pos1 = cumsum_exclusive(mask_1, axis=-2) * mask_1
            mask_1 = mask_1 * (pos1 < cap_f).astype(mask_1.dtype)
            mask_1_count = jnp.sum(mask_1, axis=-2, keepdims=True)
            mask_1_flat = jnp.sum(mask_1, axis=-1)
            pos1 = jnp.sum(pos1, axis=-1)
            gate_1 = gate_1 * mask_1_flat
            pos2 = (cumsum_exclusive(mask_2, axis=-2) + mask_1_count) * mask_2
            mask_2 = mask_2 * (pos2 < cap_f).astype(mask_2.dtype)
            mask_2_flat = jnp.sum(mask_2, axis=-1)
            pos2 = jnp.sum(pos2, axis=-1)
            gate_2 = gate_2 * mask_2_flat
            combine = gate_1[..., None, None] * mask_1_flat[..., None, None] * jax.nn.one_hot(index_1, e, dtype=x.dtype)[..., None] * safe_one_hot(pos1.astype(jnp.int32), capacity)[..., None, :] + gate_2[..., None, None] * mask_2_flat[..., None, None] * jax.nn.one_hot(index_2, e, dtype=x.dtype)[..., None] * safe_one_hot(pos2.astype(jnp.int32), capacity)[..., None, :]
            dispatch = (combine > 0).astype(combine.dtype)
            return (dispatch, combine, loss)
        key = jax.random.key(seed)
        k_x, k_g, k_w1, k_w2 = jax.random.split(key, 4)
        b, n, d, e, h = (2, 1024, 128, 16, 512)
        x = jax.random.normal(k_x, (b, n, d), dtype=jnp.float32)
        w_gating = jax.random.normal(k_g, (d, e), dtype=jnp.float32) / np.sqrt(d)
        w1 = jax.random.normal(k_w1, (e, d, h), dtype=jnp.float32) / np.sqrt(d)
        w2 = jax.random.normal(k_w2, (e, h, d), dtype=jnp.float32) / np.sqrt(h)
        return {'x': x, 'w_gating': w_gating, 'w1': w1, 'w2': w2}
    _L0_ffn_all = _L0_ffn_setup()
    _L0_ffn_in = {k: v for k, v in _L0_ffn_all.items() if k in ('w_gating', 'w1', 'w2')}
    del _L0_ffn_all
    return {'x': x, 'L0_conv_Wq': _L0_conv_in['Wq'], 'L0_conv_Wk': _L0_conv_in['Wk'], 'L0_conv_Wv': _L0_conv_in['Wv'], 'L0_conv_Wproj': _L0_conv_in['Wproj'], 'L0_conv_bproj': _L0_conv_in['bproj'], 'L0_ffn_w_gating': _L0_ffn_in['w_gating'], 'L0_ffn_w1': _L0_ffn_in['w1'], 'L0_ffn_w2': _L0_ffn_in['w2']}

def reference(x, L0_conv_Wq, L0_conv_Wk, L0_conv_Wv, L0_conv_Wproj, L0_conv_bproj, L0_ffn_w_gating, L0_ffn_w1, L0_ffn_w2):
    import jax
    import jax.numpy as jnp

    def _L0_conv_ref(x, Wq, Wk, Wv, Wproj, bproj):
        import jax, jax.numpy as jnp
        import numpy as np
        NUM_HEADS = 8
        HEAD_SIZE = 16
        N_EMBED = 128
        B, C, H, W = x.shape
        T = H * W
        xs = jnp.reshape(x, (B, T, C))
        q = jnp.einsum('btc,hcd->bhtd', xs, Wq)
        k = jnp.einsum('btc,hcd->bhtd', xs, Wk)
        v = jnp.einsum('btc,hcd->bhtd', xs, Wv)
        scale = 1.0 / jnp.sqrt(jnp.asarray(HEAD_SIZE, dtype=x.dtype))
        scores = jnp.einsum('bhtd,bhsd->bhts', q, k) * scale
        att = jax.nn.softmax(scores, axis=-1)
        out = jnp.einsum('bhts,bhsd->bhtd', att, v)
        out = jnp.transpose(out, (0, 2, 1, 3)).reshape(B, T, -1)
        out = out @ Wproj + bproj
        return jnp.reshape(out, (B, C, H, W))

    def _L0_ffn_ref(x, w_gating, w1, w2):
        import jax, jax.numpy as jnp
        import numpy as np
        MIN_EXPERT_CAPACITY = 4
        EPS = 1e-09
        CAPACITY_FACTOR = 2.0

        def cumsum_exclusive(t, axis):
            return jnp.cumsum(t, axis=axis) - t

        def safe_one_hot(idx, depth):
            return jax.nn.one_hot(idx, depth + 1)[..., :depth]

        def top2_gating(x, w_gating):
            b, n, d = x.shape
            e = w_gating.shape[-1]
            raw_gates = jax.nn.softmax(jnp.einsum('bnd,de->bne', x, w_gating), axis=-1)
            gate_1 = jnp.max(raw_gates, axis=-1)
            index_1 = jnp.argmax(raw_gates, axis=-1)
            mask_1 = jax.nn.one_hot(index_1, e, dtype=raw_gates.dtype)
            gates_without_top1 = raw_gates * (1.0 - mask_1)
            gate_2 = jnp.max(gates_without_top1, axis=-1)
            index_2 = jnp.argmax(gates_without_top1, axis=-1)
            mask_2 = jax.nn.one_hot(index_2, e, dtype=raw_gates.dtype)
            denom = gate_1 + gate_2 + EPS
            gate_1 = gate_1 / denom
            gate_2 = gate_2 / denom
            density_1 = jnp.mean(mask_1, axis=-2)
            density_1_proxy = jnp.mean(raw_gates, axis=-2)
            loss = jnp.mean(density_1_proxy * density_1) * float(e * e)
            capacity = max(min(n, int(n * 2 * CAPACITY_FACTOR / e)), MIN_EXPERT_CAPACITY)
            cap_f = float(capacity)
            pos1 = cumsum_exclusive(mask_1, axis=-2) * mask_1
            mask_1 = mask_1 * (pos1 < cap_f).astype(mask_1.dtype)
            mask_1_count = jnp.sum(mask_1, axis=-2, keepdims=True)
            mask_1_flat = jnp.sum(mask_1, axis=-1)
            pos1 = jnp.sum(pos1, axis=-1)
            gate_1 = gate_1 * mask_1_flat
            pos2 = (cumsum_exclusive(mask_2, axis=-2) + mask_1_count) * mask_2
            mask_2 = mask_2 * (pos2 < cap_f).astype(mask_2.dtype)
            mask_2_flat = jnp.sum(mask_2, axis=-1)
            pos2 = jnp.sum(pos2, axis=-1)
            gate_2 = gate_2 * mask_2_flat
            combine = gate_1[..., None, None] * mask_1_flat[..., None, None] * jax.nn.one_hot(index_1, e, dtype=x.dtype)[..., None] * safe_one_hot(pos1.astype(jnp.int32), capacity)[..., None, :] + gate_2[..., None, None] * mask_2_flat[..., None, None] * jax.nn.one_hot(index_2, e, dtype=x.dtype)[..., None] * safe_one_hot(pos2.astype(jnp.int32), capacity)[..., None, :]
            dispatch = (combine > 0).astype(combine.dtype)
            return (dispatch, combine, loss)
        dispatch, combine, loss = top2_gating(x, w_gating)
        expert_inputs = jnp.einsum('bnd,bnec->ebcd', x, dispatch)
        hidden = jax.nn.relu(jnp.einsum('ebcd,edh->ebch', expert_inputs, w1))
        expert_outputs = jnp.einsum('ebch,ehd->ebcd', hidden, w2)
        output = jnp.einsum('ebcd,bnec->bnd', expert_outputs, combine)
        return output

    def _gn(v, G=32, eps=1e-05):
        B_, C_, H_, W_ = v.shape
        g = v.reshape(B_, G, C_ // G, H_, W_)
        m = jnp.mean(g, axis=(2, 3, 4), keepdims=True)
        s = jnp.var(g, axis=(2, 3, 4), keepdims=True)
        return ((g - m) / jnp.sqrt(s + eps)).reshape(v.shape)

    def _ln_c(v, eps=1e-06):
        m = jnp.mean(v, axis=1, keepdims=True)
        s = jnp.var(v, axis=1, keepdims=True)
        return (v - m) / jnp.sqrt(s + eps)

    def _ln_t(v, eps=1e-05):
        m = jnp.mean(v, axis=-1, keepdims=True)
        s = jnp.var(v, axis=-1, keepdims=True)
        return (v - m) / jnp.sqrt(s + eps)

    def _to_tokens(v):
        B_, C_, H_, W_ = v.shape
        return v.reshape(B_, C_, H_ * W_).transpose(0, 2, 1)

    def _from_tokens(t, like):
        B_, C_, H_, W_ = like.shape
        return t.transpose(0, 2, 1).reshape(B_, C_, H_, W_)
    x = x + _L0_conv_ref(_ln_c(x), L0_conv_Wq, L0_conv_Wk, L0_conv_Wv, L0_conv_Wproj, L0_conv_bproj)
    t = _to_tokens(x)
    t = t + _L0_ffn_ref(_ln_t(t), L0_ffn_w_gating, L0_ffn_w1, L0_ffn_w2)
    x = _from_tokens(t, x)
    return x

_drawn_inputs = setup_inputs


def setup_inputs(seed=0):
    import zlib

    import numpy as np

    out = dict(_drawn_inputs(seed))
    spreads = {}
    factors = {'L0_conv_bproj': 5.471}
    for name, (base, spread) in spreads.items():
        noise = np.random.default_rng([zlib.crc32(name.encode()), seed]).standard_normal(out[name].shape)
        drawn = base * np.exp(spread * noise) if base else spread * noise
        out[name] = jnp.asarray(drawn.astype(out[name].dtype))
    for name, factor in factors.items():
        out[name] = (out[name] * factor).astype(out[name].dtype)
    return out
```

```python
from contextlib import ExitStack

import concourse.bass as bass
from concourse import mybir

FP32 = mybir.dt.float32
BF16 = mybir.dt.bfloat16
I32 = mybir.dt.int32
ALU = mybir.AluOpType
ACT = mybir.ActivationFunctionType
AX = mybir.AxisListType

P = 128
B, C, T = 16, 128, 1024
H, D = 8, 16
HG = 4
G = H // HG
TB = T // P
HALF = T // 2
SCALE = 1.0 / float(D) ** 0.5
LN1_EPS, LN2_EPS = 1e-6, 1e-5

STAGES = G * 2
UNITS = TB * HG
SLOTS = STAGES * UNITS
LEAD = 44
PRING = 16
ALL_STAGES = B * STAGES

Q_PART = (0, 0, 1, 1, 0, 2)
K_PART = (0, 1, 0, 1, 2, 0)
STACK = 16 * len(Q_PART)
MPARTS = 2
MROWS = MPARTS * HG

E = 16
HID = 512
HC = HID // P
CAP = T * 2 * 2 // E
GATE_EPS = 1e-9
REG = B * T + P
ROWW = C + 4
SKIP = 1 << 20
BLOCKS = 2 * B * T // P + E
XR = 4
TAB_STEPS = 15
ROUTE_A, ROUTE_B = 23, 18


def wait(eng, sem, value):
    if isinstance(value, int) and value <= 0:
        return
    eng.wait_ge(sem, value)


def wait_apart(eng, passed, sem, value):
    wait(eng, sem, value)
    if not isinstance(value, int):
        eng.sem_inc(passed, 1)


def metaformer(nc, x, wq, wk, wv, wproj, bproj, wgate, w1, w2, out):
    ctx = ExitStack()
    with ctx:
        def sb(name, shape, dt=FP32):
            return ctx.enter_context(nc.sbuf_tensor("sb_" + name, shape, dt))

        def sem(name):
            return ctx.enter_context(nc.semaphore(name))

        x_v = x.rearrange("b c h w -> b c (h w)")
        out_v = out.rearrange("b c h w -> b c (h w)")
        sorted_rows = nc.dram_tensor("sorted_rows", (E * REG + P, ROWW), FP32, kind="Internal").ap()
        expert_out = nc.dram_tensor("expert_out", (2 * B * T, C), FP32, kind="Internal").ap()
        table_dram = nc.dram_tensor("table_dram", (2, 3 * P), I32, kind="Internal").ap()

        arena_a = sb("arena_a", [P, PRING * HALF])
        probs = arena_a[:, :].rearrange("p (u t) -> p u t", u=PRING)
        w1_all = arena_a[:, :].rearrange("p (e h) -> p e h", e=E)
        y_in = arena_a[:, 0:4 * T].rearrange("p (s k j d) -> p s k j d", s=2, k=2, j=TB)
        o_buf = arena_a[:, 4 * T:6 * T].rearrange("p (s t) -> p s t", s=2)
        arena_b = sb("arena_b", [P, 2 * G * HG * T], BF16)
        stacks = arena_b[:, :].rearrange("p (o g h t) -> p o g h t", o=2, g=G, h=HG)
        qs, ks = stacks[:, 0], stacks[:, 1]
        w2_all = arena_b[:, :].bitcast(FP32).rearrange("p (e c d) -> p e c d", e=E, c=HC)
        arena_c = sb("arena_c", [P, 3 * T + 2 * T])
        parts = arena_c[:, 0:3 * T].bitcast(BF16).rearrange("p (o l t) -> p o l t", o=2, l=3)
        att = arena_c[:, 3 * T:5 * T].rearrange("p (g t) -> p g t", g=G)
        at = 0

        def cut(n):
            nonlocal at
            at += n
            return arena_c[:, at - n:at]
        w1_blk = cut(2 * HID).rearrange("p (s h) -> p s h", s=2)
        w2_blk = cut(2 * HID).rearrange("p (s h) -> p s h", s=2)
        hid = cut(2 * HID).rearrange("p (s h) -> p s h", s=2)
        blk_in = cut(XR * ROWW).rearrange("p (s w) -> p s w", s=XR)
        blk_y = cut(XR * P).rearrange("p (s d) -> p s d", s=XR)
        blk_xt = cut(2 * P).rearrange("p (s d) -> p s d", s=2)
        blk_dest = cut(XR).bitcast(I32)

        x1_all = sb("x1_all", [P, B, T])
        x_in = sb("x_in", [P, T])
        xt = sb("xt", [P, TB, P])
        res = sb("res", [P, T])
        x1 = res
        tok = sb("tok", [P, TB, P])
        rows = sb("rows", [P, 2, TB, ROWW])
        rows_i = rows[:, :, :, :].rearrange("p k j w -> p (k j w)").bitcast(I32).rearrange(
            "p (k j w) -> p k j w", k=2, j=TB)
        qk_f = sb("qk_f", [P, 2, HALF])
        v_st = sb("v_st", [P, TB, H, D])
        v_pad = sb("v_pad", [P, TB, H, 32])
        o_t = sb("o_t", [P, HALF // 32, 32])
        o_n = sb("o_n", [P, HALF // 32, 32])
        o_rec = sb("o_rec", [P, HALF // 32])
        m_red = sb("m_red", [P, 2, UNITS])
        m_neg = sb("m_neg", [P, 2, HG * HG])
        m_rest = sb("m_rest", [P, HG * HG])
        m_parts = sb("m_parts", [P, HG, MPARTS, HG], BF16)
        m_row = sb("m_row", [P, HALF], BF16)
        stats = sb("stats", [P, 2, TB, 6])
        mean_var = sb("mean_var", [P, 2, TB, 2])
        ln_var = sb("ln_var", [P, 2, TB])
        rstd = sb("rstd", [P, 2, TB])
        neg_mean = sb("neg_mean", [P, 2, TB])
        gat = sb("gat", [P, TB, E])
        tmp = sb("tmp", [P, TB, E])
        tmp2 = sb("tmp2", [P, TB, E])
        masks = sb("masks", [P, TB, 3, E])
        masks_b = sb("masks_b", [P, TB, 3 * E], BF16)
        counts = sb("counts", [P, TB * 3 * E + 3 * E])
        before = counts[:, 0:TB * 3 * E].rearrange("p (j m e) -> p j m e", j=TB, m=3)
        totals = counts[:, TB * 3 * E:].rearrange("p (m e) -> p m e", m=3)
        small = sb("small", [P, 12, TB])
        kept_n = sb("kept_n", [P, E])
        base2 = sb("base2", [P, E])
        base = sb("base", [P, E])
        dest_f = sb("dest_f", [P, TB, 2])
        place = sb("place", [P, 2, TB], I32)
        pad_row = sb("pad_row", [P, ROWW])
        pad_place = sb("pad_place", [P, E], I32)
        blk_f = sb("blk_f", [P, 6, 3 * E])
        blk_n = sb("blk_n", [P, E], I32)
        blk_i = sb("blk_i", [P, 2, 3], I32)
        table = x_in[0:1, 0:6 * P].bitcast(I32).rearrange("o (n b) -> o n b", n=2)
        ident = sb("ident", [P, P])
        ident_b = sb("ident_b", [P, P], BF16)
        ones_b = sb("ones_b", [P, P], BF16)
        tri_b = sb("tri_b", [P, P], BF16)
        mean_m = tok[:, 0, :]
        neg_half = sb("neg_half", [P, TB])
        e_rev = sb("e_rev", [P, TB, E])
        reg_base = sb("reg_base", [P, E])
        part_no = sb("part_no", [P, 1])
        blk_no = sb("blk_no", [P, 3])
        ones_e = sb("ones_e", [P, E])
        iota_i = tok[:, 1:3, :].rearrange("p j c -> p (j c)").bitcast(I32)
        wq_in = o_t[:, 0:8, :].rearrange("p n d -> p (n d)").rearrange("p (o h d) -> p o h d", o=2, h=H)
        wq_r = sb("wq_r", [P, 2, P])
        wv_sb = sb("wv_sb", [P, H, D])
        wp_sb = sb("wp_sb", [P, G, C])
        bias = sb("bias", [P, C])
        wg_sb = sb("wg_sb", [P, E])
        wg_c = sb("wg_c", [P, E])

        ps_score = ctx.enter_context(nc.psum_tensor("ps_score", [P, 2, 2, HALF], FP32))
        ps_max = ctx.enter_context(nc.psum_tensor("ps_max", [P, 2, HALF], FP32))
        ps_pv = ctx.enter_context(nc.psum_tensor("ps_pv", [P, HALF], FP32))
        misc = ctx.enter_context(nc.psum_tensor("misc", [P, HALF], FP32))
        ps_h = ps_score[:, 0]
        ps_xt = ps_score[:, 1]
        ps_o = ps_max

        setup = sem("setup")
        setup_v = sem("setup_v")
        weights_in = sem("weights_in")
        wg_mean = sem("wg_mean")
        x_loaded = sem("x_loaded")
        res_loaded = sem("res_loaded")
        xt_psum = sem("xt_psum")
        xt_copied = sem("xt_copied")
        ln1_stats = sem("ln1_stats")
        ln1_scale = sem("ln1_scale")
        xt_normed = sem("xt_normed")
        qk_psum = sem("qk_psum")
        qk_copied = sem("qk_copied")
        qk_parts = sem("qk_parts")
        stacked = [sem(f"stacked{g}") for g in range(G)]
        v_psum = sem("v_psum")
        v_copied = sem("v_copied")
        v_placed = sem("v_placed")
        max_ready = sem("max_ready")
        max_taken = sem("max_taken")
        m_ready = sem("m_ready")
        m_split = sem("m_split")
        m_psum = sem("m_psum")
        m_copied = sem("m_copied")
        m_loaded = sem("m_loaded")
        scores_ready = sem("scores_ready")
        exp_done = sem("exp_done")
        pv_done = sem("pv_done")
        norm_steps = sem("norm_steps")
        pj_psum = sem("pj_psum")
        res_ready = sem("res_ready")
        x1_ready = sem("x1_ready")
        x1_stored = sem("x1_stored")
        tt_psum = sem("tt_psum")
        tok_copied = sem("tok_copied")
        ln2_stats = sem("ln2_stats")
        ln2_scale = sem("ln2_scale")
        rows_normed = sem("rows_normed")
        rows_copied = sem("rows_copied")
        lg_psum = sem("lg_psum")
        lg_taken = sem("lg_taken")
        gate_shifted = sem("gate_shifted")
        gate_exp = sem("gate_exp")
        route_a = sem("route_a")
        masks_ready = sem("masks_ready")
        cs_psum = sem("cs_psum")
        cs_taken = sem("cs_taken")
        route_b = sem("route_b")
        routed_parts = sem("routed_parts")
        dest_next = sem("dest_next")
        routed = sem("routed")
        scattered = sem("scattered")
        pads_ready = sem("pads_ready")
        pads_written = sem("pads_written")
        tab_steps = sem("tab_steps")
        tab_out = sem("tab_out")
        tab_in = sem("tab_in")
        w1_loaded = sem("w1_loaded")
        w2_loaded = sem("w2_loaded")
        blk_loaded = [sem(f"blk_loaded{s}") for s in range(XR)]
        blk_tr = sem("blk_tr")
        blk_tr_copied = sem("blk_tr_copied")
        w1_copied = sem("w1_copied")
        w2_copied = sem("w2_copied")
        hid_psum = sem("hid_psum")
        hid_done = sem("hid_done")
        y_psum = sem("y_psum")
        dest_copied = sem("dest_copied")
        y_scaled = sem("y_scaled")
        y_stored = [sem(f"y_stored{s}") for s in range(XR)]
        y_loaded = [sem(f"y_loaded{s}") for s in range(2)]
        y_summed = sem("y_summed")
        yt_psum = sem("yt_psum")
        out_ready = sem("out_ready")
        out_stored = [sem(f"out_stored{s}") for s in range(2)]

        gp_passed = sem("gp_passed")
        sp_passed = sem("sp_passed")
        dve_passed = sem("dve_passed")

        SETUP = 27
        WEIGHTS = (2 + 1 + H + 1 + 1) * 16
        END_BLOCKS = BLOCKS - 1

        block = ctx.enter_context(nc.Block())

        @block.sync
        def _(sp):
            def load_x(b):
                wait_apart(sp, sp_passed, xt_psum, 2 * b)
                sp.dma_start(x_in[:, :], x_v[b] if isinstance(b, int) else x_v[bass.ds(b, 1)].rearrange(
                    "a c t -> (a c) t")).then_inc(x_loaded, 16)

            def load_res(b):
                wait_apart(sp, sp_passed, x1_stored, 16 * b)
                wait_apart(sp, sp_passed, lg_psum, b)
                wait_apart(sp, sp_passed, tt_psum, 2 * b)
                sp.dma_start(res[:, :], x_v[b] if isinstance(b, int) else x_v[bass.ds(b, 1)].rearrange(
                    "a c t -> (a c) t")).then_inc(res_loaded, 16)

            def stack(b, g):
                wait_apart(sp, sp_passed, qk_parts, 20 * (b + 1))
                wait_apart(sp, sp_passed, scores_ready, 64 * b - 64 + 32 * (g + 1))
                for o, part in ((0, Q_PART), (1, K_PART)):
                    for r, level in enumerate(part):
                        sp.dma_start(stacks[16 * r:16 * r + 16, o, g, :, :],
                                     parts[64 * g:64 * g + 64, o, level, :]).then_inc(stacked[g], 16)

            def load_m(b, s):
                g, half = s % STAGES // 2, s % 2
                wait_apart(sp, sp_passed, m_copied, STAGES * b + s + 1)
                for h in range(HG):
                    sp.dma_start(qs[STACK:STACK + MROWS, g, h, half * HALF:(half + 1) * HALF],
                                 m_row[STACK:STACK + MROWS, :]).then_inc(m_loaded, 16)

            def store_x1(b):
                wait_apart(sp, sp_passed, x1_ready, 2 * (b + 1))
                dst = x1_all[:, b, :] if isinstance(b, int) else x1_all[:, bass.ds(b, 1), :].rearrange(
                    "p a t -> p (a t)")
                sp.dma_start(dst, x1[:, :]).then_inc(x1_stored, 16)

            for o, w in ((0, wq), (1, wk)):
                sp.dma_start(wq_in[:, o], w.rearrange("h c d -> c h d")).then_inc(weights_in, 16)
            sp.dma_start(x_in[:, :], x_v[0]).then_inc(x_loaded, 16)
            sp.dma_start(wv_sb[:, :, :], wv.rearrange("h c d -> c h d")).then_inc(weights_in, 16)
            sp.dma_start(bias[:, :], bproj.rearrange("(a c) -> a c", a=1).to_broadcast([P, C])).then_inc(weights_in, 16)
            sp.dma_start(wg_sb[:, :], wgate).then_inc(weights_in, 16)
            sp.wait_ge(setup, SETUP)
            for h in range(H):
                q = 32 * (h % HG)
                sp.dma_start(wp_sb[q:q + D, h // HG, :], wproj[h * D:(h + 1) * D, :]).then_inc(weights_in, 16)
            stack(0, 0)
            load_x(1)
            load_m(0, 0)

            def batch(b, first, last):
                stack(b, 1)
                if not first:
                    store_x1(b - 1)
                load_m(b, 1)
                if not last:
                    wait_apart(sp, sp_passed, xt_psum, 2 * (b + 2))
                    if not (isinstance(b, int) and b + 2 >= B):
                        load_x(b + 2)
                load_m(b, 2)
                if not last:
                    stack(b + 1, 0)
                load_res(b)
                load_m(b, 3)
                if not last:
                    load_m(b, 4)

            batch(0, True, False)
            with sp.Fori(1, B - 2) as b:
                batch(b, False, False)
            batch(B - 2, False, False)
            batch(B - 1, False, True)
            sp.wait_ge(pv_done, 32 * B)
            sp.dma_start(w1_all, w1.rearrange("e d h -> d e h")).then_inc(w1_loaded, 16)
            sp.dma_start(w2_all, w2.rearrange("e (c p) d -> p e c d", p=P)).then_inc(w2_loaded, 16)
            store_x1(B - 1)
            sp.wait_ge(tab_steps, TAB_STEPS)
            for n in range(2):
                sp.dma_start(table_dram[n].rearrange("(p c) -> p c", p=P), blk_i[:, n, :]).then_inc(tab_out, 16)
            sp.wait_ge(tab_out, 32)
            sp.dma_start(table[:, :, :], table_dram.rearrange("(o n) b -> o n b", o=1)).then_inc(tab_in, 16)
            sp.wait_ge(tab_in, 16)
            sp.wait_ge(scattered, 256 * B)
            sp.wait_ge(pads_written, 16 * (E + 1))
            sp.wait_ge(pj_psum, 2 * B)

            def load_block(r, s):
                i = XR * r + s
                row = sp.value_load(table[0:1, 1, i:i + 1] if isinstance(i, int) else table[0:1, 1, bass.ds(i, 1)],
                                    min_val=0, max_val=E * REG)
                wait_apart(sp, sp_passed, y_scaled, i - XR + 1)
                wait_apart(sp, sp_passed, dest_copied, i - XR + 1)
                sp.dma_start(blk_in[:, s, :], sorted_rows[bass.ds(row, P), :]).then_inc(blk_loaded[s], 16)

            for s in range(XR):
                load_block(0, s)
            with sp.Fori(1, BLOCKS // XR) as r:
                for s in range(XR):
                    load_block(r, s)
            for s in range(XR):
                sp.wait_ge(y_stored[s], 16 * (BLOCKS // XR))

            def load_y(r, s):
                b = 2 * r + s
                wait_apart(sp, sp_passed, yt_psum, 2 * (b - 1))
                for k in range(2):
                    sp.dma_start(y_in[:, s, k], expert_out[bass.ds(k * B * T + b * T, T), :].rearrange(
                        "(j p) d -> p j d", p=P)).then_inc(y_loaded[s], 16)

            def store_out(r, s):
                b = 2 * r + s
                wait_apart(sp, sp_passed, out_ready, 2 * (b + 1))
                sp.dma_start(out_v[bass.ds(b, 1)].rearrange("a c t -> (a c) t"), o_buf[:, s, :]).then_inc(
                    out_stored[s], 16)

            load_y(0, 0)
            load_y(0, 1)
            with sp.Fori(0, B // 2 - 1) as r:
                for s in range(2):
                    load_y(r + 1, s)
                    store_out(r, s)
            for s in range(2):
                store_out(B // 2 - 1, s)
            for s in range(2):
                sp.wait_ge(out_stored[s], 16 * (B // 2))

        @block.gpsimd
        def _(gp):
            n = 0

            def step(inst):
                nonlocal n
                n += 1
                inst.then_inc(setup, 1)

            def eye(t, view, pattern, cm, base_, op, fill):
                gp.wait_ge(setup, n)
                step(nc.gpsimd.affine_select(out=view, in_=view, compare_op=op, fill=fill, base=base_,
                                             pattern=pattern, channel_multiplier=cm))

            step(nc.gpsimd.memset(ident[:, :], 0.0))
            eye(ident, ident[:, :], [[-1, P]], 1, 0, ALU.not_equal, 1.0)
            step(nc.gpsimd.memset(ident_b[:, :], 0.0))
            eye(ident_b, ident_b[:, :], [[-1, P]], 1, 0, ALU.not_equal, 1.0)
            step(nc.gpsimd.memset(ones_b[:, :], 1.0))
            step(nc.gpsimd.memset(tri_b[:, :], 1.0))
            eye(tri_b, tri_b[:, :], [[1, P]], -1, 0, ALU.is_gt, 0.0)
            step(nc.gpsimd.memset(mean_m[:, :], 1.0 / C))
            step(nc.gpsimd.memset(wp_sb[:, :, :], 0.0))
            step(nc.gpsimd.memset(v_pad[:, :, :, :], 1.0))
            step(nc.gpsimd.memset(o_n[:, :, :], 0.0))
            step(nc.gpsimd.memset(rows[:, :, :, C + 2:ROWW], 0.0))
            step(nc.gpsimd.memset(neg_half[:, :], -0.5))
            step(nc.gpsimd.memset(ones_e[:, :], 1.0))
            step(nc.gpsimd.memset(pad_row[:, :], 0.0))
            gp.wait_ge(setup, n)
            step(nc.gpsimd.memset(pad_row[:, C:C + 1].bitcast(I32), SKIP))
            for g in range(G):
                gp.wait_ge(setup, n)
                step(nc.gpsimd.memset(ks[STACK:STACK + MROWS, g, :, :], 0.0))
                for part in range(MPARTS):
                    eye(ks, ks[STACK:STACK + MROWS, g, :, :], [[-1, HG], [0, T]], 1, -HG * part, ALU.not_equal, 1.0)
            at_i = 0
            gp.wait_ge(setup, n)
            for pattern, start, cm, num in (
                ([[0, TB], [-1, E]], E, 0, TB * E), ([[REG, E]], 0, 0, E),
                ([[P, TB], [B * T, 2]], 0, 1, TB * 2), ([[0, 1]], 0, 1, 1), ([[1, 3]], 0, 3, 3),
            ):
                step(nc.gpsimd.iota(iota_i[:, at_i:at_i + num], pattern=pattern, base=start, channel_multiplier=cm))
                at_i += num
            assert n == SETUP, n

            def ln_factors(b, which, eps, stats_done, done):
                wait_apart(gp, gp_passed, stats_done, 16 * (b + 1))
                nc.gpsimd.tensor_scalar(ln_var[:, which, :], mean_var[:, which, :, 1], 1.0, eps,
                                        ALU.mult, ALU.add).then_inc(done, 1)
                nc.gpsimd.tensor_scalar(neg_mean[:, which, :], mean_var[:, which, :, 0], -1.0, 0.0,
                                        ALU.mult, ALU.add).then_inc(done, 1)
                wait_apart(gp, gp_passed, done, 3 * b + 2)
                nc.gpsimd.tensor_tensor(out=rstd[:, which, :], in0=ln_var[:, which, :], in1=neg_half[:, :],
                                        op=ALU.pow).then_inc(done, 1)
                wait_apart(gp, gp_passed, done, 3 * b + 3)

            def normalise_x(b):
                ln_factors(b, 0, LN1_EPS, ln1_stats, ln1_scale)
                for j in range(TB):
                    nc.gpsimd.tensor_scalar(xt[:, j, :], xt[:, j, :], neg_mean[:, 0, j:j + 1], rstd[:, 0, j:j + 1],
                                            ALU.add, ALU.mult).then_inc(xt_normed, 1)

            def split_qk(b, i):
                o, half = i // 2, i % 2
                cols = slice(half * HALF, (half + 1) * HALF)
                f = qk_f[:, i % 2, :]
                if i == 0:
                    wait_apart(gp, gp_passed, stacked[1], 192 * b)
                    wait_apart(gp, gp_passed, stacked[0], 192 * b)
                done = 20 * b + 5 * i
                wait_apart(gp, gp_passed, qk_copied, 4 * b + i + 1)
                nc.gpsimd.tensor_scalar(parts[:, o, 0, cols], f, 1.0, 0.0, ALU.mult, ALU.add).then_inc(qk_parts, 1)
                for level in (1, 2):
                    wait_apart(gp, gp_passed, qk_parts, done + 2 * level - 1)
                    nc.gpsimd.tensor_tensor(out=f, in0=f, in1=parts[:, o, level - 1, cols],
                                            op=ALU.subtract).then_inc(qk_parts, 1)
                    wait_apart(gp, gp_passed, qk_parts, done + 2 * level)
                    nc.gpsimd.tensor_scalar(parts[:, o, level, cols], f, 1.0, 0.0,
                                            ALU.mult, ALU.add).then_inc(qk_parts, 1)

            def place_v(b, g):
                wait_apart(gp, gp_passed, v_copied, 2 * (b + 1))
                wait_apart(gp, gp_passed, pv_done, 32 * b - 32 + 16 * (g + 1))
                nc.gpsimd.tensor_scalar(v_pad[:, :, HG * g:HG * g + HG, 0:D], v_st[:, :, HG * g:HG * g + HG, :],
                                        1.0, 0.0, ALU.mult, ALU.add).then_inc(v_placed, 1)

            def split_m(b, s):
                k = STAGES * b + s
                neg = m_neg[:, s % 2, :].rearrange("p (t h) -> p t h", t=HG)
                rest = m_rest[:, :].rearrange("p (t h) -> p t h", t=HG)
                wait_apart(gp, gp_passed, m_ready, k + 1)
                wait_apart(gp, gp_passed, m_psum, k)
                nc.gpsimd.tensor_scalar(m_parts[:, :, 0, :], neg, 1.0, 0.0, ALU.mult, ALU.add).then_inc(m_split, 1)
                wait_apart(gp, gp_passed, m_split, 3 * k + 1)
                nc.gpsimd.tensor_tensor(out=rest, in0=neg, in1=m_parts[:, :, 0, :],
                                        op=ALU.subtract).then_inc(m_split, 1)
                wait_apart(gp, gp_passed, m_split, 3 * k + 2)
                nc.gpsimd.tensor_scalar(m_parts[:, :, 1, :], rest, 1.0, 0.0, ALU.mult, ALU.add).then_inc(m_split, 1)

            def add_bias(b):
                wait_apart(gp, gp_passed, res_loaded, 16 * (b + 1))
                r3 = res[:, :].rearrange("p (j c) -> p j c", j=TB)
                nc.gpsimd.tensor_tensor(out=r3, in0=r3, in1=bias[:, :].unsqueeze(1).to_broadcast([P, TB, C]),
                                        op=ALU.add).then_inc(res_ready, 1)

            def normalise_tokens(b):
                ln_factors(b, 1, LN2_EPS, ln2_stats, ln2_scale)
                wait_apart(gp, gp_passed, scattered, 256 * b)
                for j in range(TB):
                    nc.gpsimd.tensor_scalar(rows[:, 0, j, 0:C], tok[:, j, :], neg_mean[:, 1, j:j + 1],
                                            rstd[:, 1, j:j + 1], ALU.add, ALU.mult).then_inc(rows_normed, 1)

            def scatter(b, k):
                wait_apart(gp, gp_passed, routed, b + 1)
                wait_apart(gp, gp_passed, rows_copied, b + 1)
                for j in range(TB):
                    nc.gpsimd.indirect_dma_start(
                        out=sorted_rows[:, :], out_offset=bass.IndirectOffsetOnAxis(ap=place[:, k, j:j + 1], axis=0),
                        in_=rows[:, k, j, :], in_offset=None).then_inc(scattered, 16)

            gp.wait_ge(weights_in, WEIGHTS)
            normalise_x(0)
            for i in range(4):
                split_qk(0, i)
            place_v(0, 0)
            split_m(0, 0)

            def batch(b, first, last):
                place_v(b, 1)
                if not first:
                    add_bias(b - 1)
                if not last:
                    normalise_x(b + 1)
                split_m(b, 1)
                if not last:
                    split_qk(b + 1, 0)
                if not first:
                    normalise_tokens(b - 1)
                if not last:
                    split_qk(b + 1, 1)
                    split_qk(b + 1, 2)
                split_m(b, 2)
                if not last:
                    split_qk(b + 1, 3)
                    place_v(b + 1, 0)
                split_m(b, 3)
                if not first:
                    scatter(b - 1, 0)
                if not last:
                    split_m(b, 4)
                if not first:
                    scatter(b - 1, 1)

            batch(0, True, False)
            with gp.Fori(1, B - 1) as b:
                batch(b, False, False)
            batch(B - 1, False, True)
            add_bias(B - 1)
            normalise_tokens(B - 1)
            scatter(B - 1, 0)
            scatter(B - 1, 1)
            gp.wait_ge(pads_ready, 1)
            gp.dma_start(sorted_rows[E * REG:E * REG + P, :], pad_row[:, :]).then_inc(pads_written, 16)
            for e in range(E):
                nc.gpsimd.indirect_dma_start(
                    out=sorted_rows[:, :], out_offset=bass.IndirectOffsetOnAxis(ap=pad_place[:, e:e + 1], axis=0),
                    in_=pad_row[:, :], in_offset=None).then_inc(pads_written, 16)

            def scatter_y(r, s):
                wait_apart(gp, gp_passed, y_scaled, XR * r + s + 1)
                wait_apart(gp, gp_passed, dest_copied, XR * r + s + 1)
                nc.gpsimd.indirect_dma_start(
                    out=expert_out[:, :], out_offset=bass.IndirectOffsetOnAxis(ap=blk_dest[:, s:s + 1], axis=0),
                    in_=blk_y[:, s, :], in_offset=None, bounds_check=2 * B * T - 1,
                    oob_is_err=False).then_inc(y_stored[s], 16)

            with gp.Fori(0, BLOCKS // XR) as r:
                for s in range(XR):
                    scatter_y(r, s)

        @block.scalar
        def _(act):
            def exp_pair(b, p):
                slot = 2 * p % PRING
                wait(act, scores_ready, 64 * b + p + 1)
                wait(act, pv_done, 32 * b + (p - PRING // 2) // 2 + 1)
                nc.scalar.activation(probs[:, slot:slot + 2, :], ps_score[:, p % 2], ACT.Exp,
                                     scale=SCALE).then_inc(exp_done, 1)

            def copy_xt(b, half):
                wait(act, xt_psum, 2 * b + half + 1)
                wait(act, v_psum, 2 * b)
                nc.scalar.activation(xt[:, 4 * half:4 * half + 4, :],
                                     misc[:, :].rearrange("p (j c) -> p j c", j=4), ACT.Copy).then_inc(xt_copied, 1)

            def copy_qk(b, i):
                wait(act, qk_psum, 4 * b + i + 1)
                wait(act, qk_parts, 20 * b + 5 * (i - 1))
                nc.scalar.activation(qk_f[:, i % 2, :], misc[:, :], ACT.Copy).then_inc(qk_copied, 1)

            def copy_v(b, half):
                wait(act, v_psum, 2 * b + half + 1)
                wait(act, v_placed, 2 * b)
                nc.scalar.activation(v_st[:, 4 * half:4 * half + 4, :, :].rearrange("p j h d -> p j (h d)"),
                                     misc[:, :].rearrange("p (j n) -> p j n", j=4), ACT.Copy).then_inc(v_copied, 1)

            def copy_m(b, s):
                k = STAGES * b + s
                wait(act, m_psum, k + 1)
                wait(act, m_loaded, 64 * k)
                nc.scalar.activation(m_row[STACK:STACK + MROWS, :], misc[STACK:STACK + MROWS, :],
                                     ACT.Copy).then_inc(m_copied, 1)

            def copy_tokens(b, half):
                wait(act, tt_psum, 2 * b + half + 1)
                wait(act, rows_normed, TB * b)
                nc.scalar.activation(tok[:, 4 * half:4 * half + 4, :],
                                     misc[:, :].rearrange("p (j c) -> p j c", j=4), ACT.Copy).then_inc(tok_copied, 1)

            def gate_exponentials(b):
                wait(act, gate_shifted, b + 1)
                nc.scalar.activation(tmp[:, :, :], gat[:, :, :], ACT.Exp).then_inc(gate_exp, 1)

            def copy_rows(b):
                wait(act, rows_normed, TB * (b + 1))
                wait(act, scattered, 256 * b)
                nc.scalar.activation(rows[:, 1, :, 0:C], rows[:, 0, :, 0:C], ACT.Copy).then_inc(rows_copied, 1)

            copy_xt(0, 0)
            copy_xt(0, 1)
            for i in range(4):
                copy_qk(0, i)
            copy_v(0, 0)
            copy_v(0, 1)
            copy_m(0, 0)

            def batch(b, first, last):
                for p in range(SLOTS // 2):
                    exp_pair(b, p)
                    u = 2 * p
                    if not last:
                        if u == 2:
                            copy_xt(b + 1, 0)
                        if u == 6:
                            copy_xt(b + 1, 1)
                        if u == 22:
                            copy_qk(b + 1, 0)
                        if u == 38:
                            copy_qk(b + 1, 1)
                        if u == 42:
                            copy_qk(b + 1, 2)
                        if u == 46:
                            copy_qk(b + 1, 3)
                        if u == 50:
                            copy_v(b + 1, 0)
                        if u == 54:
                            copy_v(b + 1, 1)
                    if not first:
                        if u == 30:
                            copy_tokens(b - 1, 0)
                        if u == 34:
                            copy_tokens(b - 1, 1)
                        if u == 64:
                            copy_rows(b - 1)
                        if u == 72:
                            gate_exponentials(b - 1)
                    if u % UNITS == 26 and not (last and u > 96):
                        copy_m(b, u // UNITS + 1)

            batch(0, True, False)
            with act.Fori(1, B - 1) as b:
                batch(b, False, False)
            batch(B - 1, False, True)
            copy_tokens(B - 1, 0)
            copy_tokens(B - 1, 1)
            copy_rows(B - 1)
            gate_exponentials(B - 1)

            def block_act(r, s):
                i = XR * r + s
                wait(act, blk_tr, i + 1)
                wait(act, hid_psum, i - 1)
                nc.scalar.activation(blk_xt[:, s % 2, :], ps_xt[:, s % 2, 0:P], ACT.Copy).then_inc(blk_tr_copied, 1)
                wait(act, hid_psum, i + 1)
                wait(act, y_psum, i - 1)
                nc.scalar.activation(hid[:, s % 2, :], ps_h[:, s % 2, :], ACT.Relu).then_inc(hid_done, 1)

            for s in range(XR):
                block_act(0, s)
            with act.Fori(1, BLOCKS // XR) as r:
                for s in range(XR):
                    block_act(r, s)

        @block.vector
        def _(dve):
            dve.wait_ge(setup, SETUP)
            at_i = 0
            for dst, num in ((e_rev[:, :, :].rearrange("p j e -> p (j e)"), TB * E), (reg_base[:, :], E),
                             (dest_f[:, :, :].rearrange("p j k -> p (j k)"), TB * 2), (part_no[:, :], 1),
                             (blk_no[:, :], 3)):
                nc.vector.tensor_copy(dst, iota_i[:, at_i:at_i + num]).then_inc(setup_v, 1)
                at_i += num
            nc.vector.tensor_copy(base[:, :], iota_i[:, TB * E:TB * E + E]).then_inc(setup_v, 1)
            dve.wait_ge(weights_in, WEIGHTS)
            for o in range(2):
                nc.vector.tensor_copy(wq_r[:, o, :].rearrange("c (g d h) -> c g d h", g=G, d=D),
                                      wq_in[:, o].rearrange("c (g h) d -> c g d h", g=G)).then_inc(setup_v, 1)
            dve.wait_ge(wg_mean, 1)
            nc.vector.tensor_tensor(out=wg_c[:, :], in0=misc[:, 0:E], in1=wg_sb[:, :],
                                    op=ALU.subtract).then_inc(setup_v, 1)
            dve.wait_ge(setup_v, 9)
            nc.vector.tensor_scalar(wg_c[:, :], wg_c[:, :], -1.0, None, ALU.mult).then_inc(setup_v, 1)

            def take_max(b, m):
                s, u = m // UNITS, m % UNITS
                wait(dve, max_ready, SLOTS * b + m + 1)
                nc.vector.tensor_reduce(out=m_red[:, s % 2, u:u + 1], in_=ps_max[:, m % 2, :], axis=AX.X,
                                        op=ALU.max).then_inc(max_taken, 1)

            def row_maxima(b, s):
                k = STAGES * b + s
                wait(dve, max_taken, UNITS * (k + 1))
                wait(dve, m_split, 3 * (k - 1))
                nc.vector.tensor_reduce(out=m_neg[:, s % 2, :],
                                        in_=m_red[:, s % 2, :].rearrange("p (n s) -> p n s", s=2),
                                        axis=AX.X, op=ALU.max, negate=True).then_inc(m_ready, 1)

            def divide(b, s, step):
                k = STAGES * b + s
                g, half = s % STAGES // 2, s % 2
                wait(dve, norm_steps, 4 * k + step)
                if step == 0:
                    wait(dve, pv_done, 8 * (k + 1))
                    nc.vector.transpose(o_t[:, :, :].rearrange("p n d -> p (n d)"), ps_pv[:, :]).then_inc(norm_steps, 1)
                if step == 1:
                    nc.vector.reciprocal(o_rec[:, :], o_t[:, :, D]).then_inc(norm_steps, 1)
                if step == 2:
                    nc.vector.tensor_tensor(out=o_n[:, :, 0:D], in0=o_t[:, :, 0:D],
                                            in1=o_rec[:, :].unsqueeze(2).to_broadcast([P, HALF // 32, D]),
                                            op=ALU.mult).then_inc(norm_steps, 1)
                if step == 3:
                    wait(dve, pj_psum, 2 * b if s >= 0 else 2 * (b - 1))
                    nc.vector.transpose(att[:, g, half * HALF:(half + 1) * HALF],
                                        o_n[:, :, :].rearrange("p n d -> p (n d)")).then_inc(norm_steps, 1)

            def norm_stats(b, which, copied, done, half):
                src = xt if which == 0 else tok
                wait(dve, copied, 2 * b + half + 1)
                for j in range(4 * half, 4 * half + 4):
                    nc.vector.bn_stats(stats[:, which, j, :], src[:, j, :]).then_inc(done, 1)
                if half:
                    wait_apart(dve, dve_passed, done, 16 * b + TB)
                    for j in range(TB):
                        nc.vector.bn_aggr(mean_var[:, which, j, :], stats[:, which, j:j + 1, :]).then_inc(done, 1)

            def add_residual(b, half):
                cols = slice(half * HALF, (half + 1) * HALF)
                wait(dve, pj_psum, 2 * b + half + 1)
                wait(dve, res_ready, b + 1)
                nc.vector.tensor_tensor(out=x1[:, cols], in0=misc[:, :], in1=res[:, cols],
                                        op=ALU.add).then_inc(x1_ready, 1)

            def wide(t, n=E):
                return t.unsqueeze(2).to_broadcast([P, TB, n])

            def choose(b):
                count = [0]

                def step(inst):
                    inst.then_inc(route_a, 1)
                    count[0] += 1
                    wait(dve, route_a, ROUTE_A * b + count[0])

                m1, m2, m2s = (masks[:, :, i, :] for i in range(3))
                wait(dve, lg_psum, b + 1)
                wait(dve, ln2_scale, 3 * (b + 1))
                nc.vector.tensor_tensor(out=gat[:, :, :], in0=misc[:, 0:TB * E].rearrange("p (j e) -> p j e", j=TB),
                                        in1=wide(rstd[:, 1, :]), op=ALU.mult).then_inc(lg_taken, 1)
                wait(dve, lg_taken, b + 1)
                step(nc.vector.tensor_reduce(out=small[:, 0, :], in_=gat[:, :, :], axis=AX.X, op=ALU.max))
                nc.vector.tensor_tensor(out=gat[:, :, :], in0=gat[:, :, :], in1=wide(small[:, 0, :]),
                                        op=ALU.subtract).then_inc(gate_shifted, 1)

            def choose2(b):
                count = [1]

                def step(inst):
                    inst.then_inc(route_a, 1)
                    count[0] += 1
                    wait(dve, route_a, ROUTE_A * b + count[0])

                m1, m2, m2s = (masks[:, :, i, :] for i in range(3))
                wait(dve, gate_exp, b + 1)
                step(nc.vector.tensor_reduce(out=small[:, 1, :], in_=tmp[:, :, :], axis=AX.X, op=ALU.add))
                step(nc.vector.reciprocal(small[:, 2, :], small[:, 1, :]))
                step(nc.vector.tensor_tensor(out=gat[:, :, :], in0=tmp[:, :, :], in1=wide(small[:, 2, :]), op=ALU.mult))
                for i, mask in ((0, m1), (1, m2)):
                    step(nc.vector.tensor_reduce(out=small[:, 3 + i, :], in_=gat[:, :, :], axis=AX.X, op=ALU.max))
                    step(nc.vector.tensor_tensor(out=tmp[:, :, :], in0=gat[:, :, :], in1=wide(small[:, 3 + i, :]),
                                                 op=ALU.is_ge))
                    step(nc.vector.tensor_tensor(out=tmp[:, :, :], in0=tmp[:, :, :], in1=e_rev[:, :, :], op=ALU.mult))
                    step(nc.vector.tensor_reduce(out=small[:, 5, :], in_=tmp[:, :, :], axis=AX.X, op=ALU.max))
                    step(nc.vector.tensor_tensor(out=mask, in0=tmp[:, :, :], in1=wide(small[:, 5, :]),
                                                 op=ALU.is_equal))
                    if i == 0:
                        step(nc.vector.tensor_scalar(tmp[:, :, :], mask, -1.0, 1.0, ALU.mult, ALU.add))
                        step(nc.vector.tensor_tensor(out=gat[:, :, :], in0=gat[:, :, :], in1=tmp[:, :, :],
                                                     op=ALU.mult))
                step(nc.vector.tensor_copy(m2s, m2))
                step(nc.vector.tensor_tensor(out=small[:, 6, :], in0=m1[:, :, 0], in1=m2[:, :, 0], op=ALU.mult))
                step(nc.vector.tensor_tensor(out=m2s[:, :, 0], in0=m2[:, :, 0], in1=small[:, 6, :], op=ALU.subtract))
                step(nc.vector.tensor_tensor(out=m2s[:, :, 1], in0=m2[:, :, 1], in1=small[:, 6, :], op=ALU.add))
                nc.vector.tensor_copy(masks_b[:, :, :], masks[:, :, :, :].rearrange(
                    "p j m e -> p j (m e)")).then_inc(masks_ready, 1)
                step(nc.vector.tensor_tensor(out=small[:, 7, :], in0=small[:, 3, :], in1=small[:, 4, :], op=ALU.add))
                step(nc.vector.tensor_scalar(small[:, 7, :], small[:, 7, :], GATE_EPS, None, ALU.add))
                step(nc.vector.reciprocal(small[:, 7, :], small[:, 7, :]))
                assert count[0] == ROUTE_A, count

            def place_rows(b):
                count = [0]

                def step(inst):
                    inst.then_inc(route_b, 1)
                    count[0] += 1
                    wait(dve, route_b, ROUTE_B * b + count[0])

                def over(t):
                    return t.unsqueeze(1).to_broadcast([P, TB, E])

                m1, m2, m2s = (masks[:, :, i, :] for i in range(3))
                wait(dve, cs_psum, b + 1)
                nc.vector.tensor_copy(counts[:, :], misc[:, 0:TB * 3 * E + 3 * E]).then_inc(cs_taken, 1)
                wait(dve, cs_taken, b + 1)
                step(nc.vector.tensor_tensor(out=tmp[:, :, :], in0=before[:, :, 0, :], in1=m1, op=ALU.mult))
                step(nc.vector.tensor_reduce(out=small[:, 8, :], in_=tmp[:, :, :], axis=AX.X, op=ALU.add))
                step(nc.vector.tensor_scalar(kept_n[:, :], totals[:, 0, :], float(CAP), None, ALU.min))
                step(nc.vector.tensor_tensor(out=tmp2[:, :, :], in0=before[:, :, 1, :], in1=over(kept_n[:, :]),
                                             op=ALU.add))
                step(nc.vector.tensor_tensor(out=tmp2[:, :, :], in0=tmp2[:, :, :], in1=m2, op=ALU.mult))
                step(nc.vector.tensor_reduce(out=small[:, 9, :], in_=tmp2[:, :, :], axis=AX.X, op=ALU.add))
                wait(dve, scattered, 256 * b)
                for k in range(2):
                    step(nc.vector.tensor_scalar(small[:, 8 + k, :], small[:, 8 + k, :], float(CAP), None, ALU.is_lt))
                    step(nc.vector.tensor_tensor(out=small[:, 10 + k, :], in0=small[:, 3 + k, :], in1=small[:, 7, :],
                                                 op=ALU.mult))
                    nc.vector.tensor_tensor(out=rows[:, k, :, C + 1], in0=small[:, 10 + k, :],
                                            in1=small[:, 8 + k, :], op=ALU.mult).then_inc(routed_parts, 1)
                    nc.vector.tensor_copy(rows_i[:, k, :, C], dest_f[:, :, k]).then_inc(routed_parts, 1)
                step(nc.vector.tensor_tensor(out=base2[:, :], in0=base[:, :], in1=totals[:, 0, :], op=ALU.add))
                for k, mask, start in ((0, m1, base), (1, m2s, base2)):
                    step(nc.vector.tensor_tensor(out=tmp[:, :, :], in0=before[:, :, 2 * k, :], in1=over(start[:, :]),
                                                 op=ALU.add))
                    step(nc.vector.tensor_tensor(out=tmp[:, :, :], in0=tmp[:, :, :], in1=mask, op=ALU.mult))
                    step(nc.vector.tensor_reduce(out=small[:, 8 + k, :], in_=tmp[:, :, :], axis=AX.X, op=ALU.add))
                step(nc.vector.tensor_tensor(out=base[:, :], in0=base2[:, :], in1=totals[:, 2, :], op=ALU.add))
                wait(dve, routed_parts, 4 * (b + 1))
                nc.vector.tensor_scalar(dest_f[:, :, :], dest_f[:, :, :], float(T), None,
                                        ALU.add).then_inc(dest_next, 1)
                nc.vector.tensor_copy(place[:, :, :], small[:, 8:10, :]).then_inc(routed, 1)
                wait(dve, dest_next, b + 1)
                assert count[0] == ROUTE_B, count

            for half in range(2):
                norm_stats(0, 0, xt_copied, ln1_stats, half)
            for m in range(LEAD):
                take_max(0, m)
                if m == UNITS:
                    row_maxima(0, 0)

            def batch(b, first, last):
                for u in range(SLOTS):
                    m = u + LEAD
                    if not (last and m >= SLOTS):
                        take_max(b, m)
                    if m % UNITS == 0 and not (last and m > SLOTS):
                        row_maxima(b, m // UNITS - 1)
                    if 4 <= u % UNITS < 8 and not (first and u < UNITS):
                        divide(b, u // UNITS - 1, u % UNITS - 4)
                    if not last:
                        if u == 3:
                            norm_stats(b + 1, 0, xt_copied, ln1_stats, 0)
                        if u == 8:
                            norm_stats(b + 1, 0, xt_copied, ln1_stats, 1)
                    if not first:
                        if u == 13:
                            add_residual(b - 1, 0)
                        if u == 17:
                            add_residual(b - 1, 1)
                        if u == 31:
                            norm_stats(b - 1, 1, tok_copied, ln2_stats, 0)
                        if u == 35:
                            norm_stats(b - 1, 1, tok_copied, ln2_stats, 1)
                        if u == 66:
                            choose(b - 1)
                        if u == 76:
                            choose2(b - 1)
                        if u == 97:
                            place_rows(b - 1)

            batch(0, True, False)
            with dve.Fori(1, B - 1) as b:
                batch(b, False, False)
            batch(B - 1, False, True)
            for step in range(4):
                divide(B, -1, step)
            add_residual(B - 1, 0)
            add_residual(B - 1, 1)
            norm_stats(B - 1, 1, tok_copied, ln2_stats, 0)
            norm_stats(B - 1, 1, tok_copied, ln2_stats, 1)
            choose(B - 1)
            choose2(B - 1)
            place_rows(B - 1)
            nc.vector.tensor_scalar(pad_place[:, :], base[:, :], part_no[:, 0:1], None, ALU.add).then_inc(pads_ready, 1)

            tabs = 0

            def tab(inst):
                nonlocal tabs
                tabs += 1
                inst.then_inc(tab_steps, 1)
                dve.wait_ge(tab_steps, tabs)

            rows_n, blocks_n, ends = (blk_f[:, i, 0:E] for i in range(3))
            le = blk_f[:, 3, :].rearrange("p (c e) -> p c e", c=3)
            lb = blk_f[:, 4, :].rearrange("p (c e) -> p c e", c=3)
            e_of, before_of, row_of = (blk_f[:, 5, 3 * i:3 * i + 3] for i in range(3))

            def three(t):
                return t.unsqueeze(1).to_broadcast([P, 3, E])

            tab(nc.vector.tensor_tensor(out=rows_n, in0=base[:, :], in1=reg_base[:, :], op=ALU.subtract))
            tab(nc.vector.tensor_scalar(blk_n[:, :], rows_n, float(P - 1), None, ALU.add))
            tab(nc.vector.tensor_single_scalar(blk_n[:, :], blk_n[:, :], 7, op=ALU.logical_shift_right))
            tab(nc.vector.tensor_copy(blocks_n, blk_n[:, :]))
            tab(nc.vector.tensor_tensor_scan(out=ends, data0=ones_e[:, :], data1=blocks_n, initial=0.0,
                                             op0=ALU.mult, op1=ALU.add))
            tab(nc.vector.tensor_tensor(out=le, in0=three(ends), in1=blk_no[:, :].unsqueeze(2).to_broadcast([P, 3, E]),
                                        op=ALU.is_le))
            tab(nc.vector.tensor_reduce(out=e_of, in_=le, axis=AX.X, op=ALU.add))
            tab(nc.vector.tensor_tensor(out=lb, in0=le, in1=three(blocks_n), op=ALU.mult))
            tab(nc.vector.tensor_reduce(out=before_of, in_=lb, axis=AX.X, op=ALU.add))
            tab(nc.vector.tensor_tensor(out=row_of, in0=blk_no[:, :], in1=before_of, op=ALU.subtract))
            tab(nc.vector.tensor_scalar(row_of, row_of, float(P), None, ALU.mult))
            tab(nc.vector.tensor_scalar(before_of, e_of, float(REG), None, ALU.mult))
            tab(nc.vector.tensor_tensor(out=row_of, in0=row_of, in1=before_of, op=ALU.add))
            tab(nc.vector.tensor_scalar(blk_i[:, 1, :], row_of, float(E * REG), None, ALU.min))
            tab(nc.vector.tensor_scalar(blk_i[:, 0, :], e_of, float(E - 1), None, ALU.min))
            assert tabs == TAB_STEPS, tabs

            dve.wait_ge(tab_in, 16)
            dve.wait_ge(w1_loaded, 16)
            dve.wait_ge(w2_loaded, 16)
            dve.wait_ge(pj_psum, 2 * B)

            def copy_weights(i, s):
                e = dve.value_load(table[0:1, 0, i:i + 1] if isinstance(i, int) else table[0:1, 0, bass.ds(i, 1)],
                                   min_val=0, max_val=E - 1)
                wait(dve, hid_psum, i - 1)
                nc.vector.tensor_copy(w1_blk[:, s % 2, :], w1_all[:, bass.ds(e, 1), :].rearrange(
                    "p a h -> p (a h)")).then_inc(w1_copied, 1)
                wait(dve, y_psum, i - 1)
                nc.vector.tensor_copy(w2_blk[:, s % 2, :], w2_all[:, bass.ds(e, 1), :, :].rearrange(
                    "p a c d -> p (a c d)")).then_inc(w2_copied, 1)

            def scale_y(r, s):
                i = XR * r + s
                wait(dve, y_stored[s], 16 * r)
                wait(dve, blk_loaded[s], 16 * (r + 1))
                nc.vector.tensor_copy(blk_dest[:, s:s + 1], blk_in[:, s, C:C + 1].bitcast(I32)).then_inc(dest_copied, 1)
                wait(dve, y_psum, i + 1)
                nc.vector.tensor_scalar(blk_y[:, s, :], ps_o[:, s % 2, 0:P], blk_in[:, s, C + 1:C + 2], None,
                                        ALU.mult).then_inc(y_scaled, 1)

            copy_weights(0, 0)
            for s in range(XR):
                copy_weights(s + 1, s + 1)
                scale_y(0, s)
            with dve.Fori(1, BLOCKS // XR - 1) as r:
                for s in range(XR):
                    copy_weights(XR * r + s + 1, s + 1)
                    scale_y(r, s)
            r = BLOCKS // XR - 1
            for s in range(XR):
                if s < XR - 1:
                    copy_weights(XR * r + s + 1, s + 1)
                scale_y(r, s)

            def sum_y(r, s):
                b = 2 * r + s
                wait(dve, y_loaded[s], 32 * (r + 1))
                nc.vector.tensor_tensor(out=y_in[:, s, 0], in0=y_in[:, s, 0], in1=y_in[:, s, 1],
                                        op=ALU.add).then_inc(y_summed, 1)

            def add_x1(r, s):
                b = 2 * r + s
                wait(dve, out_stored[s], 16 * r)
                for half in range(2):
                    cols = slice(half * HALF, (half + 1) * HALF)
                    wait(dve, yt_psum, 2 * b + half + 1)
                    res_b = (x1_all[:, b, cols] if isinstance(b, int) else x1_all[:, bass.ds(b, 1), cols].rearrange(
                        "p a t -> p (a t)"))
                    nc.vector.tensor_tensor(out=o_buf[:, s, cols], in0=ps_score[:, s, half, :], in1=res_b,
                                            op=ALU.add).then_inc(out_ready, 1)

            dve.wait_ge(x1_stored, 16 * B)
            def image_pair(r):
                sum_y(r, 1)
                add_x1(r, 0)
                sum_y(r + 1, 0)
                add_x1(r, 1)

            sum_y(0, 0)
            image_pair(0)
            with dve.Fori(1, B // 2 - 1) as r:
                image_pair(r)
            r = B // 2 - 1
            sum_y(r, 1)
            add_x1(r, 0)
            add_x1(r, 1)

        @block.tensor
        def _(pe):
            freed = [None]

            def misc_free(sem_, value):
                if freed[0] is not None:
                    pe.wait_ge(*freed[0])
                freed[0] = (sem_, value)

            def transpose_x(b, half):
                misc_free(xt_copied, 2 * b + half + 1)
                wait(pe, x_loaded, 16 * (b + 1))
                for j in range(4):
                    last = nc.tensor.transpose(misc[:, j * P:(j + 1) * P],
                                               x_in[:, (4 * half + j) * P:(4 * half + j + 1) * P], ident[:, :])
                last.then_inc(xt_psum, 1)

            def project_qk(b, i):
                o, half = i // 2, i % 2
                misc_free(qk_copied, 4 * b + i + 1)
                wait(pe, xt_normed, TB * (b + 1))
                nc.tensor.matmul(misc[:, :], wq_r[:, o, :], xt[:, 4 * half:4 * half + 4, :], start=True,
                                 stop=True).then_inc(qk_psum, 1)

            def project_v(b, half):
                misc_free(v_copied, 2 * b + half + 1)
                for j in range(4):
                    last = nc.tensor.matmul(misc[:, j * P:(j + 1) * P], xt[:, 4 * half + j, :], wv_sb[:, :, :],
                                            start=True, stop=True)
                last.then_inc(v_psum, 1)

            def max_unit(b, m):
                s, u = m // UNITS, m % UNITS
                bb = b + s // STAGES
                g, half = s % STAGES // 2, s % 2
                h, t, kh = u // 8, u // 2 % 4, u % 2
                if u == 0 and half == 0:
                    wait(pe, stacked[g], 192 * (bb + 1))
                wait(pe, max_taken, SLOTS * b + m - 1)
                nc.tensor.matmul(ps_max[:, m % 2, :], qs[0:STACK, g, h, half * HALF + t * P:half * HALF + (t + 1) * P],
                                 ks[0:STACK, g, h, kh * HALF:(kh + 1) * HALF], start=True,
                                 stop=True).then_inc(max_ready, 1)

            def rows_of_maxima(b, s):
                k = STAGES * b + s
                misc_free(m_copied, k + 1)
                wait(pe, m_split, 3 * (k + 1))
                for t in range(4):
                    last = nc.tensor.matmul(misc[STACK:STACK + MROWS, t * P:(t + 1) * P],
                                            m_parts[:, t, :, :].rearrange("p a h -> p (a h)"), ident_b[:, :],
                                            start=True, stop=True)
                last.then_inc(m_psum, 1)

            def score_unit(b, u):
                s = u // UNITS
                g, half = s // 2, s % 2
                i, h = u % UNITS // HG, u % HG
                if u % UNITS == 0:
                    wait(pe, m_loaded, 64 * (STAGES * b + s + 1))
                if u % 2 == 0:
                    wait(pe, exp_done, 64 * b + u // 2 - 1)
                mm = nc.tensor.matmul(ps_score[:, u // 2 % 2, u % 2, :],
                                      ks[0:STACK + MROWS, g, h, i * P:(i + 1) * P],
                                      qs[0:STACK + MROWS, g, h, half * HALF:(half + 1) * HALF], start=True, stop=True)
                if u % 2:
                    mm.then_inc(scores_ready, 1)

            def weigh(b, n):
                s, i = n // 8, n % 8
                g = s % STAGES // 2
                bb = b + s // STAGES
                if i == 0:
                    wait(pe, norm_steps, 4 * (STAGES * b + s - 1) + 1)
                    wait(pe, v_placed, 2 * bb + g + 1)
                wait(pe, exp_done, 64 * b + 2 * n + 2)
                for h in range(HG):
                    last = nc.tensor.matmul(ps_pv[32 * h:32 * h + 32, :], v_pad[:, i, HG * g + h, :],
                                            probs[:, (4 * n + h) % PRING, :], start=(i == 0), stop=(i == TB - 1))
                last.then_inc(pv_done, 1)

            def project_out(b, half):
                misc_free(x1_ready, 2 * b + half + 1)
                wait(pe, norm_steps, 16 * (b + 1))
                for j in range(4):
                    for g in range(G):
                        last = nc.tensor.matmul(misc[:, j * P:(j + 1) * P],
                                                att[:, g, (4 * half + j) * P:(4 * half + j + 1) * P],
                                                wp_sb[:, g, :], start=(g == 0), stop=(g == G - 1))
                last.then_inc(pj_psum, 1)

            def transpose_tokens(b, half):
                misc_free(tok_copied, 2 * b + half + 1)
                wait(pe, x1_ready, 2 * b + half + 1)
                for j in range(4):
                    last = nc.tensor.transpose(misc[:, j * P:(j + 1) * P],
                                               x1[:, (4 * half + j) * P:(4 * half + j + 1) * P], ident[:, :])
                last.then_inc(tt_psum, 1)

            def logits(b):
                misc_free(lg_taken, b + 1)
                for j in range(TB):
                    last = nc.tensor.matmul(misc[:, j * E:(j + 1) * E], x1[:, j * P:(j + 1) * P], wg_c[:, :],
                                            start=True, stop=True)
                last.then_inc(lg_psum, 1)

            def count_tokens(b):
                w = 3 * E
                misc_free(cs_taken, b + 1)
                wait(pe, masks_ready, b + 1)
                nc.tensor.matmul(misc[:, 0:TB * w], tri_b[:, :], masks_b[:, :, :], start=True, stop=False)
                for d in range(1, TB):
                    nc.tensor.matmul(misc[:, d * w:TB * w], ones_b[:, :], masks_b[:, 0:TB - d, :], start=False,
                                     stop=(d == TB - 1))
                for j in range(TB):
                    last = nc.tensor.matmul(misc[:, TB * w:(TB + 1) * w], ones_b[:, :], masks_b[:, j, :],
                                            start=(j == 0), stop=(j == TB - 1))
                last.then_inc(cs_psum, 1)

            pe.wait_ge(setup, SETUP)
            pe.wait_ge(weights_in, WEIGHTS)
            nc.tensor.matmul(misc[:, 0:E], mean_m[:, :], wg_sb[:, :], start=True, stop=True).then_inc(wg_mean, 1)
            pe.wait_ge(setup_v, 10)
            transpose_x(0, 0)
            transpose_x(0, 1)
            for i in range(4):
                project_qk(0, i)
            project_v(0, 0)
            project_v(0, 1)
            for m in range(LEAD):
                max_unit(0, m)
                if m == 37:
                    rows_of_maxima(0, 0)

            def batch(b, first, last):
                freed[0] = (m_copied, STAGES * b + 1)
                for u in range(SLOTS):
                    score_unit(b, u)
                    if not (last and u + LEAD >= SLOTS):
                        max_unit(b, u + LEAD)
                    if u % 4 == 3 and not (first and u == 3):
                        weigh(b, u // 4 - 1)
                    if not last:
                        if u == 1:
                            transpose_x(b + 1, 0)
                        if u == 5:
                            transpose_x(b + 1, 1)
                        if u == 21:
                            project_qk(b + 1, 0)
                        if u == 37:
                            project_qk(b + 1, 1)
                        if u == 41:
                            project_qk(b + 1, 2)
                        if u == 45:
                            project_qk(b + 1, 3)
                        if u == 49:
                            project_v(b + 1, 0)
                        if u == 53:
                            project_v(b + 1, 1)
                    if not first:
                        if u == 13:
                            project_out(b - 1, 0)
                        if u == 17:
                            project_out(b - 1, 1)
                        if u == 29:
                            transpose_tokens(b - 1, 0)
                        if u == 33:
                            transpose_tokens(b - 1, 1)
                        if u == 65:
                            logits(b - 1)
                        if u == 96:
                            count_tokens(b - 1)
                    if u % UNITS == 25 and not (last and u > 96):
                        rows_of_maxima(b, u // UNITS + 1)

            batch(0, True, False)
            with pe.Fori(1, B - 1) as b:
                batch(b, False, False)
            batch(B - 1, False, True)
            weigh(B, -1)
            project_out(B - 1, 0)
            project_out(B - 1, 1)
            transpose_tokens(B - 1, 0)
            transpose_tokens(B - 1, 1)
            logits(B - 1)
            count_tokens(B - 1)

            def hidden(r, s):
                i = XR * r + s
                wait(pe, blk_loaded[s], 16 * (r + 1))
                wait(pe, blk_tr_copied, i - 1)
                nc.tensor.transpose(ps_xt[:, s % 2, 0:P], blk_in[:, s, 0:C], ident[:, :]).then_inc(blk_tr, 1)
                wait(pe, blk_tr_copied, i + 1)
                wait(pe, w1_copied, i + 1)
                wait(pe, hid_done, i - 1)
                for c in range(HC):
                    last = nc.tensor.matmul(ps_h[:, s % 2, c * P:(c + 1) * P], w1_blk[:, s % 2, c * P:(c + 1) * P],
                                            blk_xt[:, s % 2, :], start=True, stop=True)
                last.then_inc(hid_psum, 1)

            def outputs(i, s):
                wait(pe, hid_done, i + 1)
                wait(pe, w2_copied, i + 1)
                wait(pe, y_scaled, i - 1)
                for c in range(HC):
                    last = nc.tensor.matmul(ps_o[:, s % 2, 0:P], hid[:, s % 2, c * P:(c + 1) * P],
                                            w2_blk[:, s % 2, c * P:(c + 1) * P], start=(c == 0), stop=(c == HC - 1))
                last.then_inc(y_psum, 1)

            for s in range(XR):
                hidden(0, s)
                if s:
                    outputs(s - 1, s - 1)
            with pe.Fori(1, BLOCKS // XR) as r:
                for s in range(XR):
                    hidden(r, s)
                    outputs(XR * r + s - 1, s - 1)
            outputs(BLOCKS - 1, XR - 1)

            def transpose_y(r, s):
                b = 2 * r + s
                wait(pe, y_summed, b + 1)
                wait(pe, out_ready, 2 * (b - 1))
                for j in range(TB):
                    last = nc.tensor.transpose(ps_score[:, s, j // 4, j % 4 * P:(j % 4 + 1) * P], y_in[:, s, 0, j, :],
                                               ident[:, :])
                    if j % 4 == 3:
                        last.then_inc(yt_psum, 1)

            pe.wait_ge(hid_done, BLOCKS)
            for s in range(2):
                transpose_y(0, s)
            with pe.Fori(1, B // 2) as r:
                for s in range(2):
                    transpose_y(r, s)


_INS = ['x', 'L0_conv_Wq', 'L0_conv_Wk', 'L0_conv_Wv', 'L0_conv_Wproj', 'L0_conv_bproj', 'L0_ffn_w_gating',
        'L0_ffn_w1', 'L0_ffn_w2']
_OUTS = [((16, 128, 32, 32), 'float32')]


def kernel(**inputs):
    import numpy as _np
    import concourse.bacc as _bacc
    from concourse import mybir as _mybir
    from concourse.bass_utils import run_bass_kernel_spmd as _run

    nc = _bacc.Bacc("TRN2", target_bir_lowering=False, num_devices=1)
    arrays, args = {}, []
    for name in _INS:
        a = _np.ascontiguousarray(inputs[name])
        arrays[f"in_{name}_dram"] = a
        args.append(nc.dram_tensor(f"in_{name}_dram", a.shape, _mybir.dt.from_np(a.dtype), kind="ExternalInput").ap())
    for i, (shape, dtype) in enumerate(_OUTS):
        dt = _mybir.dt.from_np(_np.dtype(dtype))
        args.append(nc.dram_tensor(f"out_{i}_dram", shape, dt, kind="ExternalOutput").ap())
    metaformer(nc, *args)
    r = _run(nc, [arrays], core_ids=[0])
    got = tuple(r.results[0][f"out_{i}_dram"] for i in range(len(_OUTS)))
    return got[0]
```

```python
from contextlib import ExitStack

import concourse.bass as bass
from concourse import mybir

FP32 = mybir.dt.float32
BF16 = mybir.dt.bfloat16
I32 = mybir.dt.int32
ALU = mybir.AluOpType
ACT = mybir.ActivationFunctionType
AX = mybir.AxisListType

P = 128
B, C, T = 16, 128, 1024
H, D = 8, 16
HG = 4
G = H // HG
TB = T // P
HALF = T // 2
SCALE = 1.0 / float(D) ** 0.5
LN1_EPS, LN2_EPS = 1e-6, 1e-5

STAGES = G * 2
UNITS = TB * HG
SLOTS = STAGES * UNITS
LEAD = 44
RING = 3
PRING = 16
ALL_STAGES = B * STAGES

Q_PART = (0, 0, 1, 1, 0, 2)
K_PART = (0, 1, 0, 1, 2, 0)
STACK = 16 * len(Q_PART)
MPARTS = 2
MROWS = MPARTS * HG

E = 16
HID = 512
HC = HID // P
CAP = T * 2 * 2 // E
GATE_EPS = 1e-9
REG = B * T + P
ROWW = C + 4
SKIP = 1 << 20
BLOCKS = 2 * B * T // P + E
XR = 8
WR = 4
WLEAD = 2
TAB_STEPS = 15
ROUTE_A, ROUTE_B = 23, 18


def wait(eng, sem, value):
    if isinstance(value, int) and value <= 0:
        return
    eng.wait_ge(sem, value)


def wait_apart(eng, passed, sem, value):
    wait(eng, sem, value)
    if not isinstance(value, int):
        eng.sem_inc(passed, 1)


def ring_free(n):
    return n - RING + 1 if n % SLOTS >= SLOTS % RING else n - SLOTS % RING + 1


def metaformer(nc, x, wq, wk, wv, wproj, bproj, wgate, w1, w2, out):
    ctx = ExitStack()
    with ctx:
        def sb(name, shape, dt=FP32):
            return ctx.enter_context(nc.sbuf_tensor("sb_" + name, shape, dt))

        def sem(name):
            return ctx.enter_context(nc.semaphore(name))

        x_v = x.rearrange("b c h w -> b c (h w)")
        out_v = out.rearrange("b c h w -> b c (h w)")
        sorted_rows = nc.dram_tensor("sorted_rows", (E * REG + P, ROWW), FP32, kind="Internal").ap()
        expert_out = nc.dram_tensor("expert_out", (2 * B * T, C), FP32, kind="Internal").ap()
        table_dram = nc.dram_tensor("table_dram", (2, 3 * P), I32, kind="Internal").ap()

        arena_a = sb("arena_a", [P, PRING * HALF])
        probs = arena_a[:, :].rearrange("p (u t) -> p u t", u=PRING)
        w1_all = arena_a[:, :].rearrange("p (e h) -> p e h", e=E)
        y_in = arena_a[:, 0:4 * T].rearrange("p (s k j d) -> p s k j d", s=2, k=2, j=TB)
        o_buf = arena_a[:, 4 * T:6 * T].rearrange("p (s t) -> p s t", s=2)
        arena_b = sb("arena_b", [P, 2 * G * HG * T], BF16)
        stacks = arena_b[:, :].rearrange("p (o g h t) -> p o g h t", o=2, g=G, h=HG)
        qs, ks = stacks[:, 0], stacks[:, 1]
        w2_all = arena_b[:, :].bitcast(FP32).rearrange("p (e c d) -> p e c d", e=E, c=HC)
        arena_c = sb("arena_c", [P, 3 * T + 2 * T])
        parts = arena_c[:, 0:3 * T].bitcast(BF16).rearrange("p (o l t) -> p o l t", o=2, l=3)
        att = arena_c[:, 3 * T:5 * T].rearrange("p (g t) -> p g t", g=G)
        at = 0

        def cut(n):
            nonlocal at
            at += n
            return arena_c[:, at - n:at]
        w1_blk = cut(WR * HID).rearrange("p (s h) -> p s h", s=WR)
        w2_blk = cut(WR * HID).rearrange("p (s h) -> p s h", s=WR)
        hid = cut(2 * HID).rearrange("p (s h) -> p s h", s=2)

        x1_all = sb("x1_all", [P, B, T])
        x_in = sb("x_in", [P, T])
        xt = sb("xt", [P, TB, P])
        res = sb("res", [P, T])
        x1 = res
        tok = sb("tok", [P, TB, P])
        rows = sb("rows", [P, 2, TB, ROWW])
        rows_i = rows[:, :, :, :].rearrange("p k j w -> p (k j w)").bitcast(I32).rearrange(
            "p (k j w) -> p k j w", k=2, j=TB)
        qk_f = sb("qk_f", [P, 2, HALF])
        v_st = sb("v_st", [P, TB, H, D])
        arena_d = sb("arena_d", [P, TB * H * 32])
        v_pad = arena_d[:, :].rearrange("p (j h d) -> p j h d", j=TB, h=H)
        blk_in = arena_d[:, 0:XR * ROWW].rearrange("p (s w) -> p s w", s=XR)
        blk_y = arena_d[:, XR * ROWW:XR * ROWW + WR * P].rearrange("p (s d) -> p s d", s=WR)
        blk_xt = arena_d[:, XR * ROWW + WR * P:XR * ROWW + (WR + 2) * P].rearrange("p (s d) -> p s d", s=2)
        blk_dest = arena_d[:, XR * ROWW + (WR + 2) * P:XR * ROWW + (WR + 2) * P + WR].bitcast(I32)
        o_t = sb("o_t", [P, HALF // 32, 32])
        o_n = sb("o_n", [P, HALF // 32, 32])
        o_rec = sb("o_rec", [P, HALF // 32])
        m_red = sb("m_red", [P, 2, UNITS])
        m_neg = sb("m_neg", [P, 2, HG * HG])
        m_rest = sb("m_rest", [P, HG * HG])
        m_parts = sb("m_parts", [P, HG, MPARTS, HG], BF16)
        m_row = sb("m_row", [P, HALF], BF16)
        stats = sb("stats", [P, 2, TB, 6])
        mean_var = sb("mean_var", [P, 2, TB, 2])
        ln_var = sb("ln_var", [P, 2, TB])
        rstd = sb("rstd", [P, 2, TB])
        neg_mean = sb("neg_mean", [P, 2, TB])
        gat = sb("gat", [P, TB, E])
        tmp = sb("tmp", [P, TB, E])
        tmp2 = sb("tmp2", [P, TB, E])
        masks = sb("masks", [P, TB, 3, E])
        masks_b = sb("masks_b", [P, TB, 3 * E], BF16)
        counts = sb("counts", [P, TB * 3 * E + 3 * E])
        before = counts[:, 0:TB * 3 * E].rearrange("p (j m e) -> p j m e", j=TB, m=3)
        totals = counts[:, TB * 3 * E:].rearrange("p (m e) -> p m e", m=3)
        small = sb("small", [P, 12, TB])
        kept_n = sb("kept_n", [P, E])
        base2 = sb("base2", [P, E])
        base = sb("base", [P, E])
        dest_f = sb("dest_f", [P, TB, 2])
        place = sb("place", [P, 2, TB], I32)
        pad_row = sb("pad_row", [P, ROWW])
        pad_place = sb("pad_place", [P, E], I32)
        blk_f = sb("blk_f", [P, 6, 3 * E])
        blk_n = sb("blk_n", [P, E], I32)
        blk_i = sb("blk_i", [P, 2, 3], I32)
        table = x_in[0:1, 0:6 * P].bitcast(I32).rearrange("o (n b) -> o n b", n=2)
        ident = sb("ident", [P, P])
        ident_b = sb("ident_b", [P, P], BF16)
        ones_b = sb("ones_b", [P, P], BF16)
        tri_b = sb("tri_b", [P, P], BF16)
        mean_m = tok[:, 0, :]
        neg_half = sb("neg_half", [P, TB])
        e_rev = sb("e_rev", [P, TB, E])
        reg_base = sb("reg_base", [P, E])
        part_no = sb("part_no", [P, 1])
        blk_no = sb("blk_no", [P, 3])
        ones_e = sb("ones_e", [P, E])
        iota_i = tok[:, 1:3, :].rearrange("p j c -> p (j c)").bitcast(I32)
        wq_in = o_t[:, 0:8, :].rearrange("p n d -> p (n d)").rearrange("p (o h d) -> p o h d", o=2, h=H)
        wq_r = sb("wq_r", [P, 2, P])
        wv_sb = sb("wv_sb", [P, H, D])
        wp_sb = sb("wp_sb", [P, G, C])
        bias = sb("bias", [P, C])
        wg_sb = sb("wg_sb", [P, E])
        wg_c = sb("wg_c", [P, E])

        banks = ctx.enter_context(nc.psum_tensor("banks", [P, 8, HALF], FP32))
        ps_score, ps_max = banks[:, 0:RING], banks[:, RING:2 * RING]
        ps_pv, misc = banks[:, 6], banks[:, 7]
        ps_h, ps_o, ps_xt = banks[:, 0:2], banks[:, 2:4], banks[:, 6:8]
        ps_y = banks[:, 0:4].rearrange("p (s h) t -> p s h t", s=2)

        setup = sem("setup")
        setup_v = sem("setup_v")
        weights_in = sem("weights_in")
        wg_mean = sem("wg_mean")
        x_loaded = sem("x_loaded")
        res_loaded = sem("res_loaded")
        xt_psum = sem("xt_psum")
        xt_copied = sem("xt_copied")
        ln1_stats = sem("ln1_stats")
        ln1_scale = sem("ln1_scale")
        xt_normed = sem("xt_normed")
        qk_psum = sem("qk_psum")
        qk_copied = sem("qk_copied")
        qk_parts = sem("qk_parts")
        stacked = [sem(f"stacked{g}") for g in range(G)]
        v_psum = sem("v_psum")
        v_copied = sem("v_copied")
        v_placed = sem("v_placed")
        max_ready = sem("max_ready")
        max_taken = sem("max_taken")
        m_ready = sem("m_ready")
        m_split = sem("m_split")
        m_psum = sem("m_psum")
        m_copied = sem("m_copied")
        m_loaded = sem("m_loaded")
        scores_ready = sem("scores_ready")
        exp_done = sem("exp_done")
        pv_done = sem("pv_done")
        norm_steps = sem("norm_steps")
        pj_psum = sem("pj_psum")
        res_ready = sem("res_ready")
        x1_ready = sem("x1_ready")
        x1_stored = sem("x1_stored")
        tt_psum = sem("tt_psum")
        tok_copied = sem("tok_copied")
        ln2_stats = sem("ln2_stats")
        ln2_scale = sem("ln2_scale")
        rows_normed = sem("rows_normed")
        rows_copied = sem("rows_copied")
        lg_psum = sem("lg_psum")
        lg_taken = sem("lg_taken")
        gate_shifted = sem("gate_shifted")
        gate_exp = sem("gate_exp")
        route_a = sem("route_a")
        masks_ready = sem("masks_ready")
        cs_psum = sem("cs_psum")
        cs_taken = sem("cs_taken")
        route_b = sem("route_b")
        routed_parts = sem("routed_parts")
        dest_next = sem("dest_next")
        routed = sem("routed")
        scattered = sem("scattered")
        pads_ready = sem("pads_ready")
        pads_written = sem("pads_written")
        tab_steps = sem("tab_steps")
        tab_out = sem("tab_out")
        tab_in = sem("tab_in")
        w1_loaded = sem("w1_loaded")
        w2_loaded = sem("w2_loaded")
        blk_loaded = [sem(f"blk_loaded{s}") for s in range(XR)]
        blk_tr = sem("blk_tr")
        blk_tr_copied = sem("blk_tr_copied")
        w1_copied = sem("w1_copied")
        w2_copied = sem("w2_copied")
        hid_psum = sem("hid_psum")
        hid_done = sem("hid_done")
        y_psum = sem("y_psum")
        dest_copied = sem("dest_copied")
        y_scaled = sem("y_scaled")
        y_stored = [sem(f"y_stored{s}") for s in range(WR)]
        y_loaded = [sem(f"y_loaded{s}") for s in range(2)]
        y_summed = sem("y_summed")
        yt_psum = sem("yt_psum")
        out_ready = sem("out_ready")
        out_stored = [sem(f"out_stored{s}") for s in range(2)]

        gp_passed = sem("gp_passed")
        sp_passed = sem("sp_passed")
        dve_passed = sem("dve_passed")

        SETUP = 27
        WEIGHTS = (2 + 1 + H + 1 + 1) * 16
        END_BLOCKS = BLOCKS - 1

        block = ctx.enter_context(nc.Block())

        @block.sync
        def _(sp):
            def load_x(b):
                wait_apart(sp, sp_passed, xt_psum, 2 * b)
                sp.dma_start(x_in[:, :], x_v[b] if isinstance(b, int) else x_v[bass.ds(b, 1)].rearrange(
                    "a c t -> (a c) t")).then_inc(x_loaded, 16)

            def load_res(b):
                wait_apart(sp, sp_passed, x1_stored, 16 * b)
                wait_apart(sp, sp_passed, lg_psum, b)
                wait_apart(sp, sp_passed, tt_psum, 2 * b)
                sp.dma_start(res[:, :], x_v[b] if isinstance(b, int) else x_v[bass.ds(b, 1)].rearrange(
                    "a c t -> (a c) t")).then_inc(res_loaded, 16)

            def stack(b, g):
                wait_apart(sp, sp_passed, qk_parts, 20 * (b + 1))
                wait_apart(sp, sp_passed, scores_ready, SLOTS * (b - 1) + 2 * UNITS * (g + 1))
                for o, part in ((0, Q_PART), (1, K_PART)):
                    for r, level in enumerate(part):
                        sp.dma_start(stacks[16 * r:16 * r + 16, o, g, :, :],
                                     parts[64 * g:64 * g + 64, o, level, :]).then_inc(stacked[g], 16)

            def load_m(b, s):
                g, half = s % STAGES // 2, s % 2
                wait_apart(sp, sp_passed, m_copied, STAGES * b + s + 1)
                sp.dma_start(qs[STACK:STACK + MROWS, g, :, half * HALF:(half + 1) * HALF],
                             m_row[STACK:STACK + MROWS, :].unsqueeze(1).to_broadcast([MROWS, HG, HALF])).then_inc(
                    m_loaded, 16)

            def store_x1(b):
                wait_apart(sp, sp_passed, x1_ready, 2 * (b + 1))
                dst = x1_all[:, b, :] if isinstance(b, int) else x1_all[:, bass.ds(b, 1), :].rearrange(
                    "p a t -> p (a t)")
                sp.dma_start(dst, x1[:, :]).then_inc(x1_stored, 16)

            for o, w in ((0, wq), (1, wk)):
                sp.dma_start(wq_in[:, o], w.rearrange("h c d -> c h d")).then_inc(weights_in, 16)
            sp.dma_start(x_in[:, :], x_v[0]).then_inc(x_loaded, 16)
            sp.dma_start(wv_sb[:, :, :], wv.rearrange("h c d -> c h d")).then_inc(weights_in, 16)
            sp.dma_start(bias[:, :], bproj.rearrange("(a c) -> a c", a=1).to_broadcast([P, C])).then_inc(weights_in, 16)
            sp.dma_start(wg_sb[:, :], wgate).then_inc(weights_in, 16)
            sp.wait_ge(setup, SETUP)
            for h in range(H):
                q = 32 * (h % HG)
                sp.dma_start(wp_sb[q:q + D, h // HG, :], wproj[h * D:(h + 1) * D, :]).then_inc(weights_in, 16)
            stack(0, 0)
            load_x(1)
            load_m(0, 0)

            def batch(b, first, last):
                stack(b, 1)
                if not first:
                    store_x1(b - 1)
                load_m(b, 1)
                if not last:
                    wait_apart(sp, sp_passed, xt_psum, 2 * (b + 2))
                    if not (isinstance(b, int) and b + 2 >= B):
                        load_x(b + 2)
                load_m(b, 2)
                if not last:
                    stack(b + 1, 0)
                load_res(b)
                load_m(b, 3)
                if not last:
                    load_m(b, 4)

            batch(0, True, False)
            with sp.Fori(1, B - 2) as b:
                batch(b, False, False)
            batch(B - 2, False, False)
            batch(B - 1, False, True)
            sp.wait_ge(pv_done, 32 * B)
            sp.dma_start(w1_all, w1.rearrange("e d h -> d e h")).then_inc(w1_loaded, 16)
            sp.dma_start(w2_all, w2.rearrange("e (c p) d -> p e c d", p=P)).then_inc(w2_loaded, 16)
            store_x1(B - 1)
            sp.wait_ge(tab_steps, TAB_STEPS)
            for n in range(2):
                sp.dma_start(table_dram[n].rearrange("(p c) -> p c", p=P), blk_i[:, n, :]).then_inc(tab_out, 16)
            sp.wait_ge(tab_out, 32)
            sp.dma_start(table[:, :, :], table_dram.rearrange("(o n) b -> o n b", o=1)).then_inc(tab_in, 16)
            sp.wait_ge(tab_in, 16)
            sp.wait_ge(scattered, 256 * B)
            sp.wait_ge(pads_written, 16 * (E + 1))
            sp.wait_ge(pj_psum, 2 * B)

            def load_block(r, s):
                i = XR * r + s
                row = sp.value_load(table[0:1, 1, i:i + 1] if isinstance(i, int) else table[0:1, 1, bass.ds(i, 1)],
                                    min_val=0, max_val=E * REG)
                wait_apart(sp, sp_passed, y_scaled, i - XR + 1)
                wait_apart(sp, sp_passed, dest_copied, i - XR + 1)
                sp.dma_start(blk_in[:, s, :], sorted_rows[bass.ds(row, P), :]).then_inc(blk_loaded[s], 16)

            for s in range(XR):
                load_block(0, s)
            with sp.Fori(1, BLOCKS // XR) as r:
                for s in range(XR):
                    load_block(r, s)
            for s in range(WR):
                sp.wait_ge(y_stored[s], 16 * (BLOCKS // WR))

            def load_y(r, s):
                b = 2 * r + s
                wait_apart(sp, sp_passed, yt_psum, 2 * (b - 1))
                for k in range(2):
                    sp.dma_start(y_in[:, s, k], expert_out[bass.ds(k * B * T + b * T, T), :].rearrange(
                        "(j p) d -> p j d", p=P)).then_inc(y_loaded[s], 16)

            def store_out(r, s):
                b = 2 * r + s
                wait_apart(sp, sp_passed, out_ready, 2 * (b + 1))
                sp.dma_start(out_v[bass.ds(b, 1)].rearrange("a c t -> (a c) t"), o_buf[:, s, :]).then_inc(
                    out_stored[s], 16)

            load_y(0, 0)
            load_y(0, 1)
            with sp.Fori(0, B // 2 - 1) as r:
                for s in range(2):
                    load_y(r + 1, s)
                    store_out(r, s)
            for s in range(2):
                store_out(B // 2 - 1, s)
            for s in range(2):
                sp.wait_ge(out_stored[s], 16 * (B // 2))

        @block.gpsimd
        def _(gp):
            n = 0

            def step(inst):
                nonlocal n
                n += 1
                inst.then_inc(setup, 1)

            def eye(t, view, pattern, cm, base_, op, fill):
                gp.wait_ge(setup, n)
                step(nc.gpsimd.affine_select(out=view, in_=view, compare_op=op, fill=fill, base=base_,
                                             pattern=pattern, channel_multiplier=cm))

            step(nc.gpsimd.memset(ident[:, :], 0.0))
            eye(ident, ident[:, :], [[-1, P]], 1, 0, ALU.not_equal, 1.0)
            step(nc.gpsimd.memset(ident_b[:, :], 0.0))
            eye(ident_b, ident_b[:, :], [[-1, P]], 1, 0, ALU.not_equal, 1.0)
            step(nc.gpsimd.memset(ones_b[:, :], 1.0))
            step(nc.gpsimd.memset(tri_b[:, :], 1.0))
            eye(tri_b, tri_b[:, :], [[1, P]], -1, 0, ALU.is_gt, 0.0)
            step(nc.gpsimd.memset(mean_m[:, :], 1.0 / C))
            step(nc.gpsimd.memset(wp_sb[:, :, :], 0.0))
            step(nc.gpsimd.memset(v_pad[:, :, :, :], 1.0))
            step(nc.gpsimd.memset(o_n[:, :, :], 0.0))
            step(nc.gpsimd.memset(rows[:, :, :, C + 2:ROWW], 0.0))
            step(nc.gpsimd.memset(neg_half[:, :], -0.5))
            step(nc.gpsimd.memset(ones_e[:, :], 1.0))
            step(nc.gpsimd.memset(pad_row[:, :], 0.0))
            gp.wait_ge(setup, n)
            step(nc.gpsimd.memset(pad_row[:, C:C + 1].bitcast(I32), SKIP))
            for g in range(G):
                gp.wait_ge(setup, n)
                step(nc.gpsimd.memset(ks[STACK:STACK + MROWS, g, :, :], 0.0))
                for part in range(MPARTS):
                    eye(ks, ks[STACK:STACK + MROWS, g, :, :], [[-1, HG], [0, T]], 1, -HG * part, ALU.not_equal, 1.0)
            at_i = 0
            gp.wait_ge(setup, n)
            for pattern, start, cm, num in (
                ([[0, TB], [-1, E]], E, 0, TB * E), ([[REG, E]], 0, 0, E),
                ([[P, TB], [B * T, 2]], 0, 1, TB * 2), ([[0, 1]], 0, 1, 1), ([[1, 3]], 0, 3, 3),
            ):
                step(nc.gpsimd.iota(iota_i[:, at_i:at_i + num], pattern=pattern, base=start, channel_multiplier=cm))
                at_i += num
            assert n == SETUP, n

            def ln_factors(b, which, eps, stats_done, done):
                wait_apart(gp, gp_passed, stats_done, 16 * (b + 1))
                nc.gpsimd.tensor_scalar(ln_var[:, which, :], mean_var[:, which, :, 1], 1.0, eps,
                                        ALU.mult, ALU.add).then_inc(done, 1)
                nc.gpsimd.tensor_scalar(neg_mean[:, which, :], mean_var[:, which, :, 0], -1.0, 0.0,
                                        ALU.mult, ALU.add).then_inc(done, 1)
                wait_apart(gp, gp_passed, done, 3 * b + 2)
                nc.gpsimd.tensor_tensor(out=rstd[:, which, :], in0=ln_var[:, which, :], in1=neg_half[:, :],
                                        op=ALU.pow).then_inc(done, 1)
                wait_apart(gp, gp_passed, done, 3 * b + 3)

            def normalise_x(b):
                ln_factors(b, 0, LN1_EPS, ln1_stats, ln1_scale)
                for j in range(TB):
                    nc.gpsimd.tensor_scalar(xt[:, j, :], xt[:, j, :], neg_mean[:, 0, j:j + 1], rstd[:, 0, j:j + 1],
                                            ALU.add, ALU.mult).then_inc(xt_normed, 1)

            def split_qk(b, i):
                o, half = i // 2, i % 2
                cols = slice(half * HALF, (half + 1) * HALF)
                f = qk_f[:, i % 2, :]
                if i == 0:
                    wait_apart(gp, gp_passed, stacked[1], 192 * b)
                    wait_apart(gp, gp_passed, stacked[0], 192 * b)
                done = 20 * b + 5 * i
                wait_apart(gp, gp_passed, qk_copied, 4 * b + i + 1)
                nc.gpsimd.tensor_scalar(parts[:, o, 0, cols], f, 1.0, 0.0, ALU.mult, ALU.add).then_inc(qk_parts, 1)
                for level in (1, 2):
                    wait_apart(gp, gp_passed, qk_parts, done + 2 * level - 1)
                    nc.gpsimd.tensor_tensor(out=f, in0=f, in1=parts[:, o, level - 1, cols],
                                            op=ALU.subtract).then_inc(qk_parts, 1)
                    wait_apart(gp, gp_passed, qk_parts, done + 2 * level)
                    nc.gpsimd.tensor_scalar(parts[:, o, level, cols], f, 1.0, 0.0,
                                            ALU.mult, ALU.add).then_inc(qk_parts, 1)

            def place_v(b, g):
                wait_apart(gp, gp_passed, v_copied, 2 * (b + 1))
                wait_apart(gp, gp_passed, pv_done, 32 * b - 32 + 16 * (g + 1))
                nc.gpsimd.tensor_scalar(v_pad[:, :, HG * g:HG * g + HG, 0:D], v_st[:, :, HG * g:HG * g + HG, :],
                                        1.0, 0.0, ALU.mult, ALU.add).then_inc(v_placed, 1)

            def split_m(b, s):
                k = STAGES * b + s
                neg = m_neg[:, s % 2, :].rearrange("p (t h) -> p t h", t=HG)
                rest = m_rest[:, :].rearrange("p (t h) -> p t h", t=HG)
                wait_apart(gp, gp_passed, m_ready, k + 1)
                wait_apart(gp, gp_passed, m_psum, k)
                nc.gpsimd.tensor_scalar(m_parts[:, :, 0, :], neg, 1.0, 0.0, ALU.mult, ALU.add).then_inc(m_split, 1)
                wait_apart(gp, gp_passed, m_split, 3 * k + 1)
                nc.gpsimd.tensor_tensor(out=rest, in0=neg, in1=m_parts[:, :, 0, :],
                                        op=ALU.subtract).then_inc(m_split, 1)
                wait_apart(gp, gp_passed, m_split, 3 * k + 2)
                nc.gpsimd.tensor_scalar(m_parts[:, :, 1, :], rest, 1.0, 0.0, ALU.mult, ALU.add).then_inc(m_split, 1)

            def add_bias(b):
                wait_apart(gp, gp_passed, res_loaded, 16 * (b + 1))
                r3 = res[:, :].rearrange("p (j c) -> p j c", j=TB)
                nc.gpsimd.tensor_tensor(out=r3, in0=r3, in1=bias[:, :].unsqueeze(1).to_broadcast([P, TB, C]),
                                        op=ALU.add).then_inc(res_ready, 1)

            def normalise_tokens(b):
                ln_factors(b, 1, LN2_EPS, ln2_stats, ln2_scale)
                wait_apart(gp, gp_passed, scattered, 256 * b)
                for j in range(TB):
                    nc.gpsimd.tensor_scalar(rows[:, 0, j, 0:C], tok[:, j, :], neg_mean[:, 1, j:j + 1],
                                            rstd[:, 1, j:j + 1], ALU.add, ALU.mult).then_inc(rows_normed, 1)

            def scatter(b, k):
                wait_apart(gp, gp_passed, routed, b + 1)
                wait_apart(gp, gp_passed, rows_copied, b + 1)
                for j in range(TB):
                    nc.gpsimd.indirect_dma_start(
                        out=sorted_rows[:, :], out_offset=bass.IndirectOffsetOnAxis(ap=place[:, k, j:j + 1], axis=0),
                        in_=rows[:, k, j, :], in_offset=None).then_inc(scattered, 16)

            gp.wait_ge(weights_in, WEIGHTS)
            normalise_x(0)
            for i in range(4):
                split_qk(0, i)
            place_v(0, 0)
            split_m(0, 0)

            def batch(b, first, last):
                place_v(b, 1)
                if not first:
                    add_bias(b - 1)
                if not last:
                    normalise_x(b + 1)
                split_m(b, 1)
                if not last:
                    split_qk(b + 1, 0)
                if not first:
                    normalise_tokens(b - 1)
                if not last:
                    split_qk(b + 1, 1)
                    split_qk(b + 1, 2)
                split_m(b, 2)
                if not last:
                    split_qk(b + 1, 3)
                    place_v(b + 1, 0)
                split_m(b, 3)
                if not first:
                    scatter(b - 1, 0)
                if not last:
                    split_m(b, 4)
                if not first:
                    scatter(b - 1, 1)

            batch(0, True, False)
            with gp.Fori(1, B - 1) as b:
                batch(b, False, False)
            batch(B - 1, False, True)
            add_bias(B - 1)
            normalise_tokens(B - 1)
            scatter(B - 1, 0)
            scatter(B - 1, 1)
            gp.wait_ge(pads_ready, 1)
            gp.dma_start(sorted_rows[E * REG:E * REG + P, :], pad_row[:, :]).then_inc(pads_written, 16)
            for e in range(E):
                nc.gpsimd.indirect_dma_start(
                    out=sorted_rows[:, :], out_offset=bass.IndirectOffsetOnAxis(ap=pad_place[:, e:e + 1], axis=0),
                    in_=pad_row[:, :], in_offset=None).then_inc(pads_written, 16)

            def scatter_y(r, s):
                wait_apart(gp, gp_passed, y_scaled, XR * r + s + 1)
                wait_apart(gp, gp_passed, dest_copied, XR * r + s + 1)
                nc.gpsimd.indirect_dma_start(
                    out=expert_out[:, :], out_offset=bass.IndirectOffsetOnAxis(ap=blk_dest[:, s % WR:s % WR + 1], axis=0),
                    in_=blk_y[:, s % WR, :], in_offset=None, bounds_check=2 * B * T - 1,
                    oob_is_err=False).then_inc(y_stored[s % WR], 16)

            with gp.Fori(0, BLOCKS // XR) as r:
                for s in range(XR):
                    scatter_y(r, s)

        @block.scalar
        def _(act):
            def exp_unit(b, u):
                wait(act, scores_ready, SLOTS * b + u + 1)
                if u % 4 == 0:
                    wait(act, pv_done, 32 * b + (u - PRING) // 4 + 1)
                nc.scalar.activation(probs[:, u % PRING, :], ps_score[:, u % RING, :], ACT.Exp,
                                     scale=SCALE).then_inc(exp_done, 1)

            def copy_xt(b, half):
                wait(act, xt_psum, 2 * b + half + 1)
                wait(act, v_psum, 2 * b)
                nc.scalar.activation(xt[:, 4 * half:4 * half + 4, :],
                                     misc[:, :].rearrange("p (j c) -> p j c", j=4), ACT.Copy).then_inc(xt_copied, 1)

            def copy_qk(b, i):
                wait(act, qk_psum, 4 * b + i + 1)
                wait(act, qk_parts, 20 * b + 5 * (i - 1))
                nc.scalar.activation(qk_f[:, i % 2, :], misc[:, :], ACT.Copy).then_inc(qk_copied, 1)

            def copy_v(b, half):
                wait(act, v_psum, 2 * b + half + 1)
                wait(act, v_placed, 2 * b)
                nc.scalar.activation(v_st[:, 4 * half:4 * half + 4, :, :].rearrange("p j h d -> p j (h d)"),
                                     misc[:, :].rearrange("p (j n) -> p j n", j=4), ACT.Copy).then_inc(v_copied, 1)

            def copy_m(b, s):
                k = STAGES * b + s
                wait(act, m_psum, k + 1)
                wait(act, m_loaded, 16 * k)
                nc.scalar.activation(m_row[STACK:STACK + MROWS, :], misc[STACK:STACK + MROWS, :],
                                     ACT.Copy).then_inc(m_copied, 1)

            def copy_tokens(b, half):
                wait(act, tt_psum, 2 * b + half + 1)
                wait(act, rows_normed, TB * b)
                nc.scalar.activation(tok[:, 4 * half:4 * half + 4, :],
                                     misc[:, :].rearrange("p (j c) -> p j c", j=4), ACT.Copy).then_inc(tok_copied, 1)

            def gate_exponentials(b):
                wait(act, gate_shifted, b + 1)
                nc.scalar.activation(tmp[:, :, :], gat[:, :, :], ACT.Exp).then_inc(gate_exp, 1)

            def copy_rows(b):
                wait(act, rows_normed, TB * (b + 1))
                wait(act, scattered, 256 * b)
                nc.scalar.activation(rows[:, 1, :, 0:C], rows[:, 0, :, 0:C], ACT.Copy).then_inc(rows_copied, 1)

            copy_xt(0, 0)
            copy_xt(0, 1)
            for i in range(4):
                copy_qk(0, i)
            copy_v(0, 0)
            copy_v(0, 1)
            copy_m(0, 0)

            def batch(b, first, last):
                for u in range(SLOTS):
                    exp_unit(b, u)
                    if not last:
                        if u == 2:
                            copy_xt(b + 1, 0)
                        if u == 6:
                            copy_xt(b + 1, 1)
                        if u == 21:
                            copy_qk(b + 1, 0)
                        if u == 38:
                            copy_qk(b + 1, 1)
                        if u == 42:
                            copy_qk(b + 1, 2)
                        if u == 46:
                            copy_qk(b + 1, 3)
                        if u == 50:
                            copy_v(b + 1, 0)
                        if u == 54:
                            copy_v(b + 1, 1)
                    if not first:
                        if u == 30:
                            copy_tokens(b - 1, 0)
                        if u == 34:
                            copy_tokens(b - 1, 1)
                        if u == 64:
                            copy_rows(b - 1)
                        if u == 72:
                            gate_exponentials(b - 1)
                    if u % UNITS == 24 and not (last and u > 96):
                        copy_m(b, u // UNITS + 1)

            batch(0, True, False)
            with act.Fori(1, B - 1) as b:
                batch(b, False, False)
            batch(B - 1, False, True)
            copy_tokens(B - 1, 0)
            copy_tokens(B - 1, 1)
            copy_rows(B - 1)
            gate_exponentials(B - 1)

            def copy_block(r, s):
                i = XR * r + s
                wait(act, blk_tr, i + 1)
                wait(act, hid_psum, i - 1)
                nc.scalar.activation(blk_xt[:, s % 2, :], ps_xt[:, s % 2, 0:P], ACT.Copy).then_inc(blk_tr_copied, 1)

            def block_relu(r, s):
                i = XR * r + s
                wait(act, hid_psum, i + 1)
                wait(act, y_psum, i - 1)
                nc.scalar.activation(hid[:, s % 2, :], ps_h[:, s % 2, :], ACT.Relu).then_inc(hid_done, 1)

            copy_block(0, 0)
            for s in range(XR):
                copy_block(0, s + 1)
                block_relu(0, s)
            with act.Fori(1, BLOCKS // XR - 1) as r:
                for s in range(XR):
                    copy_block(r, s + 1)
                    block_relu(r, s)
            for s in range(XR):
                if s < XR - 1:
                    copy_block(BLOCKS // XR - 1, s + 1)
                block_relu(BLOCKS // XR - 1, s)

        @block.vector
        def _(dve):
            dve.wait_ge(setup, SETUP)
            at_i = 0
            for dst, num in ((e_rev[:, :, :].rearrange("p j e -> p (j e)"), TB * E), (reg_base[:, :], E),
                             (dest_f[:, :, :].rearrange("p j k -> p (j k)"), TB * 2), (part_no[:, :], 1),
                             (blk_no[:, :], 3)):
                nc.vector.tensor_copy(dst, iota_i[:, at_i:at_i + num]).then_inc(setup_v, 1)
                at_i += num
            nc.vector.tensor_copy(base[:, :], iota_i[:, TB * E:TB * E + E]).then_inc(setup_v, 1)
            dve.wait_ge(weights_in, WEIGHTS)
            for o in range(2):
                nc.vector.tensor_copy(wq_r[:, o, :].rearrange("c (g d h) -> c g d h", g=G, d=D),
                                      wq_in[:, o].rearrange("c (g h) d -> c g d h", g=G)).then_inc(setup_v, 1)
            dve.wait_ge(wg_mean, 1)
            nc.vector.tensor_tensor(out=wg_c[:, :], in0=misc[:, 0:E], in1=wg_sb[:, :],
                                    op=ALU.subtract).then_inc(setup_v, 1)
            dve.wait_ge(setup_v, 9)
            nc.vector.tensor_scalar(wg_c[:, :], wg_c[:, :], -1.0, None, ALU.mult).then_inc(setup_v, 1)

            def take_max(b, m):
                s, u = m // UNITS, m % UNITS
                wait(dve, max_ready, SLOTS * b + m + 1)
                nc.vector.tensor_reduce(out=m_red[:, s % 2, u:u + 1], in_=ps_max[:, m % SLOTS % RING, :], axis=AX.X,
                                        op=ALU.max).then_inc(max_taken, 1)

            def row_maxima(b, s):
                k = STAGES * b + s
                wait(dve, max_taken, UNITS * (k + 1))
                wait(dve, m_split, 3 * (k - 1))
                nc.vector.tensor_reduce(out=m_neg[:, s % 2, :],
                                        in_=m_red[:, s % 2, :].rearrange("p (n s) -> p n s", s=2),
                                        axis=AX.X, op=ALU.max, negate=True).then_inc(m_ready, 1)

            def divide(b, s, step):
                k = STAGES * b + s
                g, half = s % STAGES // 2, s % 2
                wait(dve, norm_steps, 4 * k + step)
                if step == 0:
                    wait(dve, pv_done, 8 * (k + 1))
                    nc.vector.transpose(o_t[:, :, :].rearrange("p n d -> p (n d)"), ps_pv[:, :]).then_inc(norm_steps, 1)
                if step == 1:
                    nc.vector.reciprocal(o_rec[:, :], o_t[:, :, D]).then_inc(norm_steps, 1)
                if step == 2:
                    nc.vector.tensor_tensor(out=o_n[:, :, 0:D], in0=o_t[:, :, 0:D],
                                            in1=o_rec[:, :].unsqueeze(2).to_broadcast([P, HALF // 32, D]),
                                            op=ALU.mult).then_inc(norm_steps, 1)
                if step == 3:
                    wait(dve, pj_psum, 2 * b if s >= 0 else 2 * (b - 1))
                    nc.vector.transpose(att[:, g, half * HALF:(half + 1) * HALF],
                                        o_n[:, :, :].rearrange("p n d -> p (n d)")).then_inc(norm_steps, 1)

            def norm_stats(b, which, copied, done, half):
                src = xt if which == 0 else tok
                wait(dve, copied, 2 * b + half + 1)
                for j in range(4 * half, 4 * half + 4):
                    nc.vector.bn_stats(stats[:, which, j, :], src[:, j, :]).then_inc(done, 1)
                if half:
                    wait_apart(dve, dve_passed, done, 16 * b + TB)
                    for j in range(TB):
                        nc.vector.bn_aggr(mean_var[:, which, j, :], stats[:, which, j:j + 1, :]).then_inc(done, 1)

            def add_residual(b, half):
                cols = slice(half * HALF, (half + 1) * HALF)
                wait(dve, pj_psum, 2 * b + half + 1)
                wait(dve, res_ready, b + 1)
                nc.vector.tensor_tensor(out=x1[:, cols], in0=misc[:, :], in1=res[:, cols],
                                        op=ALU.add).then_inc(x1_ready, 1)

            def wide(t, n=E):
                return t.unsqueeze(2).to_broadcast([P, TB, n])

            def choose(b):
                count = [0]

                def step(inst):
                    inst.then_inc(route_a, 1)
                    count[0] += 1

                def after():
                    wait(dve, route_a, ROUTE_A * b + count[0])

                m1, m2, m2s = (masks[:, :, i, :] for i in range(3))
                wait(dve, lg_psum, b + 1)
                wait(dve, ln2_scale, 3 * (b + 1))
                nc.vector.tensor_tensor(out=gat[:, :, :], in0=misc[:, 0:TB * E].rearrange("p (j e) -> p j e", j=TB),
                                        in1=wide(rstd[:, 1, :]), op=ALU.mult).then_inc(lg_taken, 1)
                wait(dve, lg_taken, b + 1)
                step(nc.vector.tensor_reduce(out=small[:, 0, :], in_=gat[:, :, :], axis=AX.X, op=ALU.max))
                after()
                nc.vector.tensor_tensor(out=gat[:, :, :], in0=gat[:, :, :], in1=wide(small[:, 0, :]),
                                        op=ALU.subtract).then_inc(gate_shifted, 1)

            def choose_experts(b):
                count = [1]

                def step(inst):
                    inst.then_inc(route_a, 1)
                    count[0] += 1

                def after():
                    wait(dve, route_a, ROUTE_A * b + count[0])

                m1, m2, m2s = (masks[:, :, i, :] for i in range(3))
                wait(dve, gate_exp, b + 1)
                step(nc.vector.tensor_reduce(out=small[:, 1, :], in_=tmp[:, :, :], axis=AX.X, op=ALU.add))
                yield
                after()
                step(nc.vector.reciprocal(small[:, 2, :], small[:, 1, :]))
                yield
                after()
                step(nc.vector.tensor_tensor(out=gat[:, :, :], in0=tmp[:, :, :], in1=wide(small[:, 2, :]), op=ALU.mult))
                yield
                after()
                for i, mask in ((0, m1), (1, m2)):
                    step(nc.vector.tensor_reduce(out=small[:, 3 + i, :], in_=gat[:, :, :], axis=AX.X, op=ALU.max))
                    yield
                    after()
                    step(nc.vector.tensor_tensor(out=tmp[:, :, :], in0=gat[:, :, :], in1=wide(small[:, 3 + i, :]),
                                                 op=ALU.is_ge))
                    yield
                    after()
                    step(nc.vector.tensor_tensor(out=tmp[:, :, :], in0=tmp[:, :, :], in1=e_rev[:, :, :], op=ALU.mult))
                    yield
                    after()
                    step(nc.vector.tensor_reduce(out=small[:, 5, :], in_=tmp[:, :, :], axis=AX.X, op=ALU.max))
                    yield
                    after()
                    step(nc.vector.tensor_tensor(out=mask, in0=tmp[:, :, :], in1=wide(small[:, 5, :]),
                                                 op=ALU.is_equal))
                    yield
                    after()
                    if i == 0:
                        step(nc.vector.tensor_scalar(tmp[:, :, :], mask, -1.0, 1.0, ALU.mult, ALU.add))
                        yield
                        after()
                        step(nc.vector.tensor_tensor(out=gat[:, :, :], in0=gat[:, :, :], in1=tmp[:, :, :],
                                                     op=ALU.mult))
                        yield
                        after()
                step(nc.vector.tensor_copy(m2s, m2))
                yield
                after()
                step(nc.vector.tensor_tensor(out=small[:, 6, :], in0=m1[:, :, 0], in1=m2[:, :, 0], op=ALU.mult))
                yield
                after()
                step(nc.vector.tensor_tensor(out=m2s[:, :, 0], in0=m2[:, :, 0], in1=small[:, 6, :], op=ALU.subtract))
                yield
                after()
                step(nc.vector.tensor_tensor(out=m2s[:, :, 1], in0=m2[:, :, 1], in1=small[:, 6, :], op=ALU.add))
                yield
                after()
                nc.vector.tensor_copy(masks_b[:, :, :], masks[:, :, :, :].rearrange(
                    "p j m e -> p j (m e)")).then_inc(masks_ready, 1)
                step(nc.vector.tensor_tensor(out=small[:, 7, :], in0=small[:, 3, :], in1=small[:, 4, :], op=ALU.add))
                yield
                after()
                step(nc.vector.tensor_scalar(small[:, 7, :], small[:, 7, :], GATE_EPS, None, ALU.add))
                yield
                after()
                step(nc.vector.reciprocal(small[:, 7, :], small[:, 7, :]))
                yield
                after()
                assert count[0] == ROUTE_A, count

            def place_rows(b):
                count = [0]

                def step(inst):
                    inst.then_inc(route_b, 1)
                    count[0] += 1

                def after():
                    wait(dve, route_b, ROUTE_B * b + count[0])

                def over(t):
                    return t.unsqueeze(1).to_broadcast([P, TB, E])

                m1, m2, m2s = (masks[:, :, i, :] for i in range(3))
                wait(dve, cs_psum, b + 1)
                nc.vector.tensor_copy(counts[:, :], misc[:, 0:TB * 3 * E + 3 * E]).then_inc(cs_taken, 1)
                wait(dve, cs_taken, b + 1)
                step(nc.vector.tensor_tensor(out=tmp[:, :, :], in0=before[:, :, 0, :], in1=m1, op=ALU.mult))
                yield
                after()
                step(nc.vector.tensor_reduce(out=small[:, 8, :], in_=tmp[:, :, :], axis=AX.X, op=ALU.add))
                yield
                after()
                step(nc.vector.tensor_scalar(kept_n[:, :], totals[:, 0, :], float(CAP), None, ALU.min))
                yield
                after()
                step(nc.vector.tensor_tensor(out=tmp2[:, :, :], in0=before[:, :, 1, :], in1=over(kept_n[:, :]),
                                             op=ALU.add))
                yield
                after()
                step(nc.vector.tensor_tensor(out=tmp2[:, :, :], in0=tmp2[:, :, :], in1=m2, op=ALU.mult))
                yield
                after()
                step(nc.vector.tensor_reduce(out=small[:, 9, :], in_=tmp2[:, :, :], axis=AX.X, op=ALU.add))
                yield
                after()
                wait(dve, scattered, 256 * b)
                for k in range(2):
                    step(nc.vector.tensor_scalar(small[:, 8 + k, :], small[:, 8 + k, :], float(CAP), None, ALU.is_lt))
                    yield
                    after()
                    step(nc.vector.tensor_tensor(out=small[:, 10 + k, :], in0=small[:, 3 + k, :], in1=small[:, 7, :],
                                                 op=ALU.mult))
                    yield
                    after()
                    nc.vector.tensor_tensor(out=rows[:, k, :, C + 1], in0=small[:, 10 + k, :],
                                            in1=small[:, 8 + k, :], op=ALU.mult).then_inc(routed_parts, 1)
                    nc.vector.tensor_copy(rows_i[:, k, :, C], dest_f[:, :, k]).then_inc(routed_parts, 1)
                step(nc.vector.tensor_tensor(out=base2[:, :], in0=base[:, :], in1=totals[:, 0, :], op=ALU.add))
                yield
                after()
                for k, mask, start in ((0, m1, base), (1, m2s, base2)):
                    step(nc.vector.tensor_tensor(out=tmp[:, :, :], in0=before[:, :, 2 * k, :], in1=over(start[:, :]),
                                                 op=ALU.add))
                    yield
                    after()
                    step(nc.vector.tensor_tensor(out=tmp[:, :, :], in0=tmp[:, :, :], in1=mask, op=ALU.mult))
                    yield
                    after()
                    step(nc.vector.tensor_reduce(out=small[:, 8 + k, :], in_=tmp[:, :, :], axis=AX.X, op=ALU.add))
                    yield
                    after()
                step(nc.vector.tensor_tensor(out=base[:, :], in0=base2[:, :], in1=totals[:, 2, :], op=ALU.add))
                yield
                after()
                wait(dve, routed_parts, 4 * (b + 1))
                nc.vector.tensor_scalar(dest_f[:, :, :], dest_f[:, :, :], float(T), None,
                                        ALU.add).then_inc(dest_next, 1)
                nc.vector.tensor_copy(place[:, :, :], small[:, 8:10, :]).then_inc(routed, 1)
                wait(dve, dest_next, b + 1)
                assert count[0] == ROUTE_B, count

            for half in range(2):
                norm_stats(0, 0, xt_copied, ln1_stats, half)
            for m in range(LEAD):
                take_max(0, m)
                if m == UNITS:
                    row_maxima(0, 0)

            def batch(b, first, last):
                for u in range(SLOTS):
                    m = u + LEAD
                    if not (last and m >= SLOTS):
                        take_max(b, m)
                    if m % UNITS == 0 and not (last and m > SLOTS):
                        row_maxima(b, m // UNITS - 1)
                    if 4 <= u % UNITS < 8 and not (first and u < UNITS):
                        divide(b, u // UNITS - 1, u % UNITS - 4)
                    if not last:
                        if u == 3:
                            norm_stats(b + 1, 0, xt_copied, ln1_stats, 0)
                        if u == 8:
                            norm_stats(b + 1, 0, xt_copied, ln1_stats, 1)
                    if not first:
                        if u == 13:
                            add_residual(b - 1, 0)
                        if u == 17:
                            add_residual(b - 1, 1)
                        if u == 31:
                            norm_stats(b - 1, 1, tok_copied, ln2_stats, 0)
                        if u == 35:
                            norm_stats(b - 1, 1, tok_copied, ln2_stats, 1)
                        if u == 66:
                            choose(b - 1)
                        if u == 74:
                            routing = choose_experts(b - 1)
                        if u == 98:
                            routing = place_rows(b - 1)
                        if u >= 74:
                            next(routing, None)

            batch(0, True, False)
            with dve.Fori(1, B - 1) as b:
                batch(b, False, False)
            batch(B - 1, False, True)
            for step in range(4):
                divide(B, -1, step)
            add_residual(B - 1, 0)
            add_residual(B - 1, 1)
            norm_stats(B - 1, 1, tok_copied, ln2_stats, 0)
            norm_stats(B - 1, 1, tok_copied, ln2_stats, 1)
            choose(B - 1)
            for _ in choose_experts(B - 1):
                pass
            for _ in place_rows(B - 1):
                pass
            nc.vector.tensor_scalar(pad_place[:, :], base[:, :], part_no[:, 0:1], None, ALU.add).then_inc(pads_ready, 1)

            tabs = 0

            def tab(inst):
                nonlocal tabs
                tabs += 1
                inst.then_inc(tab_steps, 1)
                dve.wait_ge(tab_steps, tabs)

            rows_n, blocks_n, ends = (blk_f[:, i, 0:E] for i in range(3))
            le = blk_f[:, 3, :].rearrange("p (c e) -> p c e", c=3)
            lb = blk_f[:, 4, :].rearrange("p (c e) -> p c e", c=3)
            e_of, before_of, row_of = (blk_f[:, 5, 3 * i:3 * i + 3] for i in range(3))

            def three(t):
                return t.unsqueeze(1).to_broadcast([P, 3, E])

            tab(nc.vector.tensor_tensor(out=rows_n, in0=base[:, :], in1=reg_base[:, :], op=ALU.subtract))
            tab(nc.vector.tensor_scalar(blk_n[:, :], rows_n, float(P - 1), None, ALU.add))
            tab(nc.vector.tensor_single_scalar(blk_n[:, :], blk_n[:, :], 7, op=ALU.logical_shift_right))
            tab(nc.vector.tensor_copy(blocks_n, blk_n[:, :]))
            tab(nc.vector.tensor_tensor_scan(out=ends, data0=ones_e[:, :], data1=blocks_n, initial=0.0,
                                             op0=ALU.mult, op1=ALU.add))
            tab(nc.vector.tensor_tensor(out=le, in0=three(ends), in1=blk_no[:, :].unsqueeze(2).to_broadcast([P, 3, E]),
                                        op=ALU.is_le))
            tab(nc.vector.tensor_reduce(out=e_of, in_=le, axis=AX.X, op=ALU.add))
            tab(nc.vector.tensor_tensor(out=lb, in0=le, in1=three(blocks_n), op=ALU.mult))
            tab(nc.vector.tensor_reduce(out=before_of, in_=lb, axis=AX.X, op=ALU.add))
            tab(nc.vector.tensor_tensor(out=row_of, in0=blk_no[:, :], in1=before_of, op=ALU.subtract))
            tab(nc.vector.tensor_scalar(row_of, row_of, float(P), None, ALU.mult))
            tab(nc.vector.tensor_scalar(before_of, e_of, float(REG), None, ALU.mult))
            tab(nc.vector.tensor_tensor(out=row_of, in0=row_of, in1=before_of, op=ALU.add))
            tab(nc.vector.tensor_scalar(blk_i[:, 1, :], row_of, float(E * REG), None, ALU.min))
            tab(nc.vector.tensor_scalar(blk_i[:, 0, :], e_of, float(E - 1), None, ALU.min))
            assert tabs == TAB_STEPS, tabs

            dve.wait_ge(tab_in, 16)
            dve.wait_ge(w1_loaded, 16)
            dve.wait_ge(w2_loaded, 16)
            dve.wait_ge(pj_psum, 2 * B)

            e_regs = [dve.alloc_register(f"expert{s}") for s in range(XR)]

            def experts_of(i):
                dve.reg_load(e_regs, table[0:1, 0, i:i + XR] if isinstance(i, int) else table[0:1, 0, bass.ds(i, XR)])
                return [dve.snap(reg, min_val=0, max_val=E - 1) for reg in e_regs]

            def copy_weights(i, s, e):
                wait(dve, hid_psum, i - WR + 1)
                nc.vector.tensor_copy(w1_blk[:, s % WR, :], w1_all[:, bass.ds(e, 1), :].rearrange(
                    "p a h -> p (a h)")).then_inc(w1_copied, 1)
                wait(dve, y_psum, i - WR + 1)
                nc.vector.tensor_copy(w2_blk[:, s % WR, :], w2_all[:, bass.ds(e, 1), :, :].rearrange(
                    "p a c d -> p (a c d)")).then_inc(w2_copied, 1)

            def scale_y(r, s):
                i = XR * r + s
                wait(dve, y_stored[s % WR], 16 * (XR // WR * r + s // WR))
                wait(dve, blk_loaded[s], 16 * (r + 1))
                nc.vector.tensor_copy(blk_dest[:, s % WR:s % WR + 1], blk_in[:, s, C:C + 1].bitcast(I32)).then_inc(dest_copied, 1)
                wait(dve, y_psum, i + 1)
                nc.vector.tensor_scalar(blk_y[:, s % WR, :], ps_o[:, s % 2, 0:P], blk_in[:, s, C + 1:C + 2], None,
                                        ALU.mult).then_inc(y_scaled, 1)

            def blocks(r, count):
                experts = experts_of(XR * r + WLEAD)
                for s in range(XR):
                    if s < count:
                        copy_weights(XR * r + s + WLEAD, s + WLEAD, experts[s])
                    scale_y(r, s)

            experts = experts_of(0)
            for s in range(WLEAD):
                copy_weights(s, s, experts[s])
            blocks(0, XR)
            with dve.Fori(1, BLOCKS // XR - 1) as r:
                blocks(r, XR)
            blocks(BLOCKS // XR - 1, XR - WLEAD)

            def sum_y(r, s):
                b = 2 * r + s
                wait(dve, y_loaded[s], 32 * (r + 1))
                nc.vector.tensor_tensor(out=y_in[:, s, 0], in0=y_in[:, s, 0], in1=y_in[:, s, 1],
                                        op=ALU.add).then_inc(y_summed, 1)

            def add_x1(r, s):
                b = 2 * r + s
                wait(dve, out_stored[s], 16 * r)
                for half in range(2):
                    cols = slice(half * HALF, (half + 1) * HALF)
                    wait(dve, yt_psum, 2 * b + half + 1)
                    res_b = (x1_all[:, b, cols] if isinstance(b, int) else x1_all[:, bass.ds(b, 1), cols].rearrange(
                        "p a t -> p (a t)"))
                    nc.vector.tensor_tensor(out=o_buf[:, s, cols], in0=ps_y[:, s, half, :], in1=res_b,
                                            op=ALU.add).then_inc(out_ready, 1)

            dve.wait_ge(x1_stored, 16 * B)
            def image_pair(r):
                sum_y(r, 1)
                add_x1(r, 0)
                sum_y(r + 1, 0)
                add_x1(r, 1)

            sum_y(0, 0)
            image_pair(0)
            with dve.Fori(1, B // 2 - 1) as r:
                image_pair(r)
            r = B // 2 - 1
            sum_y(r, 1)
            add_x1(r, 0)
            add_x1(r, 1)

        @block.tensor
        def _(pe):
            freed = [None]

            def misc_free(sem_, value):
                if freed[0] is not None:
                    pe.wait_ge(*freed[0])
                freed[0] = (sem_, value)

            def transpose_x(b, half):
                misc_free(xt_copied, 2 * b + half + 1)
                wait(pe, x_loaded, 16 * (b + 1))
                for j in range(4):
                    last = nc.tensor.transpose(misc[:, j * P:(j + 1) * P],
                                               x_in[:, (4 * half + j) * P:(4 * half + j + 1) * P], ident[:, :])
                last.then_inc(xt_psum, 1)

            def project_qk(b, i):
                o, half = i // 2, i % 2
                misc_free(qk_copied, 4 * b + i + 1)
                wait(pe, xt_normed, TB * (b + 1))
                nc.tensor.matmul(misc[:, :], wq_r[:, o, :], xt[:, 4 * half:4 * half + 4, :], start=True,
                                 stop=True).then_inc(qk_psum, 1)

            def project_v(b, half):
                misc_free(v_copied, 2 * b + half + 1)
                for j in range(4):
                    last = nc.tensor.matmul(misc[:, j * P:(j + 1) * P], xt[:, 4 * half + j, :], wv_sb[:, :, :],
                                            start=True, stop=True)
                last.then_inc(v_psum, 1)

            def max_unit(b, m):
                s, u = m // UNITS, m % UNITS
                bb = b + s // STAGES
                g, half = s % STAGES // 2, s % 2
                h, t, kh = u // 8, u // 2 % 4, u % 2
                if u == 0 and half == 0:
                    wait(pe, stacked[g], 192 * (bb + 1))
                wait(pe, max_taken, SLOTS * b + ring_free(m))
                nc.tensor.matmul(ps_max[:, m % SLOTS % RING, :], qs[0:STACK, g, h, half * HALF + t * P:half * HALF + (t + 1) * P],
                                 ks[0:STACK, g, h, kh * HALF:(kh + 1) * HALF], start=True,
                                 stop=True).then_inc(max_ready, 1)

            def rows_of_maxima(b, s):
                k = STAGES * b + s
                misc_free(m_copied, k + 1)
                wait(pe, m_split, 3 * (k + 1))
                for t in range(4):
                    last = nc.tensor.matmul(misc[STACK:STACK + MROWS, t * P:(t + 1) * P],
                                            m_parts[:, t, :, :].rearrange("p a h -> p (a h)"), ident_b[:, :],
                                            start=True, stop=True)
                last.then_inc(m_psum, 1)

            def score_unit(b, u):
                s = u // UNITS
                g, half = s // 2, s % 2
                i, h = u % UNITS // HG, u % HG
                if u % UNITS == 0:
                    wait(pe, m_loaded, 16 * (STAGES * b + s + 1))
                wait(pe, exp_done, SLOTS * b + ring_free(u))
                nc.tensor.matmul(ps_score[:, u % RING, :], ks[0:STACK + MROWS, g, h, i * P:(i + 1) * P],
                                 qs[0:STACK + MROWS, g, h, half * HALF:(half + 1) * HALF], start=True,
                                 stop=True).then_inc(scores_ready, 1)

            def weigh(b, n, part):
                s, i = n // 8, n % 8
                g = s % STAGES // 2
                bb = b + s // STAGES
                if part == 0:
                    if i == 0:
                        wait(pe, norm_steps, 4 * (STAGES * b + s - 1) + 1)
                        wait(pe, v_placed, 2 * bb + g + 1)
                    wait(pe, exp_done, SLOTS * b + 4 * n + 4)
                cols = slice(part * HALF // 2, (part + 1) * HALF // 2)
                for h in range(HG):
                    last = nc.tensor.matmul(ps_pv[32 * h:32 * h + 32, cols], v_pad[:, i, HG * g + h, :],
                                            probs[:, (4 * n + h) % PRING, cols], start=(i == 0 and part == 0),
                                            stop=(i == TB - 1), skip_group_check=True)
                if part:
                    last.then_inc(pv_done, 1)

            def project_out(b, half):
                misc_free(x1_ready, 2 * b + half + 1)
                wait(pe, norm_steps, 16 * (b + 1))
                for j in range(4):
                    for g in range(G):
                        last = nc.tensor.matmul(misc[:, j * P:(j + 1) * P],
                                                att[:, g, (4 * half + j) * P:(4 * half + j + 1) * P],
                                                wp_sb[:, g, :], start=(g == 0), stop=(g == G - 1))
                last.then_inc(pj_psum, 1)

            def transpose_tokens(b, half):
                misc_free(tok_copied, 2 * b + half + 1)
                wait(pe, x1_ready, 2 * b + half + 1)
                for j in range(4):
                    last = nc.tensor.transpose(misc[:, j * P:(j + 1) * P],
                                               x1[:, (4 * half + j) * P:(4 * half + j + 1) * P], ident[:, :])
                last.then_inc(tt_psum, 1)

            def logits(b):
                misc_free(lg_taken, b + 1)
                for j in range(TB):
                    last = nc.tensor.matmul(misc[:, j * E:(j + 1) * E], x1[:, j * P:(j + 1) * P], wg_c[:, :],
                                            start=True, stop=True)
                last.then_inc(lg_psum, 1)

            def count_tokens(b):
                w = 3 * E
                misc_free(cs_taken, b + 1)
                wait(pe, masks_ready, b + 1)
                nc.tensor.matmul(misc[:, 0:TB * w], tri_b[:, :], masks_b[:, :, :], start=True, stop=False)
                for d in range(1, TB):
                    nc.tensor.matmul(misc[:, d * w:TB * w], ones_b[:, :], masks_b[:, 0:TB - d, :], start=False,
                                     stop=(d == TB - 1))
                for j in range(TB):
                    last = nc.tensor.matmul(misc[:, TB * w:(TB + 1) * w], ones_b[:, :], masks_b[:, j, :],
                                            start=(j == 0), stop=(j == TB - 1))
                last.then_inc(cs_psum, 1)

            pe.wait_ge(setup, SETUP)
            pe.wait_ge(weights_in, WEIGHTS)
            nc.tensor.matmul(misc[:, 0:E], mean_m[:, :], wg_sb[:, :], start=True, stop=True).then_inc(wg_mean, 1)
            pe.wait_ge(setup_v, 10)
            transpose_x(0, 0)
            transpose_x(0, 1)
            for i in range(4):
                project_qk(0, i)
            project_v(0, 0)
            project_v(0, 1)
            for m in range(LEAD):
                max_unit(0, m)
                if m == 37:
                    rows_of_maxima(0, 0)

            def batch(b, first, last):
                freed[0] = (m_copied, STAGES * b + 1)
                for u in range(SLOTS):
                    if u % 2 == 0:
                        if not (last and u + LEAD >= SLOTS):
                            max_unit(b, u + LEAD)
                        score_unit(b, u)
                    else:
                        score_unit(b, u)
                        if not (last and u + LEAD >= SLOTS):
                            max_unit(b, u + LEAD)
                        if not (first and u < 4):
                            weigh(b, u // 4 - 1, u % 4 // 2)
                    if not last:
                        if u == 1:
                            transpose_x(b + 1, 0)
                        if u == 5:
                            transpose_x(b + 1, 1)
                        if u == 21:
                            project_qk(b + 1, 0)
                        if u == 37:
                            project_qk(b + 1, 1)
                        if u == 41:
                            project_qk(b + 1, 2)
                        if u == 45:
                            project_qk(b + 1, 3)
                        if u == 49:
                            project_v(b + 1, 0)
                        if u == 53:
                            project_v(b + 1, 1)
                    if not first:
                        if u == 13:
                            project_out(b - 1, 0)
                        if u == 17:
                            project_out(b - 1, 1)
                        if u == 29:
                            transpose_tokens(b - 1, 0)
                        if u == 33:
                            transpose_tokens(b - 1, 1)
                        if u == 65:
                            logits(b - 1)
                        if u == 97:
                            count_tokens(b - 1)
                    if u % UNITS == 23 and not (last and u > 96):
                        rows_of_maxima(b, u // UNITS + 1)

            batch(0, True, False)
            nc.disable_value_cache = True
            with pe.Fori(1, B - 1) as b:
                batch(b, False, False)
            nc.disable_value_cache = False
            batch(B - 1, False, True)
            weigh(B, -1, 0)
            weigh(B, -1, 1)
            project_out(B - 1, 0)
            project_out(B - 1, 1)
            transpose_tokens(B - 1, 0)
            transpose_tokens(B - 1, 1)
            logits(B - 1)
            count_tokens(B - 1)

            def transpose_block(r, s):
                i = XR * r + s
                wait(pe, blk_loaded[s % XR], 16 * (r + s // XR + 1))
                wait(pe, blk_tr_copied, i - 1)
                nc.tensor.transpose(ps_xt[:, s % 2, 0:P], blk_in[:, s % XR, 0:C], ident[:, :]).then_inc(blk_tr, 1)

            def hidden(r, s):
                i = XR * r + s
                wait(pe, blk_tr_copied, i + 1)
                wait(pe, w1_copied, i + 1)
                wait(pe, hid_done, i - 1)
                for c in range(HC):
                    last = nc.tensor.matmul(ps_h[:, s % 2, c * P:(c + 1) * P], w1_blk[:, s % WR, c * P:(c + 1) * P],
                                            blk_xt[:, s % 2, :], start=True, stop=True)
                last.then_inc(hid_psum, 1)

            def outputs(i, s):
                wait(pe, hid_done, i + 1)
                wait(pe, w2_copied, i + 1)
                wait(pe, y_scaled, i - 1)
                for c in range(HC):
                    last = nc.tensor.matmul(ps_o[:, s % 2, 0:P], hid[:, s % 2, c * P:(c + 1) * P],
                                            w2_blk[:, s % WR, c * P:(c + 1) * P], start=(c == 0), stop=(c == HC - 1))
                last.then_inc(y_psum, 1)

            def block_steps(r, s, first, last):
                if not last:
                    transpose_block(r, s + 1)
                hidden(r, s)
                if not first:
                    outputs(XR * r + s - 1, s - 1)

            pe.wait_ge(cs_taken, B)
            transpose_block(0, 0)
            for s in range(XR):
                block_steps(0, s, s == 0, False)
            with pe.Fori(1, BLOCKS // XR - 1) as r:
                for s in range(XR):
                    block_steps(r, s, False, False)
            for s in range(XR):
                block_steps(BLOCKS // XR - 1, s, False, s == XR - 1)
            outputs(BLOCKS - 1, XR - 1)

            def transpose_y(r, s):
                b = 2 * r + s
                wait(pe, y_summed, b + 1)
                wait(pe, out_ready, 2 * (b - 1))
                for j in range(TB):
                    last = nc.tensor.transpose(ps_y[:, s, j // 4, j % 4 * P:(j % 4 + 1) * P], y_in[:, s, 0, j, :],
                                               ident[:, :])
                    if j % 4 == 3:
                        last.then_inc(yt_psum, 1)

            pe.wait_ge(hid_done, BLOCKS)
            for s in range(2):
                transpose_y(0, s)
            with pe.Fori(1, B // 2) as r:
                for s in range(2):
                    transpose_y(r, s)


_INS = ['x', 'L0_conv_Wq', 'L0_conv_Wk', 'L0_conv_Wv', 'L0_conv_Wproj', 'L0_conv_bproj', 'L0_ffn_w_gating',
        'L0_ffn_w1', 'L0_ffn_w2']
_OUTS = [((16, 128, 32, 32), 'float32')]


def kernel(**inputs):
    import numpy as _np
    import concourse.bacc as _bacc
    from concourse import mybir as _mybir
    from concourse.bass_utils import run_bass_kernel_spmd as _run

    nc = _bacc.Bacc("TRN2", target_bir_lowering=False, num_devices=1)
    arrays, args = {}, []
    for name in _INS:
        a = _np.ascontiguousarray(inputs[name])
        arrays[f"in_{name}_dram"] = a
        args.append(nc.dram_tensor(f"in_{name}_dram", a.shape, _mybir.dt.from_np(a.dtype), kind="ExternalInput").ap())
    for i, (shape, dtype) in enumerate(_OUTS):
        dt = _mybir.dt.from_np(_np.dtype(dtype))
        args.append(nc.dram_tensor(f"out_{i}_dram", shape, dt, kind="ExternalOutput").ap())
    metaformer(nc, *args)
    r = _run(nc, [arrays], core_ids=[0])
    got = tuple(r.results[0][f"out_{i}_dram"] for i in range(len(_OUTS)))
    return got[0]
```

```python
from contextlib import ExitStack

import concourse.bass as bass
from concourse import mybir

FP32 = mybir.dt.float32
BF16 = mybir.dt.bfloat16
I32 = mybir.dt.int32
ALU = mybir.AluOpType
ACT = mybir.ActivationFunctionType
AX = mybir.AxisListType

P = 128
B, C, T = 16, 128, 1024
H, D = 8, 16
HG = 4
G = H // HG
TB = T // P
HALF = T // 2
SCALE = 1.0 / float(D) ** 0.5
LN1_EPS, LN2_EPS = 1e-6, 1e-5

STAGES = G * 2
UNITS = TB * HG
SLOTS = STAGES * UNITS
LEAD = 46
MSLOT = 26
RING = 3
PRING = 16
NORMS = 14
BUSY = (3, 4, 5, 6, 7, 18, 19, 20, 21)
WEIGH_AT = [(0, None)] * UNITS
for _n in range(-1, UNITS // 4 - 1):
    for _part in range(2):
        WEIGH_AT[(4 * _n + 5 if _n else 7) + (1 if _n == 0 else 2) * _part] = (_n, _part)

Q_PART = (0, 0, 1, 1, 0, 2)
K_PART = (0, 1, 0, 1, 2, 0)
STACK = 16 * len(Q_PART)
MPARTS = 2
MROWS = MPARTS * HG

E = 16
HID = 512
HC = HID // P
CAP = T * 2 * 2 // E
GATE_EPS = 1e-9
REG = B * T + P
ROWW = C + 4
SKIP = 1 << 20
BLOCKS = 2 * B * T // P + E
XR = 8
WR = 4
WLEAD = 2
TAB_STEPS = 15
ROUTE_A, ROUTE_B = 23, 30


def wait(eng, sem, value):
    if isinstance(value, int) and value <= 0:
        return
    eng.wait_ge(sem, value)


def wait_apart(eng, passed, sem, value):
    wait(eng, sem, value)
    if not isinstance(value, int):
        eng.sem_inc(passed, 1)


def ring_free(n):
    return n - RING + 1 if n % SLOTS >= SLOTS % RING else n - SLOTS % RING + 1


def norms_before(b, s):
    return NORMS * b + (-4, 0, 3, 6, 10)[s + 1]


def metaformer(nc, x, wq, wk, wv, wproj, bproj, wgate, w1, w2, out):
    ctx = ExitStack()
    with ctx:
        def sb(name, shape, dt=FP32):
            return ctx.enter_context(nc.sbuf_tensor("sb_" + name, shape, dt))

        def sem(name):
            return ctx.enter_context(nc.semaphore(name))

        x_v = x.rearrange("b c h w -> b c (h w)")
        out_v = out.rearrange("b c h w -> b c (h w)")
        sorted_rows = nc.dram_tensor("sorted_rows", (E * REG + P, ROWW), FP32, kind="Internal").ap()
        expert_out = nc.dram_tensor("expert_out", (2 * B * T, C), FP32, kind="Internal").ap()
        table_dram = nc.dram_tensor("table_dram", (2, 3 * P), I32, kind="Internal").ap()

        arena_a = sb("arena_a", [P, PRING * HALF])
        probs = arena_a[:, :].rearrange("p (u t) -> p u t", u=PRING)
        w1_all = arena_a[:, :].rearrange("p (e h) -> p e h", e=E)
        y_in = arena_a[:, 0:4 * T].rearrange("p (s k j d) -> p s k j d", s=2, k=2, j=TB)
        o_buf = arena_a[:, 4 * T:6 * T].rearrange("p (s t) -> p s t", s=2)
        arena_b = sb("arena_b", [P, 2 * G * HG * T], BF16)
        stacks = arena_b[:, :].rearrange("p (o g h t) -> p o g h t", o=2, g=G, h=HG)
        qs, ks = stacks[:, 0], stacks[:, 1]
        w2_all = arena_b[:, :].bitcast(FP32).rearrange("p (e c d) -> p e c d", e=E, c=HC)
        arena_c = sb("arena_c", [P, 3 * T + 2 * T])
        parts = arena_c[:, 0:3 * T].bitcast(BF16).rearrange("p (o l t) -> p o l t", o=2, l=3)
        att = arena_c[:, 3 * T:4 * T]
        o_n = arena_c[:, 4 * T:5 * T].rearrange("p (s n d) -> p s n d", s=2, n=HALF // 32)
        at = 0

        def cut(n):
            nonlocal at
            at += n
            return arena_c[:, at - n:at]
        w1_blk = cut(WR * HID).rearrange("p (s h) -> p s h", s=WR)
        w2_blk = cut(WR * HID).rearrange("p (s h) -> p s h", s=WR)
        hid = cut(2 * HID).rearrange("p (s h) -> p s h", s=2)

        x1_all = sb("x1_all", [P, B, T])
        x_in = sb("x_in", [P, T])
        xt = sb("xt", [P, TB, P])
        res = sb("res", [P, T])
        x1 = res
        tok = sb("tok", [P, TB, P])
        rows = sb("rows", [P, 2, TB, ROWW])
        rows_i = rows[:, :, :, :].rearrange("p k j w -> p (k j w)").bitcast(I32).rearrange(
            "p (k j w) -> p k j w", k=2, j=TB)
        qk_f = sb("qk_f", [P, 2, HALF])
        v_st = sb("v_st", [P, TB, H, D])
        arena_d = sb("arena_d", [P, TB * H * 32])
        v_pad = arena_d[:, :].rearrange("p (j h d) -> p j h d", j=TB, h=H)
        blk_in = arena_d[:, 0:XR * ROWW].rearrange("p (s w) -> p s w", s=XR)
        blk_y = arena_d[:, XR * ROWW:XR * ROWW + WR * P].rearrange("p (s d) -> p s d", s=WR)
        blk_xt = arena_d[:, XR * ROWW + WR * P:XR * ROWW + (WR + 2) * P].rearrange("p (s d) -> p s d", s=2)
        blk_dest = arena_d[:, XR * ROWW + (WR + 2) * P:XR * ROWW + (WR + 2) * P + WR].bitcast(I32)
        o_t = sb("o_t", [P, HALF // 32, 32])
        o_rec = sb("o_rec", [P, HALF // 32])
        m_red = sb("m_red", [P, 2, UNITS])
        m_neg = sb("m_neg", [P, 2, HG * HG])
        m_rest = sb("m_rest", [P, HG * HG])
        m_parts = sb("m_parts", [P, HG, MPARTS, HG], BF16)
        m_row = sb("m_row", [P, HALF], BF16)
        stats = sb("stats", [P, 2, TB, 6])
        mean_var = sb("mean_var", [P, 2, TB, 2])
        ln_var = sb("ln_var", [P, 2, TB])
        rstd = sb("rstd", [P, 2, TB])
        neg_mean = sb("neg_mean", [P, 2, TB])
        gat = sb("gat", [P, TB, E])
        tmp = sb("tmp", [P, TB, E])
        tmp2 = sb("tmp2", [P, TB, E])
        folds = sb("folds", [P, TB, E // 2])
        masks = sb("masks", [P, TB, 3, E])
        masks_b = sb("masks_b", [P, TB, 3 * E], BF16)
        counts = sb("counts", [P, TB * 3 * E + 3 * E])
        before = counts[:, 0:TB * 3 * E].rearrange("p (j m e) -> p j m e", j=TB, m=3)
        totals = counts[:, TB * 3 * E:].rearrange("p (m e) -> p m e", m=3)
        small = sb("small", [P, 12, TB])
        kept_n = sb("kept_n", [P, E])
        base2 = sb("base2", [P, E])
        base = sb("base", [P, E])
        dest_f = sb("dest_f", [P, TB, 2])
        place = sb("place", [P, 2, TB], I32)
        pad_row = sb("pad_row", [P, ROWW])
        pad_place = sb("pad_place", [P, E], I32)
        blk_f = sb("blk_f", [P, 6, 3 * E])
        blk_n = sb("blk_n", [P, E], I32)
        blk_i = sb("blk_i", [P, 2, 3], I32)
        table = x_in[0:1, 0:6 * P].bitcast(I32).rearrange("o (n b) -> o n b", n=2)
        ident = sb("ident", [P, P])
        ident_b = sb("ident_b", [P, P], BF16)
        ones_b = sb("ones_b", [P, P], BF16)
        tri_b = sb("tri_b", [P, P], BF16)
        mean_m = tok[:, 0, :]
        neg_half = sb("neg_half", [P, TB])
        e_rev = sb("e_rev", [P, TB, E])
        reg_base = sb("reg_base", [P, E])
        part_no = sb("part_no", [P, 1])
        blk_no = sb("blk_no", [P, 3])
        ones_e = sb("ones_e", [P, E])
        iota_i = tok[:, 1:3, :].rearrange("p j c -> p (j c)").bitcast(I32)
        wq_in = o_t[:, 0:8, :].rearrange("p n d -> p (n d)").rearrange("p (o h d) -> p o h d", o=2, h=H)
        wq_r = sb("wq_r", [P, 2, P])
        wv_sb = sb("wv_sb", [P, H, D])
        wp_sb = sb("wp_sb", [P, C])
        bias = sb("bias", [P, C])
        wg_sb = sb("wg_sb", [P, E])
        wg_c = sb("wg_c", [P, E])

        banks = ctx.enter_context(nc.psum_tensor("banks", [P, 8, HALF], FP32))
        ps_score, ps_max = banks[:, 0:RING], banks[:, RING:2 * RING]
        ps_pv, misc = banks[:, 6], banks[:, 7]
        ps_h, ps_o, ps_xt = banks[:, 0:2], banks[:, 2:4], banks[:, 6:8]
        ps_y = banks[:, 0:4].rearrange("p (s h) t -> p s h t", s=2)

        setup = sem("setup")
        key_rows = sem("key_rows")
        setup_v = sem("setup_v")
        weights_in = sem("weights_in")
        wg_mean = sem("wg_mean")
        x_loaded = sem("x_loaded")
        res_loaded = sem("res_loaded")
        xt_psum = sem("xt_psum")
        xt_copied = sem("xt_copied")
        ln1_stats = sem("ln1_stats")
        ln1_scale = sem("ln1_scale")
        xt_normed = sem("xt_normed")
        qk_psum = sem("qk_psum")
        qk_copied = sem("qk_copied")
        qk_parts = sem("qk_parts")
        stacked = [sem(f"stacked{g}") for g in range(G)]
        v_psum = sem("v_psum")
        v_copied = sem("v_copied")
        v_placed = sem("v_placed")
        max_ready = sem("max_ready")
        max_taken = sem("max_taken")
        m_ready = sem("m_ready")
        m_split = sem("m_split")
        m_psum = sem("m_psum")
        m_copied = sem("m_copied")
        m_loaded = sem("m_loaded")
        scores_ready = sem("scores_ready")
        exp_done = sem("exp_done")
        pv_done = sem("pv_done")
        norm_steps = sem("norm_steps")
        pj_psum = sem("pj_psum")
        res_ready = sem("res_ready")
        x1_ready = sem("x1_ready")
        x1_stored = sem("x1_stored")
        tt_psum = sem("tt_psum")
        tok_copied = sem("tok_copied")
        ln2_stats = sem("ln2_stats")
        ln2_scale = sem("ln2_scale")
        rows_normed = sem("rows_normed")
        rows_copied = sem("rows_copied")
        lg_psum = sem("lg_psum")
        lg_taken = sem("lg_taken")
        gate_shifted = sem("gate_shifted")
        gate_exp = sem("gate_exp")
        route_a = sem("route_a")
        masks_ready = sem("masks_ready")
        cs_psum = sem("cs_psum")
        cs_taken = sem("cs_taken")
        route_b = sem("route_b")
        routed_parts = sem("routed_parts")
        dest_next = sem("dest_next")
        routed = sem("routed")
        scattered = sem("scattered")
        pads_ready = sem("pads_ready")
        pads_written = sem("pads_written")
        tab_steps = sem("tab_steps")
        tab_out = sem("tab_out")
        tab_in = sem("tab_in")
        w1_loaded = sem("w1_loaded")
        w2_loaded = sem("w2_loaded")
        blk_loaded = [sem(f"blk_loaded{s}") for s in range(XR)]
        blk_tr = sem("blk_tr")
        blk_tr_copied = sem("blk_tr_copied")
        w1_copied = sem("w1_copied")
        w2_copied = sem("w2_copied")
        hid_psum = sem("hid_psum")
        hid_done = sem("hid_done")
        y_psum = sem("y_psum")
        dest_copied = sem("dest_copied")
        y_scaled = sem("y_scaled")
        y_stored = [sem(f"y_stored{s}") for s in range(WR)]
        y_loaded = [sem(f"y_loaded{s}") for s in range(2)]
        y_summed = sem("y_summed")
        yt_psum = sem("yt_psum")
        out_ready = sem("out_ready")
        out_stored = [sem(f"out_stored{s}") for s in range(2)]

        gp_passed = sem("gp_passed")
        sp_passed = sem("sp_passed")
        dve_passed = sem("dve_passed")

        SETUP = 19
        SETUP_IDENT = 2
        KEY_ROWS = G * (1 + MPARTS)
        WEIGHTS = (2 + 1 + H + 1 + 1) * 16

        block = ctx.enter_context(nc.Block())

        @block.sync
        def _(sp):
            def load_x(b):
                wait_apart(sp, sp_passed, xt_psum, 2 * b)
                sp.dma_start(x_in[:, :], x_v[b] if isinstance(b, int) else x_v[bass.ds(b, 1)].rearrange(
                    "a c t -> (a c) t")).then_inc(x_loaded, 16)

            def load_res(b):
                wait_apart(sp, sp_passed, x1_stored, 16 * b)
                wait_apart(sp, sp_passed, lg_psum, b)
                wait_apart(sp, sp_passed, tt_psum, 2 * b)
                sp.dma_start(res[:, :], x_v[b] if isinstance(b, int) else x_v[bass.ds(b, 1)].rearrange(
                    "a c t -> (a c) t")).then_inc(res_loaded, 16)

            def stack(b, g):
                wait_apart(sp, sp_passed, scores_ready, SLOTS * (b - 1) + 2 * UNITS * (g + 1))
                for o, part in ((0, Q_PART), (1, K_PART)):
                    wait_apart(sp, sp_passed, qk_parts, 20 * b + 10 * (o + 1))
                    for r, level in enumerate(part):
                        sp.dma_start(stacks[16 * r:16 * r + 16, o, g, :, :],
                                     parts[64 * g:64 * g + 64, o, level, :]).then_inc(stacked[g], 16)

            def load_m(b, s):
                g, half = s % STAGES // 2, s % 2
                wait_apart(sp, sp_passed, m_copied, STAGES * b + s + 1)
                sp.dma_start(qs[STACK:STACK + MROWS, g, :, half * HALF:(half + 1) * HALF],
                             m_row[STACK:STACK + MROWS, :].unsqueeze(1).to_broadcast([MROWS, HG, HALF])).then_inc(
                    m_loaded, 16)

            def store_x1(b):
                wait_apart(sp, sp_passed, x1_ready, 2 * (b + 1))
                dst = x1_all[:, b, :] if isinstance(b, int) else x1_all[:, bass.ds(b, 1), :].rearrange(
                    "p a t -> p (a t)")
                sp.dma_start(dst, x1[:, :]).then_inc(x1_stored, 16)

            sp.dma_start(x_in[:, :], x_v[0]).then_inc(x_loaded, 16)
            for o, w in ((0, wq), (1, wk)):
                sp.dma_start(wq_in[:, o], w.rearrange("h c d -> c h d")).then_inc(weights_in, 16)
            sp.dma_start(wv_sb[:, :, :], wv.rearrange("h c d -> c h d")).then_inc(weights_in, 16)
            sp.dma_start(bias[:, :], bproj.rearrange("(a c) -> a c", a=1).to_broadcast([P, C])).then_inc(weights_in, 16)
            sp.dma_start(wg_sb[:, :], wgate).then_inc(weights_in, 16)
            for h in range(H):
                q = 32 * (h % HG) + D * (h // HG)
                sp.dma_start(wp_sb[q:q + D, :], wproj[h * D:(h + 1) * D, :]).then_inc(weights_in, 16)
            stack(0, 0)
            load_x(1)
            load_m(0, 0)

            def batch(b, first, last):
                stack(b, 1)
                if not first:
                    store_x1(b - 1)
                load_m(b, 1)
                if not last:
                    wait_apart(sp, sp_passed, xt_psum, 2 * (b + 2))
                    if not (isinstance(b, int) and b + 2 >= B):
                        load_x(b + 2)
                load_m(b, 2)
                if not last:
                    stack(b + 1, 0)
                load_res(b)
                load_m(b, 3)
                if not last:
                    load_m(b, 4)

            batch(0, True, False)
            with sp.Fori(1, B - 2) as b:
                batch(b, False, False)
            batch(B - 2, False, False)
            batch(B - 1, False, True)
            sp.wait_ge(pv_done, 32 * B)
            sp.wait_ge(scattered, 256 * (B - 1))
            sp.dma_start(w1_all, w1.rearrange("e d h -> d e h")).then_inc(w1_loaded, 16)
            sp.dma_start(w2_all, w2.rearrange("e (c p) d -> p e c d", p=P)).then_inc(w2_loaded, 16)
            store_x1(B - 1)
            sp.wait_ge(setup, SETUP)
            sp.dma_start(sorted_rows[E * REG:E * REG + P, :], pad_row[:, :]).then_inc(pads_written, 16)
            pad_regs = [sp.alloc_register(f"pad{e}") for e in range(E // 2)]

            def pad_half(half):
                sp.reg_load(pad_regs, pad_place[0:1, half * E // 2:(half + 1) * E // 2])
                for reg in pad_regs:
                    row = sp.snap(reg, min_val=0, max_val=E * REG)
                    sp.dma_start(sorted_rows[bass.ds(row, P), :], pad_row[:, :]).then_inc(pads_written, 16)

            sp.wait_ge(pads_ready, 1)
            pad_half(0)
            sp.wait_ge(tab_steps, TAB_STEPS)
            for n in range(2):
                sp.dma_start(table_dram[n].rearrange("(p c) -> p c", p=P), blk_i[:, n, :]).then_inc(tab_out, 16)
            pad_half(1)
            sp.wait_ge(tab_out, 32)
            sp.dma_start(table[:, :, :], table_dram.rearrange("(o n) b -> o n b", o=1)).then_inc(tab_in, 16)
            sp.wait_ge(tab_in, 16)
            sp.wait_ge(scattered, 256 * B)
            sp.wait_ge(pads_written, 16 * (E + 1))
            sp.wait_ge(pj_psum, 2 * B)

            def load_block(r, s):
                i = XR * r + s
                row = sp.value_load(table[0:1, 1, i:i + 1] if isinstance(i, int) else table[0:1, 1, bass.ds(i, 1)],
                                    min_val=0, max_val=E * REG)
                wait_apart(sp, sp_passed, y_scaled, i - XR + 1)
                wait_apart(sp, sp_passed, dest_copied, i - XR + 1)
                sp.dma_start(blk_in[:, s, :], sorted_rows[bass.ds(row, P), :]).then_inc(blk_loaded[s], 16)

            for s in range(XR):
                load_block(0, s)
            with sp.Fori(1, BLOCKS // XR) as r:
                for s in range(XR):
                    load_block(r, s)
            for s in range(WR):
                sp.wait_ge(y_stored[s], 16 * (BLOCKS // WR))

            def load_y(r, s):
                b = 2 * r + s
                wait_apart(sp, sp_passed, yt_psum, 2 * (b - 1))
                for k in range(2):
                    sp.dma_start(y_in[:, s, k], expert_out[bass.ds(k * B * T + b * T, T), :].rearrange(
                        "(j p) d -> p j d", p=P)).then_inc(y_loaded[s], 16)

            def store_out(r, s):
                b = 2 * r + s
                wait_apart(sp, sp_passed, out_ready, 2 * (b + 1))
                sp.dma_start(out_v[bass.ds(b, 1)].rearrange("a c t -> (a c) t"), o_buf[:, s, :]).then_inc(
                    out_stored[s], 16)

            load_y(0, 0)
            load_y(0, 1)
            with sp.Fori(0, B // 2 - 1) as r:
                for s in range(2):
                    load_y(r + 1, s)
                    store_out(r, s)
            for s in range(2):
                store_out(B // 2 - 1, s)
            for s in range(2):
                sp.wait_ge(out_stored[s], 16 * (B // 2))

        @block.gpsimd
        def _(gp):
            n = 0

            def step(inst):
                nonlocal n
                n += 1
                inst.then_inc(setup, 1)

            def eye(view, pattern, cm, base_, op, fill):
                gp.wait_ge(setup, n)
                step(nc.gpsimd.affine_select(out=view, in_=view, compare_op=op, fill=fill, base=base_,
                                             pattern=pattern, channel_multiplier=cm))

            step(nc.gpsimd.memset(ident[:, :], 0.0))
            eye(ident[:, :], [[-1, P]], 1, 0, ALU.not_equal, 1.0)
            step(nc.gpsimd.memset(ident_b[:, :], 0.0))
            eye(ident_b[:, :], [[-1, P]], 1, 0, ALU.not_equal, 1.0)
            step(nc.gpsimd.memset(ones_b[:, :], 1.0))
            step(nc.gpsimd.memset(tri_b[:, :], 1.0))
            eye(tri_b[:, :], [[1, P]], -1, 0, ALU.is_gt, 0.0)
            step(nc.gpsimd.memset(mean_m[:, :], 1.0 / C))
            step(nc.gpsimd.memset(v_pad[:, :, :, :], 1.0))
            step(nc.gpsimd.memset(rows[:, :, :, C + 2:ROWW], 0.0))
            step(nc.gpsimd.memset(neg_half[:, :], -0.5))
            step(nc.gpsimd.memset(ones_e[:, :], 1.0))
            step(nc.gpsimd.memset(pad_row[:, :], 0.0))
            gp.wait_ge(setup, n)
            step(nc.gpsimd.memset(pad_row[:, C:C + 1].bitcast(I32), SKIP))
            at_i = 0
            gp.wait_ge(setup, n)
            for pattern, start, cm, num in (
                ([[0, TB], [-1, E]], E, 0, TB * E), ([[REG, E]], 0, 0, E),
                ([[P, TB], [B * T, 2]], 0, 1, TB * 2), ([[0, 1]], 0, 1, 1), ([[1, 3]], 0, 3, 3),
            ):
                step(nc.gpsimd.iota(iota_i[:, at_i:at_i + num], pattern=pattern, base=start, channel_multiplier=cm))
                at_i += num
            assert n == SETUP, n

            def ln_factors(b, which, eps, stats_done, done):
                wait_apart(gp, gp_passed, stats_done, 16 * (b + 1))
                nc.gpsimd.tensor_scalar(ln_var[:, which, :], mean_var[:, which, :, 1], 1.0, eps,
                                        ALU.mult, ALU.add).then_inc(done, 1)
                nc.gpsimd.tensor_scalar(neg_mean[:, which, :], mean_var[:, which, :, 0], -1.0, 0.0,
                                        ALU.mult, ALU.add).then_inc(done, 1)
                wait_apart(gp, gp_passed, done, 3 * b + 2)
                nc.gpsimd.tensor_tensor(out=rstd[:, which, :], in0=ln_var[:, which, :], in1=neg_half[:, :],
                                        op=ALU.pow).then_inc(done, 1)
                wait_apart(gp, gp_passed, done, 3 * b + 3)

            def normalise_x(b):
                ln_factors(b, 0, LN1_EPS, ln1_stats, ln1_scale)
                for j in range(TB):
                    nc.gpsimd.tensor_scalar(xt[:, j, :], xt[:, j, :], neg_mean[:, 0, j:j + 1], rstd[:, 0, j:j + 1],
                                            ALU.add, ALU.mult).then_inc(xt_normed, 1)

            def split_qk(b, i):
                o, half = i // 2, i % 2
                cols = slice(half * HALF, (half + 1) * HALF)
                f = qk_f[:, i % 2, :]
                if i == 0:
                    wait_apart(gp, gp_passed, stacked[1], 192 * b)
                    wait_apart(gp, gp_passed, stacked[0], 192 * b)
                done = 20 * b + 5 * i
                wait_apart(gp, gp_passed, qk_copied, 4 * b + i + 1)
                nc.gpsimd.tensor_scalar(parts[:, o, 0, cols], f, 1.0, 0.0, ALU.mult, ALU.add).then_inc(qk_parts, 1)
                for level in (1, 2):
                    wait_apart(gp, gp_passed, qk_parts, done + 2 * level - 1)
                    nc.gpsimd.tensor_tensor(out=f, in0=f, in1=parts[:, o, level - 1, cols],
                                            op=ALU.subtract).then_inc(qk_parts, 1)
                    wait_apart(gp, gp_passed, qk_parts, done + 2 * level)
                    nc.gpsimd.tensor_scalar(parts[:, o, level, cols], f, 1.0, 0.0,
                                            ALU.mult, ALU.add).then_inc(qk_parts, 1)

            def place_v(b, g):
                wait_apart(gp, gp_passed, v_copied, 2 * (b + 1))
                wait_apart(gp, gp_passed, pv_done, 32 * b - 32 + 16 * (g + 1))
                nc.gpsimd.tensor_scalar(v_pad[:, :, HG * g:HG * g + HG, 0:D], v_st[:, :, HG * g:HG * g + HG, :],
                                        1.0, 0.0, ALU.mult, ALU.add).then_inc(v_placed, 1)

            def add_bias(b):
                wait_apart(gp, gp_passed, res_loaded, 16 * (b + 1))
                r3 = res[:, :].rearrange("p (j c) -> p j c", j=TB)
                nc.gpsimd.tensor_tensor(out=r3, in0=r3, in1=bias[:, :].unsqueeze(1).to_broadcast([P, TB, C]),
                                        op=ALU.add).then_inc(res_ready, 1)

            def normalise_tokens(b):
                ln_factors(b, 1, LN2_EPS, ln2_stats, ln2_scale)
                wait_apart(gp, gp_passed, scattered, 256 * b)
                for j in range(TB):
                    nc.gpsimd.tensor_scalar(rows[:, 0, j, 0:C], tok[:, j, :], neg_mean[:, 1, j:j + 1],
                                            rstd[:, 1, j:j + 1], ALU.add, ALU.mult).then_inc(rows_normed, 1)

            def fold(out, tile, op, step, after):
                n, src = E // 2, tile
                while n:
                    dst = folds[:, :, 0:n] if n > 1 else out.unsqueeze(2)
                    step(nc.gpsimd.tensor_tensor(out=dst, in0=src[:, :, 0:n], in1=src[:, :, n:2 * n], op=op))
                    src = folds
                    if n > 1:
                        after()
                    n //= 2

            def place_rows(b):
                count = [0]

                def step(inst):
                    inst.then_inc(route_b, 1)
                    count[0] += 1

                def after():
                    wait_apart(gp, gp_passed, route_b, ROUTE_B * b + count[0])

                def over(t):
                    return t.unsqueeze(1).to_broadcast([P, TB, E])

                m1, m2, m2s = (masks[:, :, i, :] for i in range(3))
                wait_apart(gp, gp_passed, cs_taken, b + 1)
                wait_apart(gp, gp_passed, route_a, ROUTE_A * (b + 1))
                step(nc.gpsimd.tensor_tensor(out=tmp[:, :, :], in0=before[:, :, 0, :], in1=m1, op=ALU.mult))
                after()
                fold(small[:, 8, :], tmp, ALU.add, step, after)
                after()
                step(nc.gpsimd.tensor_scalar(kept_n[:, :], totals[:, 0, :], float(CAP), None, ALU.min))
                after()
                step(nc.gpsimd.tensor_tensor(out=tmp2[:, :, :], in0=before[:, :, 1, :], in1=over(kept_n[:, :]),
                                             op=ALU.add))
                after()
                step(nc.gpsimd.tensor_tensor(out=tmp2[:, :, :], in0=tmp2[:, :, :], in1=m2, op=ALU.mult))
                after()
                fold(small[:, 9, :], tmp2, ALU.add, step, after)
                after()
                wait_apart(gp, gp_passed, scattered, 256 * b)
                for k in range(2):
                    step(nc.gpsimd.tensor_scalar(small[:, 8 + k, :], small[:, 8 + k, :], float(CAP), None, ALU.is_lt))
                    after()
                    step(nc.gpsimd.tensor_tensor(out=small[:, 10 + k, :], in0=small[:, 3 + k, :], in1=small[:, 7, :],
                                                 op=ALU.mult))
                    after()
                    nc.gpsimd.tensor_tensor(out=rows[:, k, :, C + 1], in0=small[:, 10 + k, :],
                                            in1=small[:, 8 + k, :], op=ALU.mult).then_inc(routed_parts, 1)
                    nc.gpsimd.tensor_copy(rows_i[:, k, :, C], dest_f[:, :, k]).then_inc(routed_parts, 1)
                step(nc.gpsimd.tensor_tensor(out=base2[:, :], in0=base[:, :], in1=totals[:, 0, :], op=ALU.add))
                after()
                for k, mask, start in ((0, m1, base), (1, m2s, base2)):
                    step(nc.gpsimd.tensor_tensor(out=tmp[:, :, :], in0=before[:, :, 2 * k, :], in1=over(start[:, :]),
                                                 op=ALU.add))
                    after()
                    step(nc.gpsimd.tensor_tensor(out=tmp[:, :, :], in0=tmp[:, :, :], in1=mask, op=ALU.mult))
                    after()
                    fold(small[:, 8 + k, :], tmp, ALU.add, step, after)
                    after()
                step(nc.gpsimd.tensor_tensor(out=base[:, :], in0=base2[:, :], in1=totals[:, 2, :], op=ALU.add))
                after()
                wait_apart(gp, gp_passed, routed_parts, 4 * (b + 1))
                nc.gpsimd.tensor_scalar(dest_f[:, :, :], dest_f[:, :, :], float(T), None,
                                        ALU.add).then_inc(dest_next, 1)
                nc.gpsimd.tensor_copy(place[:, :, :], small[:, 8:10, :]).then_inc(routed, 1)
                wait_apart(gp, gp_passed, dest_next, b + 1)
                assert count[0] == ROUTE_B, count

            def scatter(b, k):
                wait_apart(gp, gp_passed, routed, b + 1)
                wait_apart(gp, gp_passed, rows_copied, 2 * (b + 1))
                for j in range(TB):
                    nc.gpsimd.indirect_dma_start(
                        out=sorted_rows[:, :], out_offset=bass.IndirectOffsetOnAxis(ap=place[:, k, j:j + 1], axis=0),
                        in_=rows[:, k, j, :], in_offset=None).then_inc(scattered, 16)

            gp.wait_ge(weights_in, WEIGHTS)
            normalise_x(0)
            rows_done = 0
            gp.wait_ge(xt_normed, TB)
            for g in range(G):
                indicator = ks[STACK:STACK + MROWS, g, :, :]
                if g:
                    gp.wait_ge(key_rows, rows_done)
                nc.gpsimd.memset(indicator, 0.0).then_inc(key_rows, 1)
                rows_done += 1
                for part in range(MPARTS):
                    gp.wait_ge(key_rows, rows_done)
                    nc.gpsimd.affine_select(out=indicator, in_=indicator, compare_op=ALU.not_equal, fill=1.0,
                                            base=-HG * part, pattern=[[-1, HG], [0, T]],
                                            channel_multiplier=1).then_inc(key_rows, 1)
                    rows_done += 1
            gp.wait_ge(key_rows, rows_done)
            place_v(0, 0)

            def batch(b, first, last):
                place_v(b, 1)
                if not last:
                    normalise_x(b + 1)
                if not last:
                    split_qk(b + 1, 0)
                if not first:
                    normalise_tokens(b - 1)
                if not last:
                    for i in range(1, 4):
                        split_qk(b + 1, i)
                    place_v(b + 1, 0)
                add_bias(b)
                if not first:
                    place_rows(b - 1)
                    scatter(b - 1, 0)
                    scatter(b - 1, 1)

            batch(0, True, False)
            with gp.Fori(1, B - 1) as b:
                batch(b, False, False)
            batch(B - 1, False, True)
            normalise_tokens(B - 1)
            place_rows(B - 1)
            scatter(B - 1, 0)
            scatter(B - 1, 1)

            def scatter_y(r, s):
                wait_apart(gp, gp_passed, y_scaled, XR * r + s + 1)
                wait_apart(gp, gp_passed, dest_copied, XR * r + s + 1)
                nc.gpsimd.indirect_dma_start(
                    out=expert_out[:, :], out_offset=bass.IndirectOffsetOnAxis(ap=blk_dest[:, s % WR:s % WR + 1], axis=0),
                    in_=blk_y[:, s % WR, :], in_offset=None, bounds_check=2 * B * T - 1,
                    oob_is_err=False).then_inc(y_stored[s % WR], 16)

            with gp.Fori(0, BLOCKS // XR) as r:
                for s in range(XR):
                    scatter_y(r, s)

        @block.scalar
        def _(act):
            def exp_unit(b, u):
                wait(act, scores_ready, SLOTS * b + u + 1)
                if u % 4 == 0:
                    wait(act, pv_done, 32 * b + (u - PRING) // 4 + 1)
                nc.scalar.activation(probs[:, u % PRING, :], ps_score[:, u % RING, :], ACT.Exp,
                                     scale=SCALE).then_inc(exp_done, 1)

            def copy_xt(b, half):
                wait(act, xt_psum, 2 * b + half + 1)
                wait(act, v_psum, 2 * b)
                nc.scalar.activation(xt[:, 4 * half:4 * half + 4, :],
                                     misc[:, :].rearrange("p (j c) -> p j c", j=4), ACT.Copy).then_inc(xt_copied, 1)

            def copy_qk(b, i):
                wait(act, qk_psum, 4 * b + i + 1)
                wait(act, qk_parts, 20 * b + 5 * (i - 1))
                nc.scalar.activation(qk_f[:, i % 2, :], misc[:, :], ACT.Copy).then_inc(qk_copied, 1)

            def copy_v(b, half):
                wait(act, v_psum, 2 * b + half + 1)
                wait(act, v_placed, 2 * b)
                nc.scalar.activation(v_st[:, 4 * half:4 * half + 4, :, :].rearrange("p j h d -> p j (h d)"),
                                     misc[:, :].rearrange("p (j n) -> p j n", j=4), ACT.Copy).then_inc(v_copied, 1)

            def copy_m(b, s):
                k = STAGES * b + s
                wait(act, m_psum, k + 1)
                wait(act, m_loaded, 16 * k)
                nc.scalar.activation(m_row[STACK:STACK + MROWS, :], misc[STACK:STACK + MROWS, :],
                                     ACT.Copy).then_inc(m_copied, 1)

            def copy_tokens(b, half):
                wait(act, tt_psum, 2 * b + half + 1)
                wait(act, rows_normed, TB * b)
                nc.scalar.activation(tok[:, 4 * half:4 * half + 4, :],
                                     misc[:, :].rearrange("p (j c) -> p j c", j=4), ACT.Copy).then_inc(tok_copied, 1)

            def gate_exponentials(b):
                wait(act, gate_shifted, b + 1)
                nc.scalar.activation(tmp[:, :, :], gat[:, :, :], ACT.Exp).then_inc(gate_exp, 1)

            def copy_rows(b, half):
                wait(act, rows_normed, TB * (b + 1))
                wait(act, scattered, 256 * b)
                js = slice(4 * half, 4 * half + 4)
                nc.scalar.activation(rows[:, 1, js, 0:C], rows[:, 0, js, 0:C], ACT.Copy).then_inc(rows_copied, 1)

            def copy_counts(b):
                wait(act, cs_psum, b + 1)
                wait(act, routed, b)
                nc.scalar.activation(counts[:, :], misc[:, 0:TB * 3 * E + 3 * E], ACT.Copy).then_inc(cs_taken, 1)

            copy_xt(0, 0)
            copy_xt(0, 1)
            for i in range(4):
                copy_qk(0, i)
            copy_v(0, 0)
            copy_v(0, 1)
            copy_m(0, 0)

            def batch(b, first, last):
                for u in range(SLOTS):
                    exp_unit(b, u)
                    if not last:
                        if u == 2:
                            copy_xt(b + 1, 0)
                        if u == 6:
                            copy_xt(b + 1, 1)
                        if u == 29:
                            copy_qk(b + 1, 0)
                        if u == 42:
                            copy_qk(b + 1, 1)
                        if u == 45:
                            copy_qk(b + 1, 2)
                        if u == 49:
                            copy_qk(b + 1, 3)
                        if u == 52:
                            copy_v(b + 1, 0)
                        if u == 55:
                            copy_v(b + 1, 1)
                    if not first:
                        if u == 23:
                            copy_tokens(b - 1, 0)
                        if u == 25:
                            copy_tokens(b - 1, 1)
                        if u == 41:
                            gate_exponentials(b - 1)
                        if u in (76, 80):
                            copy_rows(b - 1, (u - 76) // 4)
                        if u == 101:
                            copy_counts(b - 1)
                    if u % UNITS == MSLOT + 1 and not (last and u > 96):
                        copy_m(b, u // UNITS + 1)

            batch(0, True, False)
            with act.Fori(1, B - 1) as b:
                batch(b, False, False)
            batch(B - 1, False, True)
            copy_tokens(B - 1, 0)
            copy_tokens(B - 1, 1)
            gate_exponentials(B - 1)
            copy_rows(B - 1, 0)
            copy_rows(B - 1, 1)
            copy_counts(B - 1)

            def copy_block(r, s):
                i = XR * r + s
                wait(act, blk_tr, i + 1)
                wait(act, hid_psum, i - 1)
                nc.scalar.activation(blk_xt[:, s % 2, :], ps_xt[:, s % 2, 0:P], ACT.Copy).then_inc(blk_tr_copied, 1)

            def block_relu(r, s):
                i = XR * r + s
                wait(act, hid_psum, i + 1)
                wait(act, y_psum, i - 1)
                nc.scalar.activation(hid[:, s % 2, :], ps_h[:, s % 2, :], ACT.Relu).then_inc(hid_done, 1)

            copy_block(0, 0)
            for s in range(XR):
                copy_block(0, s + 1)
                block_relu(0, s)
            with act.Fori(1, BLOCKS // XR - 1) as r:
                for s in range(XR):
                    copy_block(r, s + 1)
                    block_relu(r, s)
            for s in range(XR):
                if s < XR - 1:
                    copy_block(BLOCKS // XR - 1, s + 1)
                block_relu(BLOCKS // XR - 1, s)

        @block.vector
        def _(dve):
            def take_max(b, m):
                s, u = m // UNITS, m % UNITS
                wait(dve, max_ready, SLOTS * b + m + 1)
                nc.vector.tensor_reduce(out=m_red[:, s % 2, u:u + 1], in_=ps_max[:, m % SLOTS % RING, :], axis=AX.X,
                                        op=ALU.max).then_inc(max_taken, 1)

            def row_maxima(b, s):
                k = STAGES * b + s
                wait(dve, max_taken, UNITS * (k + 1))
                wait(dve, m_split, 3 * (k - 1))
                nc.vector.tensor_reduce(out=m_neg[:, s % 2, :],
                                        in_=m_red[:, s % 2, :].rearrange("p (n s) -> p n s", s=2),
                                        axis=AX.X, op=ALU.max, negate=True).then_inc(m_ready, 1)

            def split_m(b, s, step):
                k = STAGES * b + s
                neg = m_neg[:, s % 2, :].rearrange("p (t h) -> p t h", t=HG)
                rest = m_rest[:, :].rearrange("p (t h) -> p t h", t=HG)
                wait(dve, m_split, 3 * k + step)
                if step == 0:
                    wait(dve, m_ready, k + 1)
                    wait(dve, m_psum, k)
                    nc.vector.tensor_copy(m_parts[:, :, 0, :], neg).then_inc(m_split, 1)
                if step == 1:
                    nc.vector.tensor_tensor(out=rest, in0=neg, in1=m_parts[:, :, 0, :],
                                            op=ALU.subtract).then_inc(m_split, 1)
                if step == 2:
                    nc.vector.tensor_copy(m_parts[:, :, 1, :], rest).then_inc(m_split, 1)

            def divide(b, s, step):
                k = STAGES * b + s
                g, half = s % STAGES // 2, s % 2
                wait(dve, norm_steps, norms_before(b, s) + step)
                if step == 0:
                    wait(dve, pv_done, 8 * (k + 1))
                    nc.vector.transpose(o_t[:, :, :].rearrange("p n d -> p (n d)"), ps_pv[:, :]).then_inc(norm_steps, 1)
                if step == 1:
                    nc.vector.reciprocal(o_rec[:, :], o_t[:, :, D]).then_inc(norm_steps, 1)
                if step == 2:
                    nc.vector.tensor_tensor(out=o_n[:, half, :, D * g:D * (g + 1)], in0=o_t[:, :, 0:D],
                                            in1=o_rec[:, :].unsqueeze(2).to_broadcast([P, HALF // 32, D]),
                                            op=ALU.mult).then_inc(norm_steps, 1)
                if step == 3 and g == G - 1:
                    wait(dve, pj_psum, 2 * b if s >= 0 else 2 * (b - 1))
                    nc.vector.transpose(att[:, half * HALF:(half + 1) * HALF],
                                        o_n[:, half, :, :].rearrange("p n d -> p (n d)")).then_inc(norm_steps, 1)

            def norm_stats(b, which, copied, done, j):
                src = xt if which == 0 else tok
                wait(dve, copied, 2 * b + j // 4 + 1)
                nc.vector.bn_stats(stats[:, which, j, :], src[:, j, :]).then_inc(done, 1)

            def norm_means(b, which, done):
                wait_apart(dve, dve_passed, done, 16 * b + TB)
                for j in range(TB):
                    nc.vector.bn_aggr(mean_var[:, which, j, :], stats[:, which, j:j + 1, :]).then_inc(done, 1)

            def add_residual(b, half):
                cols = slice(half * HALF, (half + 1) * HALF)
                wait(dve, pj_psum, 2 * b + half + 1)
                wait(dve, res_ready, b + 1)
                nc.vector.tensor_tensor(out=x1[:, cols], in0=misc[:, :], in1=res[:, cols],
                                        op=ALU.add).then_inc(x1_ready, 1)

            def wide(t, n=E):
                return t.unsqueeze(2).to_broadcast([P, TB, n])

            def choose(b):
                count = [0]

                def step(inst):
                    inst.then_inc(route_a, 1)
                    count[0] += 1

                def after():
                    wait(dve, route_a, ROUTE_A * b + count[0])

                m1, m2, m2s = (masks[:, :, i, :] for i in range(3))
                wait(dve, lg_psum, b + 1)
                wait(dve, ln2_scale, 3 * (b + 1))
                nc.vector.tensor_tensor(out=gat[:, :, :], in0=misc[:, 0:TB * E].rearrange("p (j e) -> p j e", j=TB),
                                        in1=wide(rstd[:, 1, :]), op=ALU.mult).then_inc(lg_taken, 1)
                wait(dve, lg_taken, b + 1)
                step(nc.vector.tensor_reduce(out=small[:, 0, :], in_=gat[:, :, :], axis=AX.X, op=ALU.max))
                after()
                nc.vector.tensor_tensor(out=gat[:, :, :], in0=gat[:, :, :], in1=wide(small[:, 0, :]),
                                        op=ALU.subtract).then_inc(gate_shifted, 1)

            def choose_experts(b):
                count = [1]

                def step(inst):
                    inst.then_inc(route_a, 1)
                    count[0] += 1

                def after():
                    wait(dve, route_a, ROUTE_A * b + count[0])

                m1, m2, m2s = (masks[:, :, i, :] for i in range(3))
                wait(dve, gate_exp, b + 1)
                step(nc.vector.tensor_reduce(out=small[:, 1, :], in_=tmp[:, :, :], axis=AX.X, op=ALU.add))
                yield
                after()
                step(nc.vector.reciprocal(small[:, 2, :], small[:, 1, :]))
                yield
                after()
                step(nc.vector.tensor_tensor(out=gat[:, :, :], in0=tmp[:, :, :], in1=wide(small[:, 2, :]), op=ALU.mult))
                yield
                after()
                for i, mask in ((0, m1), (1, m2)):
                    step(nc.vector.tensor_reduce(out=small[:, 3 + i, :], in_=gat[:, :, :], axis=AX.X, op=ALU.max))
                    yield
                    after()
                    step(nc.vector.tensor_tensor(out=tmp[:, :, :], in0=gat[:, :, :], in1=wide(small[:, 3 + i, :]),
                                                 op=ALU.is_ge))
                    yield
                    after()
                    step(nc.vector.tensor_tensor(out=tmp[:, :, :], in0=tmp[:, :, :], in1=e_rev[:, :, :], op=ALU.mult))
                    yield
                    after()
                    step(nc.vector.tensor_reduce(out=small[:, 5, :], in_=tmp[:, :, :], axis=AX.X, op=ALU.max))
                    yield
                    after()
                    step(nc.vector.tensor_tensor(out=mask, in0=tmp[:, :, :], in1=wide(small[:, 5, :]),
                                                 op=ALU.is_equal))
                    yield
                    after()
                    if i == 0:
                        step(nc.vector.tensor_scalar(tmp[:, :, :], mask, -1.0, 1.0, ALU.mult, ALU.add))
                        yield
                        after()
                        step(nc.vector.tensor_tensor(out=gat[:, :, :], in0=gat[:, :, :], in1=tmp[:, :, :],
                                                     op=ALU.mult))
                        yield
                        after()
                step(nc.vector.tensor_copy(m2s, m2))
                yield
                after()
                step(nc.vector.tensor_tensor(out=small[:, 6, :], in0=m1[:, :, 0], in1=m2[:, :, 0], op=ALU.mult))
                yield
                after()
                step(nc.vector.tensor_tensor(out=m2s[:, :, 0], in0=m2[:, :, 0], in1=small[:, 6, :], op=ALU.subtract))
                yield
                after()
                step(nc.vector.tensor_tensor(out=m2s[:, :, 1], in0=m2[:, :, 1], in1=small[:, 6, :], op=ALU.add))
                yield
                after()
                nc.vector.tensor_copy(masks_b[:, :, :], masks[:, :, :, :].rearrange(
                    "p j m e -> p j (m e)")).then_inc(masks_ready, 1)
                step(nc.vector.tensor_tensor(out=small[:, 7, :], in0=small[:, 3, :], in1=small[:, 4, :], op=ALU.add))
                yield
                after()
                step(nc.vector.tensor_scalar(small[:, 7, :], small[:, 7, :], GATE_EPS, None, ALU.add))
                yield
                after()
                step(nc.vector.reciprocal(small[:, 7, :], small[:, 7, :]))
                yield
                after()
                assert count[0] == ROUTE_A, count

            for j in range(TB):
                norm_stats(0, 0, xt_copied, ln1_stats, j)
            norm_means(0, 0, ln1_stats)
            dve.wait_ge(setup, SETUP)
            at_i = 0
            for dst, num in ((e_rev[:, :, :].rearrange("p j e -> p (j e)"), TB * E), (reg_base[:, :], E),
                             (dest_f[:, :, :].rearrange("p j k -> p (j k)"), TB * 2), (part_no[:, :], 1),
                             (blk_no[:, :], 3)):
                nc.vector.tensor_copy(dst, iota_i[:, at_i:at_i + num]).then_inc(setup_v, 1)
                at_i += num
            nc.vector.tensor_copy(base[:, :], iota_i[:, TB * E:TB * E + E]).then_inc(setup_v, 1)
            dve.wait_ge(weights_in, WEIGHTS)
            for o in range(2):
                nc.vector.tensor_copy(wq_r[:, o, :].rearrange("c (g d h) -> c g d h", g=G, d=D),
                                      wq_in[:, o].rearrange("c (g h) d -> c g d h", g=G)).then_inc(setup_v, 1)
            dve.wait_ge(wg_mean, 1)
            nc.vector.tensor_tensor(out=wg_c[:, :], in0=misc[:, 0:E], in1=wg_sb[:, :],
                                    op=ALU.subtract).then_inc(setup_v, 1)
            dve.wait_ge(setup_v, 9)
            nc.vector.tensor_scalar(wg_c[:, :], wg_c[:, :], -1.0, None, ALU.mult).then_inc(setup_v, 1)

            for i in range(4):
                o, half = i // 2, i % 2
                cols = slice(half * HALF, (half + 1) * HALF)
                f = qk_f[:, i % 2, :]
                dve.wait_ge(qk_copied, i + 1)
                nc.vector.tensor_copy(parts[:, o, 0, cols], f).then_inc(qk_parts, 1)
                for level in (1, 2):
                    dve.wait_ge(qk_parts, 5 * i + 2 * level - 1)
                    nc.vector.tensor_tensor(out=f, in0=f, in1=parts[:, o, level - 1, cols],
                                            op=ALU.subtract).then_inc(qk_parts, 1)
                    dve.wait_ge(qk_parts, 5 * i + 2 * level)
                    nc.vector.tensor_copy(parts[:, o, level, cols], f).then_inc(qk_parts, 1)
            for m in range(LEAD):
                take_max(0, m)
                if m == UNITS:
                    row_maxima(0, 0)
                if 0 < m - UNITS < 4:
                    split_m(0, 0, m - UNITS - 1)

            def batch(b, first, last):
                for u in range(SLOTS):
                    m = u + LEAD
                    if not (last and m >= SLOTS):
                        take_max(b, m)
                    if m % UNITS == 0 and not (last and m > SLOTS):
                        row_maxima(b, m // UNITS - 1)
                    if 0 < m % UNITS < 4 and not (last and m > SLOTS + 4):
                        split_m(b, m // UNITS - 1, m % UNITS - 1)
                    if 4 <= u % UNITS < 8 and not (first and u < UNITS):
                        divide(b, u // UNITS - 1, u % UNITS - 4)
                    if not last:
                        if 8 <= u < 16:
                            norm_stats(b + 1, 0, xt_copied, ln1_stats, u - 8)
                        if u == 17:
                            norm_means(b + 1, 0, ln1_stats)
                    if not first:
                        if u == 13:
                            add_residual(b - 1, 0)
                        if u == 17:
                            add_residual(b - 1, 1)
                        if 24 <= u < 32:
                            norm_stats(b - 1, 1, tok_copied, ln2_stats, u - 24)
                        if u == 32:
                            norm_means(b - 1, 1, ln2_stats)
                        if u == 38:
                            choose(b - 1)
                        if u == 44:
                            choice = choose_experts(b - 1)
                        if u >= 44 and u % 2 and u % UNITS not in BUSY:
                            next(choice, None)

            batch(0, True, False)
            with dve.Fori(1, B - 1) as b:
                batch(b, False, False)
            batch(B - 1, False, True)
            for step in range(4):
                divide(B, -1, step)
            add_residual(B - 1, 0)
            add_residual(B - 1, 1)
            for j in range(TB):
                norm_stats(B - 1, 1, tok_copied, ln2_stats, j)
            norm_means(B - 1, 1, ln2_stats)
            choose(B - 1)
            for _ in choose_experts(B - 1):
                pass
            dve.wait_ge(routed, B)
            nc.vector.tensor_scalar(pad_place[:, :], base[:, :], part_no[:, 0:1], None, ALU.add).then_inc(pads_ready, 1)

            tabs = 0

            def tab(inst):
                nonlocal tabs
                tabs += 1
                inst.then_inc(tab_steps, 1)
                dve.wait_ge(tab_steps, tabs)

            rows_n, blocks_n, ends = (blk_f[:, i, 0:E] for i in range(3))
            le = blk_f[:, 3, :].rearrange("p (c e) -> p c e", c=3)
            lb = blk_f[:, 4, :].rearrange("p (c e) -> p c e", c=3)
            e_of, before_of, row_of = (blk_f[:, 5, 3 * i:3 * i + 3] for i in range(3))

            def three(t):
                return t.unsqueeze(1).to_broadcast([P, 3, E])

            tab(nc.vector.tensor_tensor(out=rows_n, in0=base[:, :], in1=reg_base[:, :], op=ALU.subtract))
            tab(nc.vector.tensor_scalar(blk_n[:, :], rows_n, float(P - 1), None, ALU.add))
            tab(nc.vector.tensor_single_scalar(blk_n[:, :], blk_n[:, :], 7, op=ALU.logical_shift_right))
            tab(nc.vector.tensor_copy(blocks_n, blk_n[:, :]))
            tab(nc.vector.tensor_tensor_scan(out=ends, data0=ones_e[:, :], data1=blocks_n, initial=0.0,
                                             op0=ALU.mult, op1=ALU.add))
            tab(nc.vector.tensor_tensor(out=le, in0=three(ends), in1=blk_no[:, :].unsqueeze(2).to_broadcast([P, 3, E]),
                                        op=ALU.is_le))
            tab(nc.vector.tensor_reduce(out=e_of, in_=le, axis=AX.X, op=ALU.add))
            tab(nc.vector.tensor_tensor(out=lb, in0=le, in1=three(blocks_n), op=ALU.mult))
            tab(nc.vector.tensor_reduce(out=before_of, in_=lb, axis=AX.X, op=ALU.add))
            tab(nc.vector.tensor_tensor(out=row_of, in0=blk_no[:, :], in1=before_of, op=ALU.subtract))
            tab(nc.vector.tensor_scalar(row_of, row_of, float(P), None, ALU.mult))
            tab(nc.vector.tensor_scalar(before_of, e_of, float(REG), None, ALU.mult))
            tab(nc.vector.tensor_tensor(out=row_of, in0=row_of, in1=before_of, op=ALU.add))
            tab(nc.vector.tensor_scalar(blk_i[:, 1, :], row_of, float(E * REG), None, ALU.min))
            tab(nc.vector.tensor_scalar(blk_i[:, 0, :], e_of, float(E - 1), None, ALU.min))
            assert tabs == TAB_STEPS, tabs

            dve.wait_ge(tab_in, 16)
            dve.wait_ge(w1_loaded, 16)
            dve.wait_ge(w2_loaded, 16)
            dve.wait_ge(pj_psum, 2 * B)

            e_regs = [dve.alloc_register(f"expert{s}") for s in range(XR)]

            def experts_of(i):
                dve.reg_load(e_regs, table[0:1, 0, i:i + XR] if isinstance(i, int) else table[0:1, 0, bass.ds(i, XR)])
                return [dve.snap(reg, min_val=0, max_val=E - 1) for reg in e_regs]

            def copy_weights(i, s, e):
                wait(dve, hid_psum, i - WR + 1)
                nc.vector.tensor_copy(w1_blk[:, s % WR, :], w1_all[:, bass.ds(e, 1), :].rearrange(
                    "p a h -> p (a h)")).then_inc(w1_copied, 1)
                wait(dve, y_psum, i - WR + 1)
                nc.vector.tensor_copy(w2_blk[:, s % WR, :], w2_all[:, bass.ds(e, 1), :, :].rearrange(
                    "p a c d -> p (a c d)")).then_inc(w2_copied, 1)

            def scale_y(r, s):
                i = XR * r + s
                wait(dve, y_stored[s % WR], 16 * (XR // WR * r + s // WR))
                wait(dve, blk_loaded[s], 16 * (r + 1))
                nc.vector.tensor_copy(blk_dest[:, s % WR:s % WR + 1], blk_in[:, s, C:C + 1].bitcast(I32)).then_inc(dest_copied, 1)
                wait(dve, y_psum, i + 1)
                nc.vector.tensor_scalar(blk_y[:, s % WR, :], ps_o[:, s % 2, 0:P], blk_in[:, s, C + 1:C + 2], None,
                                        ALU.mult).then_inc(y_scaled, 1)

            def blocks(r, count):
                experts = experts_of(XR * r + WLEAD)
                for s in range(XR):
                    if s < count:
                        copy_weights(XR * r + s + WLEAD, s + WLEAD, experts[s])
                    scale_y(r, s)

            experts = experts_of(0)
            for s in range(WLEAD):
                copy_weights(s, s, experts[s])
            blocks(0, XR)
            with dve.Fori(1, BLOCKS // XR - 1) as r:
                blocks(r, XR)
            blocks(BLOCKS // XR - 1, XR - WLEAD)

            def sum_y(r, s):
                b = 2 * r + s
                wait(dve, y_loaded[s], 32 * (r + 1))
                nc.vector.tensor_tensor(out=y_in[:, s, 0], in0=y_in[:, s, 0], in1=y_in[:, s, 1],
                                        op=ALU.add).then_inc(y_summed, 1)

            def add_x1(r, s):
                b = 2 * r + s
                wait(dve, out_stored[s], 16 * r)
                for half in range(2):
                    cols = slice(half * HALF, (half + 1) * HALF)
                    wait(dve, yt_psum, 2 * b + half + 1)
                    res_b = (x1_all[:, b, cols] if isinstance(b, int) else x1_all[:, bass.ds(b, 1), cols].rearrange(
                        "p a t -> p (a t)"))
                    nc.vector.tensor_tensor(out=o_buf[:, s, cols], in0=ps_y[:, s, half, :], in1=res_b,
                                            op=ALU.add).then_inc(out_ready, 1)

            dve.wait_ge(x1_stored, 16 * B)
            def image_pair(r):
                sum_y(r, 1)
                add_x1(r, 0)
                sum_y(r + 1, 0)
                add_x1(r, 1)

            sum_y(0, 0)
            image_pair(0)
            with dve.Fori(1, B // 2 - 1) as r:
                image_pair(r)
            r = B // 2 - 1
            sum_y(r, 1)
            add_x1(r, 0)
            add_x1(r, 1)

        @block.tensor
        def _(pe):
            freed = [None]

            def misc_free(sem_, value):
                if freed[0] is not None:
                    pe.wait_ge(*freed[0])
                freed[0] = (sem_, value)

            def transpose_x(b, half):
                misc_free(xt_copied, 2 * b + half + 1)
                wait(pe, x_loaded, 16 * (b + 1))
                for j in range(4):
                    last = nc.tensor.transpose(misc[:, j * P:(j + 1) * P],
                                               x_in[:, (4 * half + j) * P:(4 * half + j + 1) * P], ident[:, :])
                last.then_inc(xt_psum, 1)

            def project_qk(b, i):
                o, half = i // 2, i % 2
                misc_free(qk_copied, 4 * b + i + 1)
                wait(pe, xt_normed, TB * (b + 1))
                nc.tensor.matmul(misc[:, :], wq_r[:, o, :], xt[:, 4 * half:4 * half + 4, :], start=True,
                                 stop=True).then_inc(qk_psum, 1)

            def project_v(b, half):
                misc_free(v_copied, 2 * b + half + 1)
                for j in range(4):
                    last = nc.tensor.matmul(misc[:, j * P:(j + 1) * P], xt[:, 4 * half + j, :], wv_sb[:, :, :],
                                            start=True, stop=True)
                last.then_inc(v_psum, 1)

            def max_unit(b, m):
                s, u = m // UNITS, m % UNITS
                bb = b + s // STAGES
                g, half = s % STAGES // 2, s % 2
                h, t, kh = u // 8, u // 2 % 4, u % 2
                if u == 0 and half == 0:
                    wait(pe, stacked[g], 192 * (bb + 1))
                wait(pe, max_taken, SLOTS * b + ring_free(m))
                nc.tensor.matmul(ps_max[:, m % SLOTS % RING, :], qs[0:STACK, g, h, half * HALF + t * P:half * HALF + (t + 1) * P],
                                 ks[0:STACK, g, h, kh * HALF:(kh + 1) * HALF], start=True,
                                 stop=True).then_inc(max_ready, 1)

            def rows_of_maxima(b, s):
                k = STAGES * b + s
                misc_free(m_copied, k + 1)
                wait(pe, m_split, 3 * (k + 1))
                for t in range(4):
                    last = nc.tensor.matmul(misc[STACK:STACK + MROWS, t * P:(t + 1) * P],
                                            m_parts[:, t, :, :].rearrange("p a h -> p (a h)"), ident_b[:, :],
                                            start=True, stop=True)
                last.then_inc(m_psum, 1)

            def score_unit(b, u):
                s = u // UNITS
                g, half = s // 2, s % 2
                i, h = u % UNITS // HG, u % HG
                if u % UNITS == 0:
                    wait(pe, m_loaded, 16 * (STAGES * b + s + 1))
                wait(pe, exp_done, SLOTS * b + ring_free(u))
                nc.tensor.matmul(ps_score[:, u % RING, :], ks[0:STACK + MROWS, g, h, i * P:(i + 1) * P],
                                 qs[0:STACK + MROWS, g, h, half * HALF:(half + 1) * HALF], start=True,
                                 stop=True).then_inc(scores_ready, 1)

            def weigh(b, n, part):
                s, i = n // 8, n % 8
                g = s % STAGES // 2
                bb = b + s // STAGES
                if part == 0:
                    if i == 0:
                        wait(pe, norm_steps, norms_before(b, s - 1) + 1)
                        wait(pe, v_placed, 2 * bb + g + 1)
                    wait(pe, exp_done, SLOTS * b + 4 * n + 4)
                cols = slice(part * HALF // 2, (part + 1) * HALF // 2)
                for h in range(HG):
                    last = nc.tensor.matmul(ps_pv[32 * h:32 * h + 32, cols], v_pad[:, i, HG * g + h, :],
                                            probs[:, (4 * n + h) % PRING, cols], start=(i == 0 and part == 0),
                                            stop=(i == TB - 1), skip_group_check=True)
                if part:
                    last.then_inc(pv_done, 1)

            def project_out(b, half):
                misc_free(x1_ready, 2 * b + half + 1)
                wait(pe, norm_steps, NORMS * (b + 1))
                for j in range(4):
                    last = nc.tensor.matmul(misc[:, j * P:(j + 1) * P], att[:, (4 * half + j) * P:(4 * half + j + 1) * P],
                                            wp_sb[:, :], start=True, stop=True)
                last.then_inc(pj_psum, 1)

            def transpose_tokens(b, half):
                misc_free(tok_copied, 2 * b + half + 1)
                wait(pe, x1_ready, 2 * b + half + 1)
                for j in range(4):
                    last = nc.tensor.transpose(misc[:, j * P:(j + 1) * P],
                                               x1[:, (4 * half + j) * P:(4 * half + j + 1) * P], ident[:, :])
                last.then_inc(tt_psum, 1)

            def logits(b):
                misc_free(lg_taken, b + 1)
                for j in range(TB):
                    last = nc.tensor.matmul(misc[:, j * E:(j + 1) * E], x1[:, j * P:(j + 1) * P], wg_c[:, :],
                                            start=True, stop=True)
                last.then_inc(lg_psum, 1)

            def count_tokens(b):
                w = 3 * E
                misc_free(cs_taken, b + 1)
                wait(pe, masks_ready, b + 1)
                nc.tensor.matmul(misc[:, 0:TB * w], tri_b[:, :], masks_b[:, :, :], start=True, stop=False)
                for d in range(1, TB):
                    nc.tensor.matmul(misc[:, d * w:TB * w], ones_b[:, :], masks_b[:, 0:TB - d, :], start=False,
                                     stop=(d == TB - 1))
                for j in range(TB):
                    last = nc.tensor.matmul(misc[:, TB * w:(TB + 1) * w], ones_b[:, :], masks_b[:, j, :],
                                            start=(j == 0), stop=(j == TB - 1))
                last.then_inc(cs_psum, 1)

            pe.wait_ge(setup, SETUP_IDENT)
            transpose_x(0, 0)
            transpose_x(0, 1)
            pe.wait_ge(setup, SETUP)
            pe.wait_ge(weights_in, WEIGHTS)
            misc_free(setup_v, 10)
            nc.tensor.matmul(misc[:, 0:E], mean_m[:, :], wg_sb[:, :], start=True, stop=True).then_inc(wg_mean, 1)
            for i in range(4):
                project_qk(0, i)
            project_v(0, 0)
            project_v(0, 1)
            for m in range(LEAD):
                max_unit(0, m)
                if m == 37:
                    rows_of_maxima(0, 0)
            pe.wait_ge(key_rows, KEY_ROWS)

            def batch(b, first, last):
                freed[0] = (m_copied, STAGES * b + 1)
                for u in range(SLOTS):
                    if u % 2 == 0:
                        if not (last and u + LEAD >= SLOTS):
                            max_unit(b, u + LEAD)
                        score_unit(b, u)
                    else:
                        score_unit(b, u)
                        if not (last and u + LEAD >= SLOTS):
                            max_unit(b, u + LEAD)
                    n, part = WEIGH_AT[u % UNITS]
                    if part is not None and not (first and u // UNITS * 8 + n < 0):
                        weigh(b, u // UNITS * 8 + n, part)
                    if not last:
                        if u == 1:
                            transpose_x(b + 1, 0)
                        if u == 5:
                            transpose_x(b + 1, 1)
                        if u == 29:
                            project_qk(b + 1, 0)
                        if u == 41:
                            project_qk(b + 1, 1)
                        if u == 44:
                            project_qk(b + 1, 2)
                        if u == 48:
                            project_qk(b + 1, 3)
                        if u == 51:
                            project_v(b + 1, 0)
                        if u == 54:
                            project_v(b + 1, 1)
                    if not first:
                        if u == 13:
                            project_out(b - 1, 0)
                        if u == 17:
                            project_out(b - 1, 1)
                        if u == 22:
                            transpose_tokens(b - 1, 0)
                        if u == 24:
                            transpose_tokens(b - 1, 1)
                        if u == 36:
                            logits(b - 1)
                        if u == 100:
                            count_tokens(b - 1)
                    if u % UNITS == MSLOT and not (last and u > 96):
                        rows_of_maxima(b, u // UNITS + 1)

            batch(0, True, False)
            nc.disable_value_cache = True
            with pe.Fori(1, B - 1) as b:
                batch(b, False, False)
            nc.disable_value_cache = False
            batch(B - 1, False, True)
            weigh(B, -1, 0)
            weigh(B, -1, 1)
            project_out(B - 1, 0)
            project_out(B - 1, 1)
            transpose_tokens(B - 1, 0)
            transpose_tokens(B - 1, 1)
            logits(B - 1)
            count_tokens(B - 1)

            def transpose_block(r, s):
                i = XR * r + s
                wait(pe, blk_loaded[s % XR], 16 * (r + s // XR + 1))
                wait(pe, blk_tr_copied, i - 1)
                nc.tensor.transpose(ps_xt[:, s % 2, 0:P], blk_in[:, s % XR, 0:C], ident[:, :]).then_inc(blk_tr, 1)

            def hidden(r, s):
                i = XR * r + s
                wait(pe, blk_tr_copied, i + 1)
                wait(pe, w1_copied, i + 1)
                wait(pe, hid_done, i - 1)
                for c in range(HC):
                    last = nc.tensor.matmul(ps_h[:, s % 2, c * P:(c + 1) * P], w1_blk[:, s % WR, c * P:(c + 1) * P],
                                            blk_xt[:, s % 2, :], start=True, stop=True)
                last.then_inc(hid_psum, 1)

            def outputs(i, s):
                wait(pe, hid_done, i + 1)
                wait(pe, w2_copied, i + 1)
                wait(pe, y_scaled, i - 1)
                for c in range(HC):
                    last = nc.tensor.matmul(ps_o[:, s % 2, 0:P], hid[:, s % 2, c * P:(c + 1) * P],
                                            w2_blk[:, s % WR, c * P:(c + 1) * P], start=(c == 0), stop=(c == HC - 1))
                last.then_inc(y_psum, 1)

            def block_steps(r, s, first, last):
                if not last:
                    transpose_block(r, s + 1)
                hidden(r, s)
                if not first:
                    outputs(XR * r + s - 1, s - 1)

            pe.wait_ge(cs_taken, B)
            transpose_block(0, 0)
            for s in range(XR):
                block_steps(0, s, s == 0, False)
            with pe.Fori(1, BLOCKS // XR - 1) as r:
                for s in range(XR):
                    block_steps(r, s, False, False)
            for s in range(XR):
                block_steps(BLOCKS // XR - 1, s, False, s == XR - 1)
            outputs(BLOCKS - 1, XR - 1)

            def transpose_y(r, s):
                b = 2 * r + s
                wait(pe, y_summed, b + 1)
                wait(pe, out_ready, 2 * (b - 1))
                for j in range(TB):
                    last = nc.tensor.transpose(ps_y[:, s, j // 4, j % 4 * P:(j % 4 + 1) * P], y_in[:, s, 0, j, :],
                                               ident[:, :])
                    if j % 4 == 3:
                        last.then_inc(yt_psum, 1)

            pe.wait_ge(hid_done, BLOCKS)
            for s in range(2):
                transpose_y(0, s)
            with pe.Fori(1, B // 2) as r:
                for s in range(2):
                    transpose_y(r, s)


_INS = ['x', 'L0_conv_Wq', 'L0_conv_Wk', 'L0_conv_Wv', 'L0_conv_Wproj', 'L0_conv_bproj', 'L0_ffn_w_gating',
        'L0_ffn_w1', 'L0_ffn_w2']
_OUTS = [((16, 128, 32, 32), 'float32')]


def kernel(**inputs):
    import numpy as _np
    import concourse.bacc as _bacc
    from concourse import mybir as _mybir
    from concourse.bass_utils import run_bass_kernel_spmd as _run

    nc = _bacc.Bacc("TRN2", target_bir_lowering=False, num_devices=1)
    arrays, args = {}, []
    for name in _INS:
        a = _np.ascontiguousarray(inputs[name])
        arrays[f"in_{name}_dram"] = a
        args.append(nc.dram_tensor(f"in_{name}_dram", a.shape, _mybir.dt.from_np(a.dtype), kind="ExternalInput").ap())
    for i, (shape, dtype) in enumerate(_OUTS):
        dt = _mybir.dt.from_np(_np.dtype(dtype))
        args.append(nc.dram_tensor(f"out_{i}_dram", shape, dt, kind="ExternalOutput").ap())
    metaformer(nc, *args)
    r = _run(nc, [arrays], core_ids=[0])
    got = tuple(r.results[0][f"out_{i}_dram"] for i in range(len(_OUTS)))
    return got[0]
```
